# Optimizing a Trainium2 kernel written in Bass

```python
import numpy as np
import jax
import jax.numpy as jnp

def _softmax(x, axis=-1):
    return jax.nn.softmax(x, axis=axis)

def _gelu(x):
    return jax.nn.gelu(x, approximate=True)

def _silu(x):
    return jax.nn.silu(x)

def _sigmoid(x):
    return jax.nn.sigmoid(x)

def _layernorm(x, axis=-1, eps=1e-05):
    m = jnp.mean(x, axis=axis, keepdims=True)
    v = jnp.var(x, axis=axis, keepdims=True)
    return (x - m) / jnp.sqrt(v + eps)

def _scatter_add(tgt, idx, src, axis=0):
    return tgt.at[idx].add(src)

def _segment_sum(src, seg, n):
    return jax.ops.segment_sum(src, seg, n)
kernel_name = 'mk_vit_tower_d1_tok_img512_r4_1c4fde'

def setup_inputs(seed: int=0):
    np.random.seed(seed)
    _w = jnp.asarray

    def _rec_inputs():
        import jax
        import jax.numpy as jnp
        _rk = jax.random.key(seed)
        x = 7.22013e-05 + 1.00017 * jax.random.normal(jax.random.fold_in(_rk, 1), (8, 512, 64, 2), jnp.float32)
        return x
    x = _rec_inputs()

    def _L0_tok_setup():
        import jax, jax.numpy as jnp
        import numpy as np
        B, L, C = (8, 512, 64)
        D = C // 8

        def _attn(q, k, v, scale):
            scores = jnp.einsum('bld,bmd->blm', q, k) / scale
            w = jax.nn.softmax(scores, axis=-1)
            return jnp.einsum('blm,bmd->bld', w, v)
        key = jax.random.key(seed)
        ks = jax.random.split(key, 16)
        he = lambda k, cin, cout: jax.random.normal(k, (cin, cout), jnp.float32) * np.sqrt(2.0 / cin)
        inp = {'x': jax.random.normal(ks[0], (B, L, C, 2), jnp.float32)}
        dims = [D, D, C, D, D, C, D, D, C, D, D, C]
        for i, dout in enumerate(dims):
            inp[f'w{i + 1}'] = he(ks[i + 1], C, dout)
        inp['alpha'] = jnp.zeros((1,), jnp.float32)
        inp['gamma'] = jnp.zeros((1,), jnp.float32)
        return inp
    _L0_tok_all = _L0_tok_setup()
    _L0_tok_in = {k: v for k, v in _L0_tok_all.items() if k in ('w1', 'w2', 'w3', 'w4', 'w5', 'w6', 'w7', 'w8', 'w9', 'w10', 'w11', 'w12', 'alpha', 'gamma')}
    del _L0_tok_all

    def _L0_attn_setup():
        import jax, jax.numpy as jnp
        import numpy as np
        LEAK = 0.95
        SPECTRAL_RADIUS = 1.2
        SPARSITY = 0.1
        EPS_LN = 1e-05

        def _ln(x, g, b):
            m = jnp.mean(x, axis=-1, keepdims=True)
            v = jnp.var(x, axis=-1, keepdims=True)
            return (x - m) / jnp.sqrt(v + EPS_LN) * g + b
        key = jax.random.key(seed)
        ks = jax.random.split(key, 12)
        Bsz, S, D, H = (8, 512, 128, 256)
        x = jax.random.normal(ks[0], (Bsz, S, D), jnp.float32)
        W_in = jax.random.uniform(ks[1], (H, D), jnp.float32, -1.0, 1.0) / jnp.sqrt(D)
        W_res = jax.random.normal(ks[2], (H, H), jnp.float32)
        mask = (jax.random.uniform(ks[3], (H, H)) > SPARSITY).astype(jnp.float32)
        W_res = W_res * mask
        est_radius = jnp.sqrt(H * (1.0 - SPARSITY))
        W_res = W_res * (SPECTRAL_RADIUS / est_radius)
        A = -jnp.ones((H,), jnp.float32) * 10.0
        W_B = jax.random.normal(ks[4], (H, D), jnp.float32) / jnp.sqrt(D)
        w_delta = jax.random.normal(ks[5], (D,), jnp.float32) / jnp.sqrt(D)
        b_delta = jnp.zeros((), jnp.float32)
        ro_g = jnp.ones((H,), jnp.float32)
        ro_b = jnp.zeros((H,), jnp.float32)
        W_ro = jax.random.normal(ks[6], (D, H), jnp.float32) / jnp.sqrt(H)
        b_ro = jnp.zeros((D,), jnp.float32)
        W_gate = jax.random.normal(ks[7], (D, D), jnp.float32) / jnp.sqrt(D)
        b_gate = jnp.zeros((D,), jnp.float32)
        norm_g = jnp.ones((D,), jnp.float32)
        norm_b = jnp.zeros((D,), jnp.float32)
        return {'x': x, 'norm_g': norm_g, 'norm_b': norm_b, 'W_in': W_in, 'W_res': W_res, 'A': A, 'W_B': W_B, 'w_delta': w_delta, 'b_delta': b_delta, 'ro_g': ro_g, 'ro_b': ro_b, 'W_ro': W_ro, 'b_ro': b_ro, 'W_gate': W_gate, 'b_gate': b_gate}
    _L0_attn_all = _L0_attn_setup()
    _L0_attn_in = {k: v for k, v in _L0_attn_all.items() if k in ('norm_g', 'norm_b', 'W_in', 'W_res', 'A', 'W_B', 'w_delta', 'b_delta', 'ro_g', 'ro_b', 'W_ro', 'b_ro', 'W_gate', 'b_gate')}
    del _L0_attn_all

    def _L0_ffn_setup():
        import jax, jax.numpy as jnp
        import numpy as np
        MARK_AX, OP_ADD, OP_SUB = (0, 1, 2)
        ALU_LO, ALU_HI = (16, 32)
        AX_CARRY_LO, AX_CARRY_HI = (48, 64)
        OPCODE_BASE = 80
        OUTPUT_LO, OUTPUT_HI, CARRY = (128, 144, 160)
        NIB_A, NIB_B, OP_START = (0, 1, 10)
        RESULT, CARRY_OUT = (100, 101)
        GE_POS, GE_DIM = (8, 160)
        OPC_ADD, OPC_SUB = (25, 26)
        B, S, D = (8, 1024, 128)

        def _decode_nibble(x, base):
            return jnp.argmax(x[..., base:base + 16] > 0.5, axis=-1).astype(x.dtype)

        def _pipeline(h, W, b):
            for i in range(3):
                h = jnp.einsum('bspd,od->bspo', h, W[i]) + b[i]
                if i < 2:
                    h = jax.nn.relu(h)
            return h
        key = jax.random.key(seed)
        kx, k1, k2, k3, k4 = jax.random.split(key, 5)
        x_bd = jax.random.uniform(kx, (B, S, D), dtype=jnp.float32)
        Wa = jax.random.normal(k1, (3, GE_DIM, GE_DIM), dtype=jnp.float32) * 0.05
        ba = jax.random.normal(k2, (3, GE_DIM), dtype=jnp.float32) * 0.05
        Ws = jax.random.normal(k3, (3, GE_DIM, GE_DIM), dtype=jnp.float32) * 0.05
        bs = jax.random.normal(k4, (3, GE_DIM), dtype=jnp.float32) * 0.05
        return {'x_bd': x_bd, 'Wa': Wa, 'ba': ba, 'Ws': Ws, 'bs': bs}
    _L0_ffn_all = _L0_ffn_setup()
    _L0_ffn_in = {k: v for k, v in _L0_ffn_all.items() if k in ('Wa', 'ba', 'Ws', 'bs')}
    del _L0_ffn_all
    return {'x': x, 'L0_tok_w1': _L0_tok_in['w1'], 'L0_tok_w2': _L0_tok_in['w2'], 'L0_tok_w3': _L0_tok_in['w3'], 'L0_tok_w4': _L0_tok_in['w4'], 'L0_tok_w5': _L0_tok_in['w5'], 'L0_tok_w6': _L0_tok_in['w6'], 'L0_tok_w7': _L0_tok_in['w7'], 'L0_tok_w8': _L0_tok_in['w8'], 'L0_tok_w9': _L0_tok_in['w9'], 'L0_tok_w10': _L0_tok_in['w10'], 'L0_tok_w11': _L0_tok_in['w11'], 'L0_tok_w12': _L0_tok_in['w12'], 'L0_tok_alpha': _L0_tok_in['alpha'], 'L0_tok_gamma': _L0_tok_in['gamma'], 'L0_attn_norm_g': _L0_attn_in['norm_g'], 'L0_attn_norm_b': _L0_attn_in['norm_b'], 'L0_attn_W_in': _L0_attn_in['W_in'], 'L0_attn_W_res': _L0_attn_in['W_res'], 'L0_attn_A': _L0_attn_in['A'], 'L0_attn_W_B': _L0_attn_in['W_B'], 'L0_attn_w_delta': _L0_attn_in['w_delta'], 'L0_attn_b_delta': _L0_attn_in['b_delta'], 'L0_attn_ro_g': _L0_attn_in['ro_g'], 'L0_attn_ro_b': _L0_attn_in['ro_b'], 'L0_attn_W_ro': _L0_attn_in['W_ro'], 'L0_attn_b_ro': _L0_attn_in['b_ro'], 'L0_attn_W_gate': _L0_attn_in['W_gate'], 'L0_attn_b_gate': _L0_attn_in['b_gate'], 'L0_ffn_Wa': _L0_ffn_in['Wa'], 'L0_ffn_ba': _L0_ffn_in['ba'], 'L0_ffn_Ws': _L0_ffn_in['Ws'], 'L0_ffn_bs': _L0_ffn_in['bs']}

def reference(x, L0_tok_w1, L0_tok_w2, L0_tok_w3, L0_tok_w4, L0_tok_w5, L0_tok_w6, L0_tok_w7, L0_tok_w8, L0_tok_w9, L0_tok_w10, L0_tok_w11, L0_tok_w12, L0_tok_alpha, L0_tok_gamma, L0_attn_norm_g, L0_attn_norm_b, L0_attn_W_in, L0_attn_W_res, L0_attn_A, L0_attn_W_B, L0_attn_w_delta, L0_attn_b_delta, L0_attn_ro_g, L0_attn_ro_b, L0_attn_W_ro, L0_attn_b_ro, L0_attn_W_gate, L0_attn_b_gate, L0_ffn_Wa, L0_ffn_ba, L0_ffn_Ws, L0_ffn_bs):
    import jax
    import jax.numpy as jnp

    def _L0_tok_ref(x, w1, w2, w3, w4, w5, w6, w7, w8, w9, w10, w11, w12, alpha, gamma):
        import jax, jax.numpy as jnp
        import numpy as np
        B, L, C = (8, 512, 64)
        D = C // 8

        def _attn(q, k, v, scale):
            scores = jnp.einsum('bld,bmd->blm', q, k) / scale
            w = jax.nn.softmax(scores, axis=-1)
            return jnp.einsum('blm,bmd->bld', w, v)
        ecg = x[:, :, :, 0]
        pcg = x[:, :, :, 1]
        proj = lambda f, w: jnp.einsum('blc,cd->bld', f, w)
        scale = jnp.sqrt(jnp.asarray(D, x.dtype))
        qkv_ecg_intra = _attn(proj(ecg, w1), proj(ecg, w2), proj(ecg, w3), scale)
        qkv_ecg_inter = _attn(proj(ecg, w4), proj(pcg, w5), proj(pcg, w6), scale)
        ecg_out = qkv_ecg_inter + alpha * qkv_ecg_intra
        qkv_pcg_intra = _attn(proj(pcg, w7), proj(pcg, w8), proj(pcg, w9), scale)
        qkv_pcg_inter = _attn(proj(pcg, w10), proj(ecg, w11), proj(ecg, w12), scale)
        pcg_out = qkv_pcg_inter + gamma * qkv_pcg_intra
        return jnp.concatenate([ecg_out, pcg_out], axis=-1)

    def _L0_attn_ref(x, norm_g, norm_b, W_in, W_res, A, W_B, w_delta, b_delta, ro_g, ro_b, W_ro, b_ro, W_gate, b_gate):
        import jax, jax.numpy as jnp
        import numpy as np
        LEAK = 0.95
        SPECTRAL_RADIUS = 1.2
        SPARSITY = 0.1
        EPS_LN = 1e-05

        def _ln(x, g, b):
            m = jnp.mean(x, axis=-1, keepdims=True)
            v = jnp.var(x, axis=-1, keepdims=True)
            return (x - m) / jnp.sqrt(v + EPS_LN) * g + b
        Bsz, S, D = x.shape
        H = W_in.shape[0]
        x_norm = _ln(x, norm_g, norm_b)
        xin = jnp.einsum('bsd,hd->sbh', x_norm, W_in)
        h0 = jnp.zeros((Bsz, H), x.dtype)

        def res_step(prev, xt):
            new = jnp.tanh(xt + prev @ W_res.T)
            new = LEAK * new + (1.0 - LEAK) * prev
            return (new, new)
        _, res_states = jax.lax.scan(res_step, h0, xin)
        res_states = jnp.swapaxes(res_states, 0, 1)

        def readout(s):
            return jax.nn.gelu(_ln(s, ro_g, ro_b) @ W_ro.T + b_ro, approximate=False)
        reservoir_out = readout(res_states)
        Bm = jnp.einsum('bsd,hd->bsh', x_norm, W_B)
        delta = jax.nn.softplus(jnp.einsum('bsd,d->bs', x_norm, w_delta) + b_delta)
        A_bar = jnp.exp(A * delta[..., None])
        B_bar = Bm * (1.0 - A_bar) / (A + 1e-08)

        def ssm_step(prev, ab_bb):
            ab, bb = ab_bb
            h = ab * prev + bb
            return (h, h)
        _, ssm_states = jax.lax.scan(ssm_step, h0, (jnp.swapaxes(A_bar, 0, 1), jnp.swapaxes(B_bar, 0, 1)))
        ssm_states = jnp.swapaxes(ssm_states, 0, 1)
        ssm_out = readout(ssm_states)
        gate = jax.nn.sigmoid(x @ W_gate.T + b_gate)
        return reservoir_out * gate + ssm_out * (1.0 - gate)

    def _L0_ffn_ref(x_bd, Wa, ba, Ws, bs):
        import jax, jax.numpy as jnp
        import numpy as np
        MARK_AX, OP_ADD, OP_SUB = (0, 1, 2)
        ALU_LO, ALU_HI = (16, 32)
        AX_CARRY_LO, AX_CARRY_HI = (48, 64)
        OPCODE_BASE = 80
        OUTPUT_LO, OUTPUT_HI, CARRY = (128, 144, 160)
        NIB_A, NIB_B, OP_START = (0, 1, 10)
        RESULT, CARRY_OUT = (100, 101)
        GE_POS, GE_DIM = (8, 160)
        OPC_ADD, OPC_SUB = (25, 26)
        B, S, D = (8, 1024, 128)

        def _decode_nibble(x, base):
            return jnp.argmax(x[..., base:base + 16] > 0.5, axis=-1).astype(x.dtype)

        def _pipeline(h, W, b):
            for i in range(3):
                h = jnp.einsum('bspd,od->bspo', h, W[i]) + b[i]
                if i < 2:
                    h = jax.nn.relu(h)
            return h
        x = x_bd
        Bsz, seq, _ = x.shape
        x_ge = jnp.zeros((Bsz, seq, GE_POS, GE_DIM), dtype=x.dtype)
        x_ge = x_ge.at[..., 0, NIB_A].set(_decode_nibble(x, ALU_LO))
        x_ge = x_ge.at[..., 1, NIB_A].set(_decode_nibble(x, ALU_HI))
        x_ge = x_ge.at[..., 0, NIB_B].set(_decode_nibble(x, AX_CARRY_LO))
        x_ge = x_ge.at[..., 1, NIB_B].set(_decode_nibble(x, AX_CARRY_HI))
        x_ge = x_ge.at[..., :, OP_START + OPC_ADD].set(x[..., OPCODE_BASE + OPC_ADD][..., None])
        x_ge = x_ge.at[..., :, OP_START + OPC_SUB].set(x[..., OPCODE_BASE + OPC_SUB][..., None])
        mark = x[..., MARK_AX] > 0.5
        m_add = mark & (x[..., OP_ADD] > 0.5)
        m_sub = mark & ~(x[..., OP_ADD] > 0.5) & (x[..., OP_SUB] > 0.5)
        active = (m_add | m_sub).astype(x.dtype)
        y_add = _pipeline(x_ge, Wa, ba)
        y_sub = _pipeline(x_ge, Ws, bs)
        y = jnp.where(m_add[..., None, None], y_add, jnp.where(m_sub[..., None, None], y_sub, x_ge))
        res_lo = jnp.clip(jnp.round(y[..., 0, RESULT]), 0, 15).astype(jnp.int32)
        res_hi = jnp.clip(jnp.round(y[..., 1, RESULT]), 0, 15).astype(jnp.int32)
        oh_lo = jax.nn.one_hot(res_lo, 16, dtype=x.dtype) * active[..., None]
        oh_hi = jax.nn.one_hot(res_hi, 16, dtype=x.dtype) * active[..., None]
        carry = (jnp.round(y[..., 1, CARRY_OUT]) > 0.5).astype(x.dtype) * active
        out = x
        out = out.at[..., OUTPUT_LO:OUTPUT_LO + 16].add(2.0 * oh_lo)
        out = out.at[..., OUTPUT_HI:OUTPUT_HI + 16].add(2.0 * oh_hi)
        out = out.at[..., CARRY].add(carry)
        return out
    h = _L0_tok_ref(x, L0_tok_w1, L0_tok_w2, L0_tok_w3, L0_tok_w4, L0_tok_w5, L0_tok_w6, L0_tok_w7, L0_tok_w8, L0_tok_w9, L0_tok_w10, L0_tok_w11, L0_tok_w12, L0_tok_alpha, L0_tok_gamma)
    h = h + _L0_attn_ref(_layernorm(h, axis=-1), L0_attn_norm_g, L0_attn_norm_b, L0_attn_W_in, L0_attn_W_res, L0_attn_A, L0_attn_W_B, L0_attn_w_delta, L0_attn_b_delta, L0_attn_ro_g, L0_attn_ro_b, L0_attn_W_ro, L0_attn_b_ro, L0_attn_W_gate, L0_attn_b_gate)
    h = h + _L0_ffn_ref(_layernorm(h, axis=-1), L0_ffn_Wa, L0_ffn_ba, L0_ffn_Ws, L0_ffn_bs)
    return h

_drawn_inputs = setup_inputs


def setup_inputs(seed=0):
    import zlib

    import numpy as np

    out = dict(_drawn_inputs(seed))
    spreads = {'L0_attn_norm_g': (1.0, 0.2),
     'L0_attn_norm_b': (0.0, 0.1),
     'L0_attn_A': (-10.0, 0.2),
     'L0_attn_ro_g': (1.0, 0.2),
     'L0_attn_ro_b': (0.0, 0.1),
     'L0_attn_b_ro': (0.0, 0.1),
     'L0_attn_b_gate': (0.0, 0.31)}
    factors = {}
    for name, (base, spread) in spreads.items():
        noise = np.random.default_rng([zlib.crc32(name.encode()), seed]).standard_normal(out[name].shape)
        drawn = base * np.exp(spread * noise) if base else spread * noise
        out[name] = jnp.asarray(drawn.astype(out[name].dtype))
    for name, factor in factors.items():
        out[name] = (out[name] * factor).astype(out[name].dtype)
    return out
```

```python
from contextlib import ExitStack

import numpy as np
import concourse.bass as bass
from concourse import mybir

F32 = mybir.dt.float32
F16 = mybir.dt.float16
BF16 = mybir.dt.bfloat16
I32 = mybir.dt.int32
ALU = mybir.AluOpType
ACT = mybir.ActivationFunctionType
AX_X = mybir.AxisListType.X

B, L, C = 8, 512, 64
D = C // 8
P = 128
NA = 4
NQ = L // P
NT = NQ * B
H = 256
NH = H // P
STEPS = 16
BODIES = L // STEPS
SB = STEPS * B
HALF = SB // 2
AHEAD = 9
SLOT = 64
VW = 194
LEAK, KEEP = 0.95, 1.0 - 0.95
EPS = 1e-5
STATE_UP = 4096.0
WEIGHT_UP = 128.0
SHIFT = 24.0


def build(nc, x, w, alpha, gamma, norm_g, norm_b, w_in, w_res, ssm_a, w_b, w_delta, b_delta,
          ro_g, ro_b, w_ro, b_ro, w_gate, b_gate, out):
    ctx = ExitStack()
    with ctx:
        def sb(name, shape, dt=F32):
            return ctx.enter_context(nc.sbuf_tensor(name, shape, dt))

        def sem(name):
            return ctx.enter_context(nc.semaphore(name))

        ident = sb("ident", [P, P])
        ident16 = sb("ident16", [P, P], BF16)
        ones = sb("ones", [P, P])
        neg_rows = sb("neg_rows", [P, P], BF16)
        wall = sb("wall", [P, 64 + NA * C])
        res_nat = sb("res_nat", [P, NH, H])
        in_nat = sb("in_nat", [P, NH, P])
        b_nat = sb("b_nat", [P, NH, P])
        ro_nat = sb("ro_nat", [P, H])
        ro_g_row = sb("ro_g_row", [P, H])
        ro_b_row = sb("ro_b_row", [P, H])
        ro_tmp = sb("ro_tmp", [P, H])
        gate_nat = sb("gate_nat", [P, P])
        b_gate_row = sb("b_gate_row", [P, P])
        cols = sb("cols", [P, 8])
        a_cols = sb("a_cols", [P, NH])
        neg_inv_a = sb("neg_inv_a", [P, NH])
        mix = sb("mix", [P, NA])
        setup = sb("setup", [P, 16])
        res_hi = sb("res_hi", [P, NH, H], F16)
        res_lo = sb("res_lo", [P, NH, H], F16)
        in_t = sb("in_t", [P, H])
        b_t = sb("b_t", [P, H])
        gate_t = sb("gate_t", [P, P + 1])
        ro_t = sb("ro_t", [P, NH, P])
        ro_row = sb("ro_row", [P, P])

        states = sb("states", [P, BODIES, STEPS * NH * B])
        early = states[:, :, :].rearrange("p i n -> p (i n)")
        x_in = early[:, 0:1024].rearrange("p (i k n) -> p i k n", i=2, k=NQ)
        x_t = early[:, 1024:2048].rearrange("p (i k n) -> p i k n", i=2, k=NQ)
        rest_v = early[:, 2048:3072].rearrange("p (k n) -> p k n", k=NQ)
        rest_qk = early[:, 3072:3328].rearrange("p (h k n) -> p h k n", h=2, k=NQ)
        part = early[:, 3328:3712].bitcast(BF16).rearrange("p (l h k n) -> p l h k n", l=3, h=2, k=NQ)
        k_rows = early[:, 3712:4224].bitcast(BF16).rearrange("p (k n) -> p k n", k=NQ)
        res_abs = early[:, 4224:4224 + NH * H]
        q_rows = sb("q_rows", [P, NQ, B, NA * SLOT], BF16)
        k_cols = sb("k_cols", [P, B, 2, L], BF16)
        values = sb("values", [P, B * NQ, NA * VW], BF16)

        q_cols = sb("q_cols", [P, NA, P], BF16)
        top = sb("top", [P, 2])
        shift = sb("shift", [P, 1])
        shift_rows = sb("shift_rows", [P, P], BF16)
        shift_cols = sb("shift_cols", [P, 2, P], BF16)
        prob = sb("prob", [P, 2, L])
        prob_hi = sb("prob_hi", [P, 2, L], F16)
        prob_lo = sb("prob_lo", [P, 2, L], F16)
        o_sb = sb("o_sb", [P, NA, VW])
        o_sum = sb("o_sum", [P, NA, C])
        coef = sb("coef", [P, NA])
        h_now = sb("h_now", [P, P])
        stats = sb("stats", [P, 6])
        mean_var = sb("mean_var", [P, 2])
        small = sb("small", [P, 8])
        minus_half = sb("minus_half", [P, 1])
        eps_col = sb("eps_col", [P, 1])
        x_hat = sb("x_hat", [P, P])
        x_hat_t = sb("x_hat_t", [P, P])
        gate_pre = sb("gate_pre", [P, P])

        h_all = sb("h_all", [P, NT, P])
        gate_all = sb("gate_all", [P, NT, P])
        xn = sb("xn", [P, L * B + HALF])
        z_all = sb("z_all", [P, NT])

        y = sb("y", [P, NH * B])
        s_hi = sb("s_hi", [P, NH * B], F16)
        s_lo = sb("s_lo", [P, NH * B], F16)
        kept = sb("kept", [P, NH * B])
        s_body = sb("s_body", [P, STEPS, NH * B])

        tail_small = sb("tail_small", [P, 8])
        tail_mv = sb("tail_mv", [P, 2, 2])
        tail_st = sb("tail_st", [P, 2, 6])
        mv_out = sb("mv_out", [P, 2])
        st_out = sb("st_out", [P, 6])
        delta = sb("delta", [P, NT])
        sp_tmp = sb("sp_tmp", [P, 2, NT])
        carry = sb("carry", [P, NH, B])
        v32 = values[:, :, :].rearrange("p k n -> p (k n)").bitcast(F32)
        ssm_a_bar = v32[:, 0:NH * 4 * P].rearrange("p (m n) -> p m n", m=NH)
        ssm_b_bar = v32[:, 1024:1024 + NH * 4 * P].rearrange("p (m n) -> p m n", m=NH)
        diag = v32[:, 2048:2048 + 4 * P]
        ssm_states = v32[:, 4096:4096 + NH * 4096].rearrange("p (m q n) -> p m q n", m=NH, q=NQ)
        k32 = k_cols[:, :, :, :].rearrange("p b a n -> p (b a n)").bitcast(F32)
        r_in = k32[:, 0:2 * NH * P].rearrange("p (r m n) -> p r m n", r=2, m=NH)
        r_pre = k32[:, 512:512 + 2 * P].rearrange("p (r n) -> p r n", r=2)
        r_act = k32[:, 768:768 + 2 * P].rearrange("p (r n) -> p r n", r=2)
        r_mix = k32[:, 1024:1024 + P]
        r_h2 = k32[:, 1152:1152 + P]
        r_gate = k32[:, 1280:1280 + P]
        assert 4096 + NH * 4096 <= 12416

        PS = ctx.enter_context(nc.psum_tensor("PS", [P, 8, 512], F32))
        PRE = [PS[:, i, 0:SB].rearrange("p (m t b) -> p m t b", m=NH, b=B) for i in range(2)]
        SCORES = [PS[:, 2, :], PS[:, 3, :]]
        TURNED = PS[:, 4, :]
        TURNED16 = TURNED.bitcast(BF16)
        OUT2 = [PS[:, 5, :], PS[:, 6, :]]
        MISC = PS[:, 7, :]
        MISC16 = MISC.bitcast(BF16)

        w_loaded = sem("w_loaded")
        rows_loaded = sem("rows_loaded")
        x_loaded_even = sem("x_loaded_even")
        x_loaded_odd = sem("x_loaded_odd")
        const_ready = sem("const_ready")
        dve_seq = sem("dve_seq")
        zeros_ready = sem("zeros_ready")
        amax_ready = sem("amax_ready")
        wt_turned = sem("wt_turned")
        wt_ready = sem("wt_ready")
        cvec_ready = sem("cvec_ready")
        x_turned = sem("x_turned")
        x_t_ready = sem("x_t_ready")
        projected = sem("projected")
        v_first = sem("v_first")
        qk_first = sem("qk_first")
        v_rest = sem("v_rest")
        qk_rest = sem("qk_rest")
        v_rest2 = sem("v_rest2")
        qk_step = sem("qk_step")
        v_parts = sem("v_parts")
        k_rows_ready = sem("k_rows_ready")
        q_rows_ready = sem("q_rows_ready")
        k_turned = sem("k_turned")
        k_cols_ready = sem("k_cols_ready")
        tiles_done = sem("tiles_done")
        q_turned = sem("q_turned")
        q_ready = sem("q_ready")
        scored = sem("scored")
        top_ready = sem("top_ready")
        shift_raw = sem("shift_raw")
        shift_ready = sem("shift_ready")
        shift_turned = sem("shift_turned")
        shift_cols_ready = sem("shift_cols_ready")
        turned_ready = sem("turned_ready")
        prob_ready = sem("prob_ready")
        prob_lo_ready = sem("prob_lo_ready")
        pv_done = sem("pv_done")
        o_ready = sem("o_ready")
        inv_ready = sem("inv_ready")
        coef_ready = sem("coef_ready")
        sum_a = sem("sum_a")
        sum_b = sem("sum_b")
        sum_c = sem("sum_c")
        h_ready = sem("h_ready")
        h_kept = sem("h_kept")
        stat_a = sem("stat_a")
        stat_ready = sem("stat_ready")
        norm_step = sem("norm_step")
        norm_ready = sem("norm_ready")
        hat_ready = sem("hat_ready")
        hat_turned = sem("hat_turned")
        hat_copied = sem("hat_copied")
        xn_ready = sem("xn_ready")
        gated = sem("gated")
        gate_raw = sem("gate_raw")
        gate_ready = sem("gate_ready")
        pre_ready = sem("pre_ready")
        acted = sem("acted")
        hi_ready = sem("hi_ready")
        full_ready = sem("full_ready")
        lo_ready = sem("lo_ready")
        kept_ready = sem("kept_ready")
        saved = sem("saved")
        sp_step = sem("sp_step")
        sp_ready = sem("sp_ready")
        tail_diag = sem("tail_diag")
        tail_wide = sem("tail_wide")
        tail_a = sem("tail_a")
        tail_b = sem("tail_b")
        tail_bb = sem("tail_bb")
        tail_scan = sem("tail_scan")
        tail_carry = sem("tail_carry")
        r_copied = sem("r_copied")
        r_turned = sem("r_turned")
        r_stats = sem("r_stats")
        r_rstd = sem("r_rstd")
        r_aggr = sem("r_aggr")
        r_mul = sem("r_mul")
        readout_scaled = sem("readout_scaled")
        r_gelu = sem("r_gelu")
        readout_normed = sem("readout_normed")
        stats_waited = sem("stats_waited")
        r_dve = sem("r_dve")
        r_step = sem("r_step")
        r_ln_step = sem("r_ln_step")
        r_out = sem("r_out")
        out_done = sem("out_done")
        FREE, TWO_FREE = 1, 2
        start_free = (gate_raw, gate_ready, h_kept, inv_ready, k_cols_ready, k_rows_ready, k_turned, q_rows_ready, qk_rest, r_gelu, readout_scaled, r_stats, r_turned, saved, sum_b, tail_a, tail_bb, tail_carry, tail_scan, tail_wide, tiles_done, v_rest, x_t_ready, prob_ready, shift_turned, shift_cols_ready, o_ready, xn_ready)
        start_two_free = (top_ready, prob_lo_ready, pv_done, turned_ready)


        x_loaded = [x_loaded_even, x_loaded_odd]

        def tile_q(j):
            if isinstance(j, int):
                return j // B
            return nc.s_assert_within(j >> 3, 0, NQ - 1, skip_runtime_bounds_check_because="j is below NT = 8 * NQ")

        def chunk_q(c):
            return nc.s_assert_within(c >> 1, 0, NQ - 1, skip_runtime_bounds_check_because="c is below 2 * NQ")

        def tile_b(j):
            return j % B

        block = ctx.enter_context(nc.Block())

        def places():
            for a, (q, k, v) in enumerate(((0, 0, 0), (0, 1, 1), (1, 1, 1), (1, 0, 0))):
                for n, (signal, at, width) in enumerate(((q, a * D, D), (k, 32 + a * D, D), (v, 64 + a * C, C))):
                    yield 3 * a + n, signal, at, width

        LOADS, ROW_LOADS = 12 + 5 + NH, 12
        x_v = x.rearrange("b (k p) c s -> p b k (c s)", p=P)

        @block.sync
        def _(sp):
            for i in range(2):
                sp.dma_start(x_in[:, i, :, :], x_v[:, i, :, :]).then_inc(x_loaded[i], 16)
            sp.wait_ge(zeros_ready, 1)
            for n, signal, at, width in places():
                sp.dma_start(wall[signal::2, at:at + width], w[n]).then_inc(w_loaded, 16)
            sp.dma_start(res_nat[:, :, :], w_res.rearrange("(m p) k -> p m k", p=P)).then_inc(w_loaded, 16)
            sp.dma_start(in_nat[:, :, :], w_in.rearrange("(m p) k -> p m k", p=P)).then_inc(w_loaded, 16)
            sp.dma_start(b_nat[:, :, :], w_b.rearrange("(m p) k -> p m k", p=P)).then_inc(w_loaded, 16)
            sp.dma_start(ro_nat[:, :], w_ro).then_inc(w_loaded, 16)
            sp.dma_start(gate_nat[:, :], w_gate).then_inc(w_loaded, 16)
            for m in range(NH):
                sp.dma_start(a_cols[:, m:m + 1], ssm_a[m * P:m * P + P].rearrange("(p a) -> p a", a=1)).then_inc(w_loaded, 16)
            with sp.Fori(1, B // 2) as it:
                for i in range(2):
                    sp.wait_ge(x_turned, it * 2 + i - 1)
                    sp.dma_start(x_in[:, i, :, :], x_v[:, bass.ds(it * 2 + i, 1), :, :]).then_inc(x_loaded[i], 16)
            out_v = out.rearrange("b (q p) c -> p q b c", p=P)
            with sp.Fori(0, NT) as j:
                sp.wait_ge(r_out, j + 1)
                sp.dma_start(out_v[:, bass.ds(tile_q(j), 1), bass.ds(j % B, 1), :], gate_all[:, bass.ds(j, 1), :]
                             ).then_inc(out_done, 16)
            sp.wait_ge(out_done, 16 * NT)

        @block.gpsimd
        def _(pool):
            g = nc.gpsimd
            for one in start_free:
                pool.sem_inc(one, FREE)
            for two in start_two_free:
                pool.sem_inc(two, TWO_FREE)
            g.memset(wall[:, :], 0.0)
            g.memset(k_rows[:, :, :].rearrange("p k (a n) -> p (k a) n", n=SLOT)[:, :, 6 * D:], 0.0)
            g.memset(neg_rows[:, :], 0.0)
            g.memset(shift_rows[:, :], 0.0)
            g.memset(q_cols[:, :, :], 0.0)
            g.memset(minus_half[:, :], -0.5)
            g.memset(eps_col[:, :], EPS)
            g.memset(ones[:, :], 1.0)
            g.memset(ident[:, :], 0.0).then_inc(zeros_ready, 1)
            pool.wait_ge(zeros_ready, 1)
            g.memset(neg_rows[0:2, :], -1.0)
            g.affine_select(out=ident[:, :], in_=ident[:, :], compare_op=ALU.not_equal, fill=1.0, base=0,
                            pattern=[[-1, P]], channel_multiplier=1).then_inc(const_ready, 1)
            pool.wait_ge(const_ready, 1)
            g.tensor_copy(ident16[:, :], ident[:, :]).then_inc(const_ready, 1)
            flat = values[:, :, :].rearrange("p k (a w) -> p (k a) w", w=VW)
            g.memset(flat[:, :, 2 * C:2 * C + 2], 1.0).then_inc(const_ready, 1)
            g.memset(xn[:, L * B:], 0.0)
            pool.wait_ge(dve_seq, 3)
            g.partition_all_reduce(setup[:, 3:4], setup[:, 2:3], P, bass.bass_isa.ReduceOp.max).then_inc(amax_ready, 1)

            with pool.Fori(0, B // 2) as it:
                for i in range(2):
                    b = it * 2 + i
                    pool.wait_ge(v_parts, b + 1)
                    v3 = values[:, bass.ds(b * NQ, NQ), :].rearrange("p k (a w) -> p (k a) w", w=VW)
                    g.tensor_copy(v3[:, :, 130:130 + C], rest_v[:, :, :].rearrange("p k (a c) -> p (k a) c", c=C)
                                  ).then_inc(tiles_done, 1)

            def attention(p, j):
                if p in (8, 10, 12, 14):
                    a = (p - 8) // 2
                    pool.wait_ge(prob_ready, j * NA + (a + 1) + FREE)
                    pool.wait_ge(pv_done, j * NA + (a - 1) + TWO_FREE)
                    g.tensor_tensor(prob_lo[:, a % 2, :], prob[:, a % 2, :], prob_hi[:, a % 2, :], ALU.subtract
                                    ).then_inc(prob_lo_ready, 1)

            def finish(p, j):
                if p == 2:
                    pool.wait_ge(o_ready, j + 1 + FREE)
                    g.tensor_tensor(o_sum[:, :, :], o_sb[:, :, C:2 * C], o_sb[:, :, 130:130 + C], ALU.add).then_inc(sum_a, 1)
                    pool.wait_ge(sum_a, j + 1)
                    g.tensor_tensor(o_sum[:, :, :], o_sum[:, :, :], o_sb[:, :, 0:C], ALU.add).then_inc(sum_b, 1)
                if p == 3:
                    pool.wait_ge(coef_ready, j + 1)
                    pool.wait_ge(sum_b, j + 1 + FREE)
                    g.tensor_tensor(o_sum[:, :, :], o_sum[:, :, :], coef[:, :].unsqueeze(2).to_broadcast([P, NA, C]), ALU.mult
                                    ).then_inc(sum_c, 1)
                    pool.wait_ge(sum_c, j + 1)
                    pool.wait_ge(h_kept, j + FREE)
                    o4 = o_sum[:, :, :].rearrange("p (g k) c -> p g k c", k=2)
                    g.tensor_tensor(h_now[:, :].rearrange("p (g c) -> p g c", c=C), o4[:, :, 0, :], o4[:, :, 1, :], ALU.add
                                    ).then_inc(h_ready, 1)
                if p == 6:
                    pool.wait_ge(stat_ready, j + 1)
                    n0 = j * 6

                    def step(i, n):
                        i.then_inc(norm_step, 1)
                        pool.wait_ge(norm_step, n0 + n)
                    step(g.tensor_tensor(small[:, 0:1], mean_var[:, 1:2], eps_col[:, :], ALU.add), 1)
                    step(g.tensor_tensor(small[:, 1:2], small[:, 0:1], minus_half[:, :], ALU.pow), 2)
                    step(g.tensor_tensor(small[:, 2:3], small[:, 1:2], small[:, 1:2], ALU.mult), 3)
                    step(g.tensor_tensor(small[:, 2:3], small[:, 2:3], mean_var[:, 1:2], ALU.mult), 4)
                    step(g.tensor_tensor(small[:, 3:4], small[:, 2:3], eps_col[:, :], ALU.add), 5)
                    step(g.tensor_tensor(small[:, 4:5], small[:, 3:4], minus_half[:, :], ALU.pow), 6)
                    pool.wait_ge(gate_raw, j + FREE)
                    g.tensor_tensor(small[:, 5:6], small[:, 3:4], small[:, 4:5], ALU.mult)
                    g.tensor_tensor(small[:, 6:7], small[:, 1:2], small[:, 4:5], ALU.mult).then_inc(norm_ready, 1)

            def save(i):
                pool.wait_ge(lo_ready, i * STEPS + (STEPS + 1))
                g.tensor_copy(states[:, bass.ds(i, 1), :], s_body[:, :, :].rearrange("p t n -> p (t n)")
                              ).then_inc(saved, 1)

            pool.wait_ge(wt_ready, 1)
            for p in range(STEPS):
                attention(p, 0)
            with pool.Fori(1, AHEAD) as j:
                for p in range(STEPS):
                    finish(p, j - 1)
                    attention(p, j)
            with pool.Fori(0, NT - AHEAD) as i:
                for p in range(STEPS):
                    finish(p, i + (AHEAD - 1))
                    attention(p, i + AHEAD)
                save(i)
            for p in range(STEPS):
                finish(p, NT - 1)
            save(NT - AHEAD)
            with pool.Fori(NT - AHEAD + 1, BODIES) as i:
                save(i)

            with pool.Fori(0, NT) as j:
                pool.wait_ge(r_stats, j + 1 + FREE)
                g.tensor_tensor(tail_small[:, 0:2], tail_mv[:, :, 1:2].rearrange("p r o -> p (r o)"), eps_col[:, :].to_broadcast([P, 2]), ALU.add
                                ).then_inc(r_step, 1)
                pool.wait_ge(r_step, j * 2 + 1)
                g.tensor_tensor(tail_small[:, 2:4], tail_small[:, 0:2], minus_half[:, :].to_broadcast([P, 2]), ALU.pow
                                ).then_inc(r_rstd, 1)
                pool.wait_ge(r_aggr, j + 1)
                g.tensor_tensor(tail_small[:, 4:5], mv_out[:, 1:2], eps_col[:, :], ALU.add).then_inc(r_step, 1)
                pool.wait_ge(r_step, j * 2 + 2)
                g.tensor_tensor(tail_small[:, 5:6], tail_small[:, 4:5], minus_half[:, :], ALU.pow).then_inc(r_ln_step, 1)

        @block.scalar
        def _(act):
            a_ = nc.scalar
            for n, v in enumerate((norm_g, norm_b, w_delta, b_ro)):
                act.dma_start(cols[:, n:n + 1], v.rearrange("(p a) -> p a", a=1)).then_inc(rows_loaded, 16)
            for n, v in enumerate((b_delta, alpha, gamma)):
                act.dma_start(cols[:, 4 + n:5 + n], v.rearrange("(a n) -> a n", a=1).to_broadcast([P, 1])
                               ).then_inc(rows_loaded, 16)
            act.dma_start(mix[:, 0:1], alpha.rearrange("(a n) -> a n", a=1).to_broadcast([P, 1])).then_inc(rows_loaded, 16)
            act.dma_start(mix[:, 2:3], gamma.rearrange("(a n) -> a n", a=1).to_broadcast([P, 1])).then_inc(rows_loaded, 16)
            act.dma_start(ro_g_row[:, :], ro_g.rearrange("(a n) -> a n", a=1).to_broadcast([P, H])).then_inc(rows_loaded, 16)
            act.dma_start(ro_b_row[:, :], ro_b.rearrange("(a n) -> a n", a=1).to_broadcast([P, H])).then_inc(rows_loaded, 16)
            act.dma_start(b_gate_row[:, :], b_gate.rearrange("(a n) -> a n", a=1).to_broadcast([P, P])).then_inc(rows_loaded, 16)
            act.preload_act_table(ACT.Exp)
            with act.Fori(0, B // 2) as it:
                for i in range(2):
                    b = it * 2 + i
                    act.wait_ge(x_turned, b + 1)
                    a_.copy(x_t[:, i, :, :].rearrange("p k n -> p (k n)"), MISC).then_inc(x_t_ready, 1)
                    act.wait_ge(projected, b + 1)
                    act.wait_ge(const_ready, 3)
                    for k in range(NQ):
                        v1 = values[:, bass.ds(b * NQ + k, 1), :].rearrange("p o (a w) -> p (o a) w", w=VW)
                        last = a_.copy(v1[:, :, 0:C], PS[:, 2 + k, 64:64 + NA * C].rearrange("p (a c) -> p a c", c=C))
                    last.then_inc(v_first, 1)
                    act.wait_ge(k_rows_ready, b + FREE)
                    act.wait_ge(q_rows_ready, b + FREE)
                    a_.copy(part[:, 0, :, :, :].rearrange("p h k n -> p k h n"),
                            PS[:, 2:6, 0:64].rearrange("p k (h n) -> p k h n", h=2)).then_inc(qk_first, 1)
                    act.wait_ge(k_turned, b + 1 + FREE)
                    a_.copy(k_cols[:, bass.ds(b, 1), :, :].rearrange("p o a n -> p (o a n)"), OUT2[1].bitcast(BF16)
                            ).then_inc(k_cols_ready, 1)

            def attention(p, j):
                if p == 0:
                    act.wait_ge(q_turned, j + 1)
                    act.wait_ge(turned_ready, j * NA + TWO_FREE)
                    a_.copy(q_cols[0:64, 0::2, :], TURNED16[0:64, 0:2 * P].rearrange("p (h n) -> p h n", h=2))
                    a_.copy(q_cols[64:P, 1::2, :], TURNED16[64:P, 0:2 * P].rearrange("p (h n) -> p h n", h=2)
                            ).then_inc(q_ready, 1)
                if p in (4, 6, 8, 10):
                    a = (p - 4) // 2
                    act.wait_ge(shift_turned, j * NA + (a + 1) + FREE)
                    act.wait_ge(turned_ready, j * NA + (a - 1) + TWO_FREE)
                    a_.copy(shift_cols[:, a % 2, :], MISC16[:, 0:P]).then_inc(shift_cols_ready, 1)
                if p in (7, 9, 11, 13):
                    a = (p - 7) // 2
                    act.wait_ge(turned_ready, j * NA + (a + 1) + TWO_FREE)
                    act.wait_ge(prob_lo_ready, j * NA + (a - 1) + TWO_FREE)
                    act.wait_ge(pv_done, j * NA + (a - 1) + TWO_FREE)
                    a_.activation(prob[:, a % 2, :], TURNED, ACT.Exp, scale=float(D) ** -0.5)
                    a_.activation(prob_hi[:, a % 2, :], TURNED, ACT.Exp, scale=float(D) ** -0.5).then_inc(prob_ready, 1)

            def finish(p, j):
                if p == 1:
                    act.wait_ge(pv_done, j * NA + NA + TWO_FREE)
                    act.wait_ge(sum_b, j + FREE)
                    act.wait_ge(inv_ready, j + FREE)
                    for n in range(2):
                        last = a_.copy(o_sb[:, 2 * n:2 * n + 2, :],
                                       OUT2[n].rearrange("p (a w) -> p a w", a=2)[:, :, 0:VW])
                    last.then_inc(o_ready, 1)
                if p == 5:
                    act.wait_ge(h_ready, j + 1)
                    a_.copy(h_all[:, bass.ds(j, 1), :].rearrange("p o n -> p (o n)"), h_now[:, :]).then_inc(h_kept, 1)
                if p == 15:
                    act.wait_ge(gate_raw, j + 1 + FREE)
                    a_.activation(gate_all[:, bass.ds(j, 1), :].rearrange("p o n -> p (o n)"), gate_pre[:, :], ACT.Tanh,
                                  scale=0.5).then_inc(gate_ready, 1)

            def scan(t, i):
                act.wait_ge(pre_ready, i * STEPS + (t + 1))
                a_.activation(y[:, :].rearrange("p (m b) -> p m b", m=NH), PRE[t // 8][:, :, t % 8, :], ACT.Tanh,
                              scale=setup[:, 7:8]).then_inc(acted, 1)

            for p in range(STEPS):
                attention(p, 0)
            with act.Fori(1, AHEAD) as j:
                for p in range(STEPS):
                    attention(p, j)
                    finish(p, j - 1)
            with act.Fori(0, NT - AHEAD) as i:
                for t in range(STEPS):
                    scan(t, i)
                    attention(t, i + AHEAD)
                    finish(t, i + (AHEAD - 1))
            for t in range(STEPS):
                scan(t, NT - AHEAD)
                finish(t, NT - 1)
            with act.Fori(NT - AHEAD + 1, BODIES) as i:
                for t in range(STEPS):
                    scan(t, i)

            act.preload_act_table_set("natural_log_exp_and_others")
            act.wait_ge(sp_step, 2)
            a_.activation(sp_tmp[:, 0, :], sp_tmp[:, 0, :], ACT.Exp, scale=-1.0).then_inc(sp_ready, 1)
            act.wait_ge(sp_ready, 1)
            a_.activation(sp_tmp[:, 0, :], sp_tmp[:, 0, :], ACT.Ln, bias=1.0).then_inc(sp_ready, 1)
            with act.Fori(0, 2 * NQ) as c:
                act.wait_ge(tail_wide, c + 1 + FREE)
                act.wait_ge(tail_scan, c + FREE)
                for m in range(NH):
                    last = a_.activation(ssm_a_bar[:, m, :], PS[:, 0, :], ACT.Exp, scale=a_cols[:, m:m + 1])
                last.then_inc(tail_a, 1)
            act.preload_act_table(ACT.Gelu)
            with act.Fori(0, NT) as j:
                act.wait_ge(r_gelu, j + FREE)
                act.wait_ge(r_turned, j + FREE)
                src = states[:, bass.ds(tile_q(j) * B, B), :].rearrange("p i (t m b) -> p m (i t) b", m=NH, b=B)
                a_.mul(r_in[:, 0, :, :], src[:, :, :, bass.ds(j % B, 1)].rearrange("p m t o -> p m (t o)"), 1.0 / STATE_UP
                       )
                a_.copy(r_in[:, 1, :, :], ssm_states[:, :, bass.ds(tile_q(j), 1), bass.ds((j % B) * P, P)].rearrange("p m o n -> p m (o n)")
                        ).then_inc(r_copied, 1)
                act.wait_ge(readout_scaled, j + 1 + FREE)
                a_.activation(r_act[:, :, :], r_pre[:, :, :], ACT.Gelu).then_inc(r_gelu, 1)

        @block.vector
        def _(dve):
            v = nc.vector
            dve.wait_ge(w_loaded, 16 * LOADS)
            dve.wait_ge(rows_loaded, 16 * ROW_LOADS)
            dve.wait_ge(const_ready, 1)
            n = [0]

            def seq(i):
                n[0] += 1
                i.then_inc(dve_seq, 1)
                dve.wait_ge(dve_seq, n[0])
            seq(v.tensor_scalar(res_abs, res_nat[:, :, :].rearrange("p m k -> p (m k)"), -1.0, None, ALU.mult))
            seq(v.tensor_tensor(res_abs, res_abs,
                                res_nat[:, :, :].rearrange("p m k -> p (m k)"), ALU.max))
            seq(v.reduce_max(setup[:, 2:3], res_abs, AX_X))
            dve.wait_ge(amax_ready, 1)
            seq(v.tensor_scalar(setup[:, 4:5], setup[:, 3:4], 2.0 ** -100, None, ALU.max))
            seq(v.tensor_scalar(setup[:, 4:5].bitcast(I32), setup[:, 4:5].bitcast(I32), 0x7F800000, None, ALU.bitwise_and))
            seq(v.reciprocal(setup[:, 5:6], setup[:, 4:5]))
            v.tensor_scalar(setup[:, 6:7], setup[:, 5:6], WEIGHT_UP, None, ALU.mult)
            v.tensor_scalar(setup[:, 7:8], setup[:, 4:5], 1.0 / (WEIGHT_UP * STATE_UP), None, ALU.mult)
            seq(v.tensor_scalar(setup[:, 8:9], setup[:, 5:6], WEIGHT_UP * STATE_UP, None, ALU.mult))
            seq(v.tensor_scalar(neg_inv_a[:, :], a_cols[:, :], 1e-8, None, ALU.add))
            seq(v.reciprocal(neg_inv_a[:, :], neg_inv_a[:, :]))
            seq(v.tensor_scalar(neg_inv_a[:, :], neg_inv_a[:, :], -1.0, None, ALU.mult))
            for m in range(NH):
                v.tensor_scalar(b_nat[:, m, :], b_nat[:, m, :], neg_inv_a[:, m:m + 1], None, ALU.mult)
            v.tensor_tensor(ro_tmp[:, :], ro_nat[:, :], ro_b_row[:, :], ALU.mult)
            seq(v.tensor_tensor(ro_nat[:, :], ro_nat[:, :], ro_g_row[:, :], ALU.mult))
            v.reduce_sum(setup[:, 9:10], ro_nat[:, :], AX_X)
            seq(v.reduce_sum(setup[:, 10:11], ro_tmp[:, :], AX_X))
            seq(v.tensor_scalar(setup[:, 9:10], setup[:, 9:10], 1.0 / H, None, ALU.mult))
            v.tensor_scalar(ro_nat[:, :], ro_nat[:, :], setup[:, 9:10], None, ALU.subtract)
            seq(v.tensor_tensor(setup[:, 10:11], setup[:, 10:11], cols[:, 3:4], ALU.add))
            v.tensor_scalar(ro_tmp[:, 0:P], ident[:, :], setup[:, 10:11], None, ALU.mult)
            v.tensor_tensor(setup[:, 11:12], cols[:, 1:2], cols[:, 2:3], ALU.mult)
            v.tensor_tensor(gate_t[:, P:P + 1], cols[:, 0:1], cols[:, 2:3], ALU.mult)
            v.memset(q_rows[:, :, :, :].rearrange("p k b (a n) -> p (k b a) n", n=SLOT)[:, :, 6 * D:], 0.0)
            v.memset(mix[:, 1:2], 1.0)
            v.memset(mix[:, 3:4], 1.0)
            v.memset(kept[:, :], 0.0).then_inc(kept_ready, 1)
            v.memset(s_hi[:, :], 0.0).then_inc(hi_ready, 1)
            v.memset(s_lo[:, :], 0.0).then_inc(lo_ready, 1)
            seq(v.memset(z_all[:, :], 0.0))
            v.memset(carry[:, :, :], 0.0).then_inc(cvec_ready, 1)
            dve.wait_ge(wt_turned, 1)
            seq(v.tensor_scalar(res_hi[:, :, :].rearrange("p k m -> p (k m)"), PS[:, 2, :], setup[:, 6:7], None, ALU.mult))
            v.scalar_tensor_tensor(res_lo[:, :, :].rearrange("p k m -> p (k m)"), PS[:, 2, :], setup[:, 6:7],
                                   res_hi[:, :, :].rearrange("p k m -> p (k m)"), ALU.mult, ALU.subtract)
            v.tensor_scalar(in_t[:, :], PS[:, 3, 0:H], setup[:, 8:9], None, ALU.mult)
            v.tensor_copy(b_t[:, :], PS[:, 3, H:2 * H])
            v.tensor_copy(gate_t[:, 0:P], PS[:, 4, 0:P])
            v.tensor_copy(ro_t[:, :, :].rearrange("p m n -> p (m n)"), PS[:, 4, P:3 * P])
            v.tensor_copy(ro_row[:, :], PS[:, 5, 0:P])
            v.tensor_tensor(setup[:, 12:13], PS[:, 5, P:P + 1], cols[:, 4:5], ALU.add).then_inc(wt_ready, 1)

            with dve.Fori(0, B // 2) as it:
                for i in range(2):
                    b = it * 2 + i
                    vals = values[:, bass.ds(b * NQ, NQ), :].rearrange("p k (a w) -> p (k a) w", w=VW)
                    rest = rest_v[:, :, :].rearrange("p k (a c) -> p (k a) c", c=C)
                    dve.wait_ge(qk_first, b + 1)
                    dve.wait_ge(tiles_done, b + FREE)
                    for k in range(NQ):
                        one = values[:, bass.ds(b * NQ + k, 1), :].rearrange("p o (a w) -> p (o a) w", w=VW)
                        last = v.tensor_tensor(rest_v[:, k, :].rearrange("p (a c) -> p a c", c=C),
                                               PS[:, 2 + k, 64:64 + NA * C].rearrange("p (a c) -> p a c", c=C),
                                               one[:, :, 0:C], ALU.subtract)
                    last.then_inc(v_rest, 1)
                    v.tensor_tensor(rest_qk[:, :, :, :].rearrange("p h k n -> p k h n"),
                                    PS[:, 2:6, 0:64].rearrange("p k (h n) -> p k h n", h=2),
                                    part[:, 0, :, :, :].rearrange("p h k n -> p k h n"), ALU.subtract).then_inc(qk_rest, 1)
                    dve.wait_ge(v_rest, b + 1 + FREE)
                    v.tensor_copy(vals[:, :, C:2 * C], rest).then_inc(v_rest2, 1)
                    dve.wait_ge(qk_rest, b + 1 + FREE)
                    r = rest_qk[:, :, :, :].rearrange("p h k n -> p (h k n)")
                    p2 = part[:, 1, :, :, :].rearrange("p h k n -> p (h k n)")
                    v.tensor_copy(p2, r).then_inc(qk_step, 1)
                    dve.wait_ge(v_rest2, b + 1)
                    v.tensor_tensor(rest, rest, vals[:, :, C:2 * C], ALU.subtract).then_inc(v_parts, 1)
                    dve.wait_ge(qk_step, b * 2 + 1)
                    v.tensor_tensor(part[:, 2, :, :, :].rearrange("p h k n -> p (h k n)"), r, p2, ALU.subtract
                                    ).then_inc(qk_step, 1)
                    dve.wait_ge(qk_step, b * 2 + 2)
                    dve.wait_ge(k_turned, b + FREE)
                    kr = k_rows[:, :, :].rearrange("p k (a n) -> p (k a) n", n=SLOT)
                    qr = q_rows[:, :, bass.ds(b, 1), :].rearrange("p k o (a n) -> p k (o a) n", n=SLOT)
                    pk = part[:, :, 1, :, :].rearrange("p l k (a d) -> p l (k a) d", d=D)
                    pq = part[:, :, 0, :, :].rearrange("p l k (a d) -> p l k a d", d=D)
                    for l, slots in enumerate(((0, 1, 2), (3, 4), (5,))):
                        for z in slots:
                            last = v.tensor_copy(kr[:, :, z * D:z * D + D], pk[:, l, :, :])
                    last.then_inc(k_rows_ready, 1)
                    for l, slots in enumerate(((0, 3, 5), (1, 4), (2,))):
                        for z in slots:
                            last = v.tensor_copy(qr[:, :, :, z * D:z * D + D], pq[:, l, :, :, :])
                    last.then_inc(q_rows_ready, 1)

            def attention(p, j):
                if p in (2, 4, 6, 8):
                    a = (p - 2) // 2
                    dve.wait_ge(scored, j * NA + (a + 1))
                    v.reduce_max(top[:, a % 2:a % 2 + 1], SCORES[a % 2], AX_X).then_inc(top_ready, 1)
                if p in (3, 5, 7, 9):
                    a = (p - 3) // 2
                    dve.wait_ge(top_ready, j * NA + (a + 1) + TWO_FREE)
                    dve.wait_ge(shift_turned, j * NA + a + FREE)
                    v.tensor_scalar(shift_rows[:, 0:1], top[:, a % 2:a % 2 + 1], SHIFT, None, ALU.subtract)
                    v.tensor_scalar(shift[:, :], top[:, a % 2:a % 2 + 1], SHIFT, None, ALU.subtract).then_inc(shift_raw, 1)
                    dve.wait_ge(shift_raw, j * NA + (a + 1))
                    v.tensor_tensor(shift_rows[:, 1:2], shift[:, :], shift_rows[:, 0:1], ALU.subtract).then_inc(shift_ready, 1)

            def finish(p, j):
                if p == 2:
                    dve.wait_ge(o_ready, j + 1 + FREE)
                    v.reciprocal(coef[:, :], o_sb[:, :, 2 * C:2 * C + 1].rearrange("p a o -> p (a o)")).then_inc(inv_ready, 1)
                    dve.wait_ge(inv_ready, j + 1 + FREE)
                    v.tensor_tensor(coef[:, :], coef[:, :], mix[:, :], ALU.mult).then_inc(coef_ready, 1)
                if p == 5:
                    dve.wait_ge(h_ready, j + 1)
                    v.bn_stats(stats[:, :], h_now[:, :]).then_inc(stat_a, 1)
                    dve.wait_ge(stat_a, j + 1)
                    dve.sem_inc(stats_waited, 1)
                    v.bn_aggr(mean_var[:, :], stats[:, :]).then_inc(stat_ready, 1)
                if p == 8:
                    dve.wait_ge(norm_ready, j + 1)
                    v.tensor_scalar(x_hat[:, :], h_now[:, :], mean_var[:, 0:1], small[:, 6:7], ALU.subtract, ALU.mult
                                    ).then_inc(hat_ready, 1)
                if p == 10:
                    dve.wait_ge(hat_turned, j + 1)
                    v.tensor_copy(x_hat_t[:, :], MISC[:, 0:P]).then_inc(hat_copied, 1)
                    dst = xn[:, 0:L * B].rearrange("p (q t b) -> p q t b", q=NQ, b=B)
                    v.tensor_scalar(dst[:, bass.ds(tile_q(j), 1), :, bass.ds(j % B, 1)].rearrange("p q t o -> p (q t o)"),
                                    MISC[:, 0:P], cols[:, 0:1], cols[:, 1:2], ALU.mult, ALU.add).then_inc(xn_ready, 1)
                if p == 15:
                    dve.wait_ge(gated, j + 1)
                    dve.wait_ge(gate_ready, j + FREE)
                    v.tensor_scalar(z_all[:, bass.ds(j, 1)], MISC[:, P:P + 1], setup[:, 12:13], None, ALU.add)
                    v.scalar_tensor_tensor(gate_pre[:, :], MISC[:, 0:P], small[:, 5:6], b_gate_row[:, :], ALU.mult, ALU.add
                                           ).then_inc(gate_raw, 1)

            def scan(t, i):
                n = i * STEPS + (t + 1)
                dve.wait_ge(kept_ready, n)
                dve.wait_ge(acted, n)
                v.scalar_tensor_tensor(s_hi[:, :], y[:, :], LEAK * STATE_UP, kept[:, :], ALU.mult, ALU.add).then_inc(hi_ready, 1)
                if t == 0:
                    dve.wait_ge(saved, i + FREE)
                v.scalar_tensor_tensor(s_body[:, t, :], y[:, :], LEAK * STATE_UP, kept[:, :], ALU.mult, ALU.add
                                       ).then_inc(full_ready, 1)
                dve.wait_ge(full_ready, n)
                v.tensor_tensor(s_lo[:, :], s_body[:, t, :], s_hi[:, :], ALU.subtract).then_inc(lo_ready, 1)
                v.tensor_scalar(kept[:, :], s_body[:, t, :], KEEP, None, ALU.mult).then_inc(kept_ready, 1)

            for p in range(STEPS):
                attention(p, 0)
            with dve.Fori(1, AHEAD) as j:
                for p in range(STEPS):
                    attention(p, j)
                    finish(p, j - 1)
            with dve.Fori(0, NT - AHEAD) as i:
                for t in range(STEPS):
                    scan(t, i)
                    attention(t, i + AHEAD)
                    finish(t, i + (AHEAD - 1))
            for t in range(STEPS):
                scan(t, NT - AHEAD)
                finish(t, NT - 1)
            with dve.Fori(NT - AHEAD + 1, BODIES) as i:
                for t in range(STEPS):
                    scan(t, i)

            dve.wait_ge(gate_raw, NT + FREE)
            v.tensor_scalar(sp_tmp[:, 1, :], z_all[:, :], -1.0, None, ALU.mult).then_inc(sp_step, 1)
            dve.wait_ge(sp_step, 1)
            v.tensor_tensor(sp_tmp[:, 0, :], z_all[:, :], sp_tmp[:, 1, :], ALU.max).then_inc(sp_step, 1)
            v.tensor_scalar(delta[:, :], z_all[:, :], 0.0, None, ALU.max).then_inc(sp_step, 1)
            dve.wait_ge(sp_ready, 2)
            dve.wait_ge(sp_step, 3)
            v.tensor_tensor(delta[:, :], delta[:, :], sp_tmp[:, 0, :], ALU.add).then_inc(sp_step, 1)
            dve.wait_ge(sp_step, 4)
            dve.wait_ge(pv_done, NA * NT + TWO_FREE)
            with dve.Fori(0, 2 * NQ) as c:
                dve.wait_ge(tail_wide, c + FREE)
                for k in range(4):
                    last = v.tensor_scalar(diag[:, k * P:(k + 1) * P], ident[:, :], delta[:, bass.ds(c * 4 + k, 1)], None, ALU.mult)
                last.then_inc(tail_diag, 1)
                dve.wait_ge(tail_a, c + 1 + FREE)
                dve.wait_ge(tail_b, c + 1)
                for m in range(NH):
                    last = v.scalar_tensor_tensor(ssm_b_bar[:, m, :], ssm_a_bar[:, m, :], 1.0, PS[:, 1 + m, :],
                                                  ALU.subtract, ALU.mult)
                last.then_inc(tail_bb, 1)
                dve.wait_ge(tail_bb, c + 1 + FREE)
                dve.wait_ge(tail_carry, c + FREE)
                for m in range(NH):
                    for k in range(4):
                        at = k * P
                        last = v.tensor_tensor_scan(
                            ssm_states[:, m, bass.ds(chunk_q(c), 1), bass.ds((c % 2) * 4 * P + at, P)].rearrange("p o n -> p (o n)"),
                            ssm_a_bar[:, m, at:at + P], ssm_b_bar[:, m, at:at + P],
                            carry[:, m, bass.ds((c % 2) * 4 + k, 1)], ALU.mult, ALU.add)
                last.then_inc(tail_scan, 1)
                dve.wait_ge(tail_scan, c + 1 + FREE)
                for m in range(NH):
                    ends = ssm_states[:, m, bass.ds(chunk_q(c), 1), bass.ds((c % 2) * 4 * P, 4 * P)].rearrange("p o (k n) -> p (o k) n", n=P)
                    last = v.tensor_copy(carry[:, m, bass.ds((c % 2) * 4, 4)], ends[:, :, P - 1:P].rearrange("p k o -> p (k o)"))
                last.then_inc(tail_carry, 1)

            with dve.Fori(0, NT) as j:
                dve.wait_ge(r_turned, j + 1 + FREE)
                for r in range(2):
                    v.bn_stats(tail_st[:, r, :], PS[:, r, 0:H])
                v.memset(sp_tmp[:, 1, 0:1], 0.0).then_inc(r_dve, 1)
                dve.wait_ge(r_dve, j * 5 + 1)
                dve.sem_inc(stats_waited, 1)
                for r in range(2):
                    last = v.bn_aggr(tail_mv[:, r, :], tail_st[:, r, :])
                last.then_inc(r_stats, 1)
                dve.wait_ge(r_rstd, j + 1)
                dve.wait_ge(r_mul, j + 1)
                dve.wait_ge(r_gelu, j + FREE)
                for r in range(2):
                    last = v.scalar_tensor_tensor(r_pre[:, r, :], PS[:, 2 + r, 0:P], tail_small[:, 2 + r:3 + r], ro_row[:, :],
                                                  ALU.mult, ALU.add)
                last.then_inc(readout_scaled, 1)
                dve.wait_ge(r_gelu, j + 1 + FREE)
                gate = gate_all[:, bass.ds(j, 1), :].rearrange("p o n -> p (o n)")
                dve.wait_ge(gate_ready, NT + FREE)
                v.tensor_scalar(r_gate, gate, 0.5, 0.5, ALU.mult, ALU.add)
                v.tensor_tensor(r_mix, r_act[:, 0, :], r_act[:, 1, :], ALU.subtract).then_inc(r_dve, 1)
                dve.wait_ge(r_dve, j * 5 + 2)
                v.tensor_tensor(r_mix, r_mix, r_gate, ALU.mult)
                v.tensor_tensor(r_h2, r_act[:, 1, :], h_all[:, bass.ds(j, 1), :].rearrange("p o n -> p (o n)"), ALU.add
                                ).then_inc(r_dve, 1)
                dve.wait_ge(r_dve, j * 5 + 3)
                v.tensor_tensor(r_h2, r_h2, r_mix, ALU.add).then_inc(r_dve, 1)
                dve.wait_ge(r_dve, j * 5 + 4)
                v.bn_stats(st_out[:, :], r_h2).then_inc(r_dve, 1)
                dve.wait_ge(r_dve, j * 5 + 5)
                dve.sem_inc(stats_waited, 1)
                v.bn_aggr(mv_out[:, :], st_out[:, :]).then_inc(r_aggr, 1)
                dve.wait_ge(r_ln_step, j + 1)
                dve.wait_ge(r_aggr, j + 1)
                v.tensor_scalar(r_mix, r_h2, mv_out[:, 0:1], tail_small[:, 5:6], ALU.subtract, ALU.mult).then_inc(readout_normed, 1)
                dve.wait_ge(readout_normed, j + 1)
                v.tensor_tensor(gate, r_mix, r_h2, ALU.add).then_inc(r_out, 1)

        @block.tensor
        def _(pe):
            t_ = nc.tensor
            pe.wait_ge(cvec_ready, 1)
            pe.wait_ge(const_ready, 2)
            for m in range(NH):
                for k in range(NH):
                    t_.transpose(PS[:, 2, k * H + m * P:k * H + m * P + P], res_nat[:, m, k * P:k * P + P], ident[:, :])
                t_.transpose(PS[:, 3, m * P:m * P + P], in_nat[:, m, :], ident[:, :])
                t_.transpose(PS[:, 3, H + m * P:H + m * P + P], b_nat[:, m, :], ident[:, :])
                t_.transpose(PS[:, 4, P + m * P:2 * P + m * P], ro_nat[:, m * P:m * P + P], ident[:, :])
            t_.transpose(PS[:, 4, 0:P], gate_nat[:, :], ident[:, :])
            t_.matmul(PS[:, 5, 0:P], ones[:, :], ro_tmp[:, 0:P], start=True, stop=True)
            t_.matmul(PS[:, 5, P:P + 1], ones[:, :], setup[:, 11:12], start=True, stop=True).then_inc(wt_turned, 1)

            pe.wait_ge(wt_ready, 1)
            with pe.Fori(0, B // 2) as it:
                for i in range(2):
                    b = it * 2 + i
                    pe.wait_ge(x_loaded[i], it * 16 + 16)
                    pe.wait_ge(x_t_ready, b + FREE)
                    for k in range(NQ):
                        last = t_.transpose(MISC[:, k * P:k * P + P], x_in[:, i, k, :], ident[:, :])
                    last.then_inc(x_turned, 1)
                    pe.wait_ge(x_t_ready, b + 1 + FREE)
                    pe.wait_ge(v_rest, b + FREE)
                    pe.wait_ge(qk_rest, b + FREE)
                    for k in range(NQ):
                        last = t_.matmul(PS[:, 2 + k, 0:64 + NA * C], x_t[:, i, k, :], wall[:, :], start=True, stop=True)
                    last.then_inc(projected, 1)
                    pe.wait_ge(k_rows_ready, b + 1 + FREE)
                    pe.wait_ge(k_cols_ready, b + FREE)
                    turned = OUT2[1].bitcast(BF16).rearrange("p (a k n) -> p a k n", a=2, k=NQ)
                    for k in range(NQ):
                        for a in range(2):
                            last = t_.transpose(turned[:, a, k, :], k_rows[:, k, a * P:a * P + P], ident16[:, :])
                    last.then_inc(k_turned, 1)
            pe.wait_ge(k_cols_ready, B + FREE)
            pe.wait_ge(tiles_done, B + FREE)
            pe.wait_ge(q_rows_ready, B + FREE)

            def attention(p, j):
                if p == 0:
                    pe.wait_ge(prob_ready, j * NA + FREE)
                    rows = q_rows[:, :, :, :].rearrange("p k b n -> p (k b) n")
                    for a in range(2):
                        last = t_.transpose(TURNED16[:, a * P:a * P + P],
                                            rows[:, bass.ds(j, 1), a * P:a * P + P].rearrange("p o n -> p (o n)"), ident16[:, :])
                    last.then_inc(q_turned, 1)
                keys = k_cols[:, bass.ds(j % B, 1), :, :].rearrange("p o a n -> p (o a) n")
                if p in (1, 3, 5, 7):
                    a = (p - 1) // 2
                    pe.wait_ge(q_ready, j + 1)
                    pe.wait_ge(top_ready, j * NA + (a - 1) + TWO_FREE)
                    t_.matmul(SCORES[a % 2], q_cols[:, a, :], keys[:, a // 2, :], start=True, stop=True).then_inc(scored, 1)
                if p in (4, 6, 8, 10):
                    a = (p - 4) // 2
                    pe.wait_ge(shift_ready, j * NA + (a + 1))
                    pe.wait_ge(shift_cols_ready, j * NA + a + FREE)
                    if p == 10:
                        pe.wait_ge(xn_ready, j + FREE)
                    t_.transpose(MISC16[:, 0:P], shift_rows[:, :], ident16[:, :]).then_inc(shift_turned, 1)
                if p in (6, 8, 10, 12):
                    a = (p - 6) // 2
                    pe.wait_ge(shift_cols_ready, j * NA + (a + 1) + FREE)
                    pe.wait_ge(prob_ready, j * NA + a + FREE)
                    t_.matmul(TURNED.rearrange("p (k n) -> p k n", k=NQ), neg_rows[:, :],
                              shift_cols[:, a % 2, :].unsqueeze(1).to_broadcast([P, NQ, P]), start=True, stop=False,
                              skip_group_check=True)
                    for k in range(NQ):
                        last = t_.matmul(TURNED[:, k * P:k * P + P], keys[:, a // 2, k * P:k * P + P], q_cols[:, a, :],
                                         start=False, stop=k == NQ - 1, skip_group_check=True)
                    last.then_inc(turned_ready, 1)
                if p in (11, 13, 15):
                    weigh((p - 11) // 2, j)

            def weigh(a, j):
                pe.wait_ge(prob_lo_ready, j * NA + (a + 1) + TWO_FREE)
                if a == 0:
                    pe.wait_ge(o_ready, j + FREE)
                dst = OUT2[a // 2][:, (a % 2) * 256:(a % 2) * 256 + VW]
                for k in range(NQ):
                    vals = values[:, bass.ds((j % B) * NQ + k, 1), a * VW:a * VW + VW].rearrange("p o w -> p (o w)")
                    t_.matmul(dst, prob_hi[:, a % 2, k * P:k * P + P], vals, start=k == 0, stop=False, skip_group_check=True)
                    last = t_.matmul(dst[:, 0:130], prob_lo[:, a % 2, k * P:k * P + P], vals[:, 0:130], start=False,
                                     stop=k == NQ - 1, skip_group_check=True)
                last.then_inc(pv_done, 1)

            def finish(p, j, more=True):
                if p == 0:
                    weigh(NA - 1, j)
                if p == 9:
                    pe.wait_ge(hat_ready, j + 1)
                    if more:
                        pe.wait_ge(shift_cols_ready, (j + 1) * NA + 3 + FREE)
                    else:
                        pe.wait_ge(shift_cols_ready, (j + 1) * NA + FREE)
                    t_.transpose(MISC[:, 0:P], x_hat[:, :], ident[:, :]).then_inc(hat_turned, 1)
                if p == 14:
                    pe.wait_ge(hat_copied, j + 1)
                    pe.wait_ge(xn_ready, j + 1 + FREE)
                    if more:
                        pe.wait_ge(shift_cols_ready, (j + 2) * NA + FREE)
                    t_.matmul(MISC[:, 0:P + 1], x_hat_t[:, :], gate_t[:, :], start=True, stop=True).then_inc(gated, 1)

            def scan(t, i):
                n = i * STEPS + (t + 1)
                pe.wait_ge(hi_ready, n)
                dst = PRE[t // 8][:, :, t % 8, :]
                for wts, st in ((res_hi, s_hi), (res_lo, s_hi), (res_hi, s_lo)):
                    if st is s_lo:
                        pe.wait_ge(lo_ready, n)
                    for k in range(NH):
                        for m in range(NH):
                            last = t_.matmul(dst[:, m, :], wts[:, k, m * P:m * P + P], st[:, k * B:k * B + B],
                                             start=False, stop=st is s_lo and k == NH - 1, skip_group_check=True)
                last.then_inc(pre_ready, 1)

            def fill(m, half, i):
                src = xn[:, bass.ds(i * SB + half * HALF, HALF)]
                t_.matmul(PS[:, half, m * HALF:m * HALF + HALF], in_t[:, m * P:m * P + P], src, start=m == 0, stop=True,
                          skip_group_check=True)

            def scan_body(t, i):
                scan(t, i)
                if t in (2, 4):
                    fill((t - 2) // 2, 1, i)
                if t in (12, 14):
                    fill((t - 12) // 2, 0, i + 1)

            for p in range(STEPS):
                attention(p, 0)
            with pe.Fori(1, AHEAD) as j:
                for p in range(STEPS):
                    finish(p, j - 1)
                    attention(p, j)
            pe.wait_ge(xn_ready, B + FREE)
            fill(0, 0, 0)
            fill(1, 0, 0)
            with pe.Fori(0, NT - AHEAD) as i:
                for t in range(STEPS):
                    if t == 0:
                        scan(t, i)
                    else:
                        if t == 12:
                            pe.wait_ge(xn_ready, i + AHEAD + FREE)
                        scan_body(t, i)
                    finish(t, i + (AHEAD - 1))
                    attention(t, i + AHEAD)
            for t in range(STEPS):
                if t == 12:
                    pe.wait_ge(xn_ready, NT + FREE)
                scan_body(t, NT - AHEAD)
                finish(t, NT - 1, more=False)
            with pe.Fori(NT - AHEAD + 1, BODIES) as i:
                for t in range(STEPS):
                    scan_body(t, i)

            xq = xn[:, 0:L * B].rearrange("p (q t b) -> p q b t", q=NQ, b=B)
            pe.wait_ge(acted, L)
            with pe.Fori(0, 2 * NQ) as c:
                pe.wait_ge(tail_diag, c + 1)
                pe.wait_ge(tail_a, c + FREE)
                t_.matmul(PS[:, 0, :], ones[:, :], diag, start=True, stop=True).then_inc(tail_wide, 1)
                pe.wait_ge(tail_bb, c + FREE)
                for m in range(NH):
                    last = t_.matmul(PS[:, 1 + m, :].rearrange("p (b t) -> p b t", t=P), b_t[:, m * P:m * P + P],
                                     xq[:, bass.ds(chunk_q(c), 1), bass.ds((c % 2) * 4, 4), :].rearrange("p o b t -> p (o b) t"),
                                     start=True, stop=True)
                last.then_inc(tail_b, 1)
            pe.wait_ge(tail_bb, 2 * NQ + FREE)
            with pe.Fori(0, NT) as j:
                pe.wait_ge(r_copied, j + 1)
                pe.wait_ge(r_stats, j + FREE)
                pe.wait_ge(readout_scaled, j + FREE)
                for r in range(2):
                    for m in range(NH):
                        last = t_.transpose(PS[:, r, m * P:m * P + P], r_in[:, r, m, :], ident[:, :])
                last.then_inc(r_turned, 1)
                for r in range(2):
                    for m in range(NH):
                        last = t_.matmul(PS[:, 2 + r, 0:P], r_in[:, r, m, :], ro_t[:, m, :], start=m == 0, stop=m == NH - 1)
                last.then_inc(r_mul, 1)


_WEIGHTS = [f"L0_tok_w{n}" for n in range(1, 13)]
_OTHERS = ["L0_tok_alpha", "L0_tok_gamma", "L0_attn_norm_g", "L0_attn_norm_b", "L0_attn_W_in", "L0_attn_W_res",
           "L0_attn_A", "L0_attn_W_B", "L0_attn_w_delta", "L0_attn_b_delta", "L0_attn_ro_g", "L0_attn_ro_b",
           "L0_attn_W_ro", "L0_attn_b_ro", "L0_attn_W_gate", "L0_attn_b_gate"]


def kernel(**inputs):
    import concourse.bacc as bacc
    from concourse.bass_utils import run_bass_kernel_spmd

    nc = bacc.Bacc("TRN2", target_bir_lowering=False, num_devices=1)
    arrays, aps = {}, {}
    for name in ["x", *_WEIGHTS, *_OTHERS]:
        a = np.ascontiguousarray(inputs[name])
        if a.ndim == 0:
            a = a.reshape(1)
        arrays[f"in_{name}"] = a
        aps[name] = nc.dram_tensor(f"in_{name}", a.shape, mybir.dt.from_np(a.dtype), kind="ExternalInput").ap()
    out = nc.dram_tensor("out", (B, L, 2 * C), F32, kind="ExternalOutput").ap()
    build(nc, aps["x"], [aps[n] for n in _WEIGHTS], *[aps[n] for n in _OTHERS], out)
    r = run_bass_kernel_spmd(nc, [arrays], core_ids=[0])
    return r.results[0]["out"]
```

```python
from contextlib import ExitStack

import numpy as np
import concourse.bass as bass
from concourse import mybir

F32 = mybir.dt.float32
F16 = mybir.dt.float16
BF16 = mybir.dt.bfloat16
I32 = mybir.dt.int32
ALU = mybir.AluOpType
ACT = mybir.ActivationFunctionType
AX_X = mybir.AxisListType.X

B, L, C = 8, 512, 64
D = C // 8
P = 128
NA = 4
NQ = L // P
NT = NQ * B
H = 256
NH = H // P
STEPS = 16
BODIES = L // STEPS
SB = STEPS * B
HALF = SB // 2
HALF_STEPS = STEPS // 2
AHEAD = 10
SLOT = 64
SHIFT_AT = 32
VW = 194
LEAK, KEEP = 0.95, 1.0 - 0.95
EPS = 1e-5
STATE_UP = 4096.0
WEIGHT_UP = 128.0
SHIFT = 24.0


def build(nc, x, w, alpha, gamma, norm_g, norm_b, w_in, w_res, ssm_a, w_b, w_delta, b_delta,
          ro_g, ro_b, w_ro, b_ro, w_gate, b_gate, out):
    ctx = ExitStack()
    with ctx:
        def sb(name, shape, dt=F32):
            return ctx.enter_context(nc.sbuf_tensor(name, shape, dt))

        def sem(name):
            return ctx.enter_context(nc.semaphore(name))

        ident = sb("ident", [P, P])
        ident16 = sb("ident16", [P, P], BF16)
        ballast = sb("ballast", [P, 512], BF16)
        ones = sb("ones", [P, P])
        wall = sb("wall", [P, 64 + NA * C])
        res_nat = sb("res_nat", [P, NH, H])
        in_nat = sb("in_nat", [P, NH, P])
        b_nat = sb("b_nat", [P, NH, P])
        ro_nat = sb("ro_nat", [P, H])
        ro_g_row = sb("ro_g_row", [P, H])
        ro_b_row = sb("ro_b_row", [P, H])
        ro_tmp = sb("ro_tmp", [P, H])
        gate_nat = sb("gate_nat", [P, P])
        b_gate_row = sb("b_gate_row", [P, P])
        cols = sb("cols", [P, 8])
        a_cols = sb("a_cols", [P, NH])
        neg_inv_a = sb("neg_inv_a", [P, NH])
        mix = sb("mix", [P, NA])
        setup = sb("setup", [P, 16])
        res_hi = sb("res_hi", [P, NH, H], F16)
        res_lo = sb("res_lo", [P, NH, H], F16)
        in_t = sb("in_t", [P, H])
        b_t = sb("b_t", [P, H])
        gate_t = sb("gate_t", [P, P + 1])
        ro_pair = sb("ro_pair", [P, NH, 2 * P])
        ro_row = sb("ro_row", [P, P])

        states = sb("states", [P, BODIES, STEPS * NH * B])
        early = states[:, :, :].rearrange("p i n -> p (i n)")
        x_in = early[:, 0:1024].rearrange("p (i k n) -> p i k n", i=2, k=NQ)
        x_t = early[:, 1024:2048].rearrange("p (i k n) -> p i k n", i=2, k=NQ)
        rest_v = early[:, 2048:3072].rearrange("p (k n) -> p k n", k=NQ)
        rest_qk = early[:, 3072:3328].rearrange("p (h k n) -> p h k n", h=2, k=NQ)
        part = early[:, 3328:3712].bitcast(BF16).rearrange("p (l h k n) -> p l h k n", l=3, h=2, k=NQ)
        k_rows = early[:, 3712:4224].bitcast(BF16).rearrange("p (k n) -> p k n", k=NQ)
        res_abs = early[:, 4224:4224 + NH * H]
        q_rows = sb("q_rows", [P, NQ, B, NA * SLOT], BF16)
        k_cols = sb("k_cols", [P, B, 2, L], BF16)
        values = sb("values", [P, B * NQ, NA * VW], BF16)

        q_cols = sb("q_cols", [P, NA, P], BF16)
        top = sb("top", [P, 2])
        shift = sb("shift", [P, 1])
        shift_rows = sb("shift_rows", [P, P], BF16)
        prob = sb("prob", [P, 2, L])
        prob_hi = sb("prob_hi", [P, 2, L], F16)
        prob_lo = sb("prob_lo", [P, 2, L], F16)
        o_sb = sb("o_sb", [P, NA, VW])
        o_sum = sb("o_sum", [P, NA, C])
        coef = sb("coef", [P, NA])
        h_now = sb("h_now", [P, P])
        stats = sb("stats", [P, 6])
        mean_var = sb("mean_var", [P, 2])
        small = sb("small", [P, 8])
        minus_half = sb("minus_half", [P, 1])
        eps_col = sb("eps_col", [P, 1])
        half_col = sb("half_col", [P, 1])
        x_hat = sb("x_hat", [P, P])
        x_hat_t = sb("x_hat_t", [P, P])
        gate_pre = sb("gate_pre", [P, P])

        h_all = sb("h_all", [P, NT, P])
        gate_all = sb("gate_all", [P, NT, P])
        xn = sb("xn", [P, L * B + HALF])
        z_all = sb("z_all", [P, NT])

        y = sb("y", [P, NH * B])
        s_hi = sb("s_hi", [P, NH * B], F16)
        s_lo = sb("s_lo", [P, NH * B], F16)
        kept = sb("kept", [P, NH * B])
        s_body = sb("s_body", [P, STEPS, NH * B])


        delta = sb("delta", [P, NT])
        sp_tmp = sb("sp_tmp", [P, 2, NT])
        r_mv = sb("r_mv", [P, 2, 2])
        r_st = sb("r_st", [P, 2, 6])
        r_eps = sb("r_eps", [P, 2])
        r_var = sb("r_var", [P, 2])
        r_dev = sb("r_dev", [P, 2, 2])
        ln_st = sb("ln_st", [P, 6])
        ln_mv = sb("ln_mv", [P, 2, 2])
        ln_small = sb("ln_small", [P, 2, 2])
        v32 = values[:, :, :].rearrange("p k n -> p (k n)").bitcast(F32)
        SSM_LEN = NH * (NQ + 1) * B * P
        ssm = v32[:, 0:SSM_LEN].rearrange("p (m q n) -> p m q n", m=NH, q=NQ + 1)
        ssm_b_bar = v32[:, SSM_LEN:SSM_LEN + 2 * P].rearrange("p (s n) -> p s n", s=2)
        assert SSM_LEN + 2 * P <= B * NQ * NA * VW // 2
        k32 = k_cols[:, :, :, :].rearrange("p b a n -> p (b a n)").bitcast(F32)
        r_in = k32[:, 0:4 * NH * P].rearrange("p (e r m n) -> p e r m n", e=2, r=2, m=NH)
        r_pre = k32[:, 1024:1024 + 4 * P].rearrange("p (e r n) -> p e r n", e=2, r=2)
        r_act = k32[:, 1536:1536 + 4 * P].rearrange("p (e r n) -> p e r n", e=2, r=2)
        r_diff = k32[:, 2048:2048 + P]
        r_base = k32[:, 2176:2176 + P]

        PS = ctx.enter_context(nc.psum_tensor("PS", [P, 8, 512], F32))
        PRE = [PS[:, i, 0:SB].rearrange("p (m t b) -> p m t b", m=NH, b=B) for i in range(2)]
        SCORES = [PS[:, 2, :], PS[:, 3, :]]
        SCORES16 = [one.bitcast(BF16) for one in SCORES]
        TURNED = PS[:, 4, :]
        OUT2 = [PS[:, 5, :], PS[:, 6, :]]
        MISC = PS[:, 7, :]
        MISC16 = MISC.bitcast(BF16)

        w_loaded = sem("w_loaded")
        rows_loaded = sem("rows_loaded")
        x_loaded_even = sem("x_loaded_even")
        x_loaded_odd = sem("x_loaded_odd")
        const_ready = sem("const_ready")
        dve_seq = sem("dve_seq")
        zeros_ready = sem("zeros_ready")
        amax_ready = sem("amax_ready")
        wt_turned = sem("wt_turned")
        wt_ready = sem("wt_ready")
        cvec_ready = sem("cvec_ready")
        x_turned = sem("x_turned")
        x_t_ready = sem("x_t_ready")
        projected = sem("projected")
        v_first = sem("v_first")
        qk_first = sem("qk_first")
        v_rest = sem("v_rest")
        qk_rest = sem("qk_rest")
        v_rest2 = sem("v_rest2")
        qk_step = sem("qk_step")
        v_parts = sem("v_parts")
        k_rows_ready = sem("k_rows_ready")
        q_rows_ready = sem("q_rows_ready")
        k_turned = sem("k_turned")
        k_cols_ready = sem("k_cols_ready")
        tiles_done = sem("tiles_done")
        q_turned = sem("q_turned")
        q_ready = sem("q_ready")
        scored = sem("scored")
        top_ready = sem("top_ready")
        shift_raw = sem("shift_raw")
        shift_ready = sem("shift_ready")
        shift_turned = sem("shift_turned")
        shift_placed = sem("shift_placed")
        turned_ready = sem("turned_ready")
        prob_ready = sem("prob_ready")
        prob_lo_ready = sem("prob_lo_ready")
        pv_done = sem("pv_done")
        o_half = sem("o_half")
        o_ready = sem("o_ready")
        inv_ready = sem("inv_ready")
        coef_ready = sem("coef_ready")
        sum_a = sem("sum_a")
        sum_b = sem("sum_b")
        sum_c = sem("sum_c")
        h_ready = sem("h_ready")
        h_kept = sem("h_kept")
        stat_a = sem("stat_a")
        stat_ready = sem("stat_ready")
        norm_step = sem("norm_step")
        norm_ready = sem("norm_ready")
        hat_ready = sem("hat_ready")
        hat_turned = sem("hat_turned")
        hat_copied = sem("hat_copied")
        xn_ready = sem("xn_ready")
        gated = sem("gated")
        gate_raw = sem("gate_raw")
        gate_ready = sem("gate_ready")
        pre_ready = sem("pre_ready")
        acted = sem("acted")
        hi_ready = sem("hi_ready")
        full_ready = sem("full_ready")
        lo_ready = sem("lo_ready")
        kept_ready = sem("kept_ready")
        saved = sem("saved")
        sp_step = sem("sp_step")
        sp_ready = sem("sp_ready")
        k_cols_free = sem("k_cols_free")
        spread = sem("spread")
        decayed = sem("decayed")
        ssm_zeroed = sem("ssm_zeroed")
        ssm_fed = sem("ssm_fed")
        ssm_scaled = sem("ssm_scaled")
        ssm_done = sem("ssm_done")
        states_in = sem("states_in")
        ssm_in = sem("ssm_in")
        read_piece = sem("read_piece")
        r_stat_a = sem("r_stat_a")
        r_stats = sem("r_stats")
        r_var_ready = sem("r_var_ready")
        r_dev_ready = sem("r_dev_ready")
        readout_scaled = sem("readout_scaled")
        r_gelu = sem("r_gelu")
        gate_scaled = sem("gate_scaled")
        r_diff_ready = sem("r_diff_ready")
        r_blend = sem("r_blend")
        r_base_ready = sem("r_base_ready")
        h2_ready = sem("h2_ready")
        ln_stat_a = sem("ln_stat_a")
        ln_stats = sem("ln_stats")
        ln_var_ready = sem("ln_var_ready")
        ln_dev_ready = sem("ln_dev_ready")
        readout_normed = sem("readout_normed")
        stats_waited = sem("stats_waited")
        pool_waited = sem("pool_waited")
        queries_waited = sem("queries_waited")
        r_out = sem("r_out")
        out_done = sem("out_done")
        FREE, TWO_FREE, FOUR_FREE, EIGHT_FREE = 1, 2, 4, 8
        start_free = (gate_raw, gate_ready, h_kept, inv_ready, k_cols_ready, k_rows_ready, k_turned, q_rows_ready, qk_rest, sum_b, r_dev_ready, tiles_done, v_rest, x_t_ready, prob_ready, shift_turned, o_half, o_ready, q_ready, xn_ready)
        start_two_free = (saved, shift_placed, prob_lo_ready, pv_done, readout_scaled, r_gelu, h2_ready)


        x_loaded = [x_loaded_even, x_loaded_odd]

        def tile_q(j):
            if isinstance(j, int):
                return j // B
            return nc.s_assert_within(j >> 3, 0, NQ - 1, skip_runtime_bounds_check_because="j is below NT = 8 * NQ")

        def place(z):
            return z * D if z < SHIFT_AT // D else (z + 1) * D

        def tiles_at(work, p, newest):
            for lag in (2, 1, 0):
                j = newest - lag
                if not isinstance(j, int) or 0 <= j < NT:
                    work(p + STEPS * lag, j)

        def half_q(c):
            if isinstance(c, int):
                return c // 2
            return nc.s_assert_within(c >> 1, 0, NQ - 1, skip_runtime_bounds_check_because="c is below 2 * NQ")

        FIRST_DECAY = NT - AHEAD + 2
        FIRST_READ = FIRST_DECAY + 2
        LAGS = 5
        IN_SCAN = (BODIES - FIRST_READ) * 4
        assert IN_SCAN * P // B <= FIRST_DECAY * STEPS and BODIES - FIRST_READ + 2 == 2 * NQ

        def body_readouts(readout, t, i):
            n = (i - FIRST_READ) * 4 + t // 4
            active = range(LAGS) if not isinstance(i, int) else range(min(LAGS, n + 1))
            readout(t % 4, n, (t // 4) % 2, active, (i - FIRST_READ) * 4 * NH + 4 * NH, FIRST_DECAY)

        def rest_of_readouts(engine, readout):
            with engine.Fori(IN_SCAN // 2, NT // 2) as two:
                for e in range(2):
                    for u in range(4):
                        readout(u, two * 2 + e, e, range(LAGS), NT * NH, BODIES)
            for n in range(NT, NT + LAGS - 1):
                for u in range(4):
                    readout(u, n, n % 2, range(n - NT + 1, LAGS), NT * NH, BODIES)

        def tile_b(j):
            return j % B

        block = ctx.enter_context(nc.Block())

        def places():
            for a, (q, k, v) in enumerate(((0, 0, 0), (0, 1, 1), (1, 1, 1), (1, 0, 0))):
                for n, (signal, at, width) in enumerate(((q, a * D, D), (k, 32 + a * D, D), (v, 64 + a * C, C))):
                    yield 3 * a + n, signal, at, width

        LOADS, ROW_LOADS = 12 + 5 + NH, 12
        x_v = x.rearrange("b (k p) c s -> p b k (c s)", p=P)

        @block.sync
        def _(sp):
            for i in range(2):
                sp.dma_start(x_in[:, i, :, :], x_v[:, i, :, :]).then_inc(x_loaded[i], 16)
            sp.wait_ge(zeros_ready, 1)
            for n, signal, at, width in places():
                sp.dma_start(wall[signal::2, at:at + width], w[n]).then_inc(w_loaded, 16)
            sp.dma_start(res_nat[:, :, :], w_res.rearrange("(m p) k -> p m k", p=P)).then_inc(w_loaded, 16)
            sp.dma_start(in_nat[:, :, :], w_in.rearrange("(m p) k -> p m k", p=P)).then_inc(w_loaded, 16)
            sp.dma_start(b_nat[:, :, :], w_b.rearrange("(m p) k -> p m k", p=P)).then_inc(w_loaded, 16)
            sp.dma_start(ro_nat[:, :], w_ro).then_inc(w_loaded, 16)
            sp.dma_start(gate_nat[:, :], w_gate).then_inc(w_loaded, 16)
            for m in range(NH):
                sp.dma_start(a_cols[:, m:m + 1], ssm_a[m * P:m * P + P].rearrange("(p a) -> p a", a=1)).then_inc(w_loaded, 16)
            with sp.Fori(1, B // 2) as it:
                for i in range(2):
                    sp.wait_ge(x_turned, it * 2 + i - 1)
                    sp.dma_start(x_in[:, i, :, :], x_v[:, bass.ds(it * 2 + i, 1), :, :]).then_inc(x_loaded[i], 16)
            out_v = out.rearrange("b (q p) c -> p q b c", p=P)
            with sp.Fori(0, NT) as j:
                sp.wait_ge(r_out, j + 1)
                sp.dma_start(out_v[:, bass.ds(tile_q(j), 1), bass.ds(j % B, 1), :], gate_all[:, bass.ds(j, 1), :]
                             ).then_inc(out_done, 16)
            sp.wait_ge(out_done, 16 * NT)

        @block.gpsimd
        def _(pool):
            g = nc.gpsimd
            for one in start_free:
                pool.sem_inc(one, FREE)
            for two in start_two_free:
                pool.sem_inc(two, TWO_FREE)
            pool.sem_inc(turned_ready, FOUR_FREE)
            for eight in (read_piece, ssm_done):
                pool.sem_inc(eight, EIGHT_FREE)
            g.memset(wall[:, :], 0.0)
            stacks = k_rows[:, :, :].rearrange("p k (a n) -> p (k a) n", n=SLOT)
            g.memset(stacks[:, :, SHIFT_AT:SHIFT_AT + 2], -1.0)
            g.memset(stacks[:, :, SHIFT_AT + 2:SHIFT_AT + D], 0.0)
            g.memset(stacks[:, :, 7 * D:], 0.0)
            g.memset(shift_rows[:, :], 0.0)
            g.memset(q_cols[:, :, :], 0.0)
            g.memset(minus_half[:, :], -0.5)
            g.memset(eps_col[:, :], EPS)
            g.memset(half_col[:, :], 0.5)
            g.memset(ones[:, :], 1.0)
            g.memset(ballast[:, :], 0.0)
            g.memset(ident[:, :], 0.0).then_inc(zeros_ready, 1)
            pool.wait_ge(zeros_ready, 1)
            g.affine_select(out=ident[:, :], in_=ident[:, :], compare_op=ALU.not_equal, fill=1.0, base=0,
                            pattern=[[-1, P]], channel_multiplier=1).then_inc(const_ready, 1)
            pool.wait_ge(const_ready, 1)
            g.tensor_copy(ident16[:, :], ident[:, :]).then_inc(const_ready, 1)
            flat = values[:, :, :].rearrange("p k (a w) -> p (k a) w", w=VW)
            g.memset(flat[:, :, 2 * C:2 * C + 2], 1.0).then_inc(const_ready, 1)
            g.memset(xn[:, L * B:], 0.0)
            g.memset(r_eps[:, 0:1], EPS * STATE_UP ** 2)
            g.memset(r_eps[:, 1:2], EPS)
            pool.wait_ge(dve_seq, 3)
            g.partition_all_reduce(setup[:, 3:4], setup[:, 2:3], P, bass.bass_isa.ReduceOp.max).then_inc(amax_ready, 1)

            with pool.Fori(0, B // 2) as it:
                for i in range(2):
                    b = it * 2 + i
                    pool.wait_ge(v_parts, b + 1)
                    v3 = values[:, bass.ds(b * NQ, NQ), :].rearrange("p k (a w) -> p (k a) w", w=VW)
                    g.tensor_copy(v3[:, :, 130:130 + C], rest_v[:, :, :].rearrange("p k (a c) -> p (k a) c", c=C)
                                  ).then_inc(tiles_done, 1)

            def work(p, j):
                if p in (14, 18, 22, 26):
                    a = (p - 14) // 4
                    pool.wait_ge(prob_ready, j * NA + (a + 1) + FREE)
                    pool.wait_ge(pv_done, j * NA + (a - 1) + TWO_FREE)
                    g.tensor_tensor(prob_lo[:, a % 2, :], prob[:, a % 2, :], prob_hi[:, a % 2, :], ALU.subtract
                                    ).then_inc(prob_lo_ready, 1)
                if p == 32:
                    pool.wait_ge(o_ready, j + 1 + FREE)
                    g.tensor_tensor(o_sum[:, :, :], o_sb[:, :, C:2 * C], o_sb[:, :, 130:130 + C], ALU.add).then_inc(sum_a, 1)
                    pool.wait_ge(sum_a, j + 1)
                    g.tensor_tensor(o_sum[:, :, :], o_sum[:, :, :], o_sb[:, :, 0:C], ALU.add).then_inc(sum_b, 1)
                if p == 33:
                    pool.wait_ge(sum_b, j + 1 + FREE)
                    pool.wait_ge(coef_ready, j + 1)
                    g.tensor_tensor(o_sum[:, :, :], o_sum[:, :, :], coef[:, :].unsqueeze(2).to_broadcast([P, NA, C]), ALU.mult
                                    ).then_inc(sum_c, 1)
                    pool.wait_ge(sum_c, j + 1)
                    pool.wait_ge(h_kept, j + FREE)
                    o4 = o_sum[:, :, :].rearrange("p (g k) c -> p g k c", k=2)
                    g.tensor_tensor(h_now[:, :].rearrange("p (g c) -> p g c", c=C), o4[:, :, 0, :], o4[:, :, 1, :], ALU.add
                                    ).then_inc(h_ready, 1)
                if p == 37:
                    pool.wait_ge(stat_ready, j + 1)
                    n0 = j * 6

                    def step(i, n):
                        i.then_inc(norm_step, 1)
                        pool.wait_ge(norm_step, n0 + n)
                    step(g.tensor_tensor(small[:, 0:1], mean_var[:, 1:2], eps_col[:, :], ALU.add), 1)
                    step(g.tensor_tensor(small[:, 1:2], small[:, 0:1], minus_half[:, :], ALU.pow), 2)
                    step(g.tensor_tensor(small[:, 2:3], small[:, 1:2], small[:, 1:2], ALU.mult), 3)
                    step(g.tensor_tensor(small[:, 2:3], small[:, 2:3], mean_var[:, 1:2], ALU.mult), 4)
                    step(g.tensor_tensor(small[:, 3:4], small[:, 2:3], eps_col[:, :], ALU.add), 5)
                    step(g.tensor_tensor(small[:, 4:5], small[:, 3:4], minus_half[:, :], ALU.pow), 6)
                    pool.wait_ge(gate_raw, j + FREE)
                    g.tensor_tensor(small[:, 5:6], small[:, 3:4], small[:, 4:5], ALU.mult)
                    g.tensor_tensor(small[:, 6:7], small[:, 1:2], small[:, 4:5], ALU.mult).then_inc(norm_ready, 1)



            pool.wait_ge(wt_ready, 1)
            for j in range(2):
                for p in range(STEPS):
                    tiles_at(work, p, j)
            with pool.Fori(2, AHEAD) as j:
                for p in range(STEPS):
                    tiles_at(work, p, j)
            with pool.Fori(0, NT - AHEAD) as i:
                for p in range(STEPS):
                    tiles_at(work, p, i + AHEAD)
            for i in range(NT - AHEAD, FIRST_DECAY):
                for p in range(STEPS):
                    tiles_at(work, p, i + AHEAD)

            def readout(u, n, e, active, fed, kept_bodies):
                if 4 in active and u == 0:
                    j = n - 4
                    pool.wait_ge(readout_normed, j + 1)
                    pool.sem_inc(pool_waited, 1)
                    res = gate_all[:, bass.ds(j, 1), :].rearrange("p o n -> p (o n)")
                    g.tensor_tensor(res, res, h_all[:, bass.ds(j, 1), :].rearrange("p o n -> p (o n)"), ALU.add
                                    ).then_inc(r_out, 1)
                if 2 in active and u == 1:
                    j = n - 2
                    now = h_all[:, bass.ds(j, 1), :].rearrange("p o n -> p (o n)")
                    pool.wait_ge(r_gelu, j + 1 + TWO_FREE)
                    g.tensor_tensor(r_diff, r_act[:, e, 0, :], r_act[:, e, 1, :], ALU.subtract).then_inc(r_diff_ready, 1)
                    g.tensor_tensor(r_base, r_act[:, e, 1, :], now, ALU.add).then_inc(r_base_ready, 1)
                if 3 in active and u == 2:
                    j = n - 3
                    s = 1 - e
                    pool.wait_ge(ln_stats, j + 1)
                    g.tensor_tensor(ln_small[:, s, 0:1], ln_mv[:, s, 1:2], eps_col[:, :], ALU.add).then_inc(ln_var_ready, 1)
                    pool.wait_ge(ln_var_ready, j + 1)
                    g.tensor_tensor(ln_small[:, s, 1:2], ln_small[:, s, 0:1], minus_half[:, :], ALU.pow
                                    ).then_inc(ln_dev_ready, 1)
                if 2 in active and u == 2:
                    j = n - 2
                    pool.wait_ge(r_diff_ready, j + 1)
                    pool.wait_ge(gate_scaled, j + 1)
                    pool.sem_inc(pool_waited, 1)
                    g.tensor_tensor(r_diff, r_diff, gate_all[:, bass.ds(j, 1), :].rearrange("p o n -> p (o n)"), ALU.mult
                                    ).then_inc(r_blend, 1)
                    now = h_all[:, bass.ds(j, 1), :].rearrange("p o n -> p (o n)")
                    pool.wait_ge(r_blend, j + 1)
                    pool.wait_ge(r_base_ready, j + 1)
                    pool.sem_inc(pool_waited, 1)
                    g.tensor_tensor(now, r_base, r_diff, ALU.add).then_inc(h2_ready, 1)
                if 1 in active and u == 2:
                    j = n - 1
                    pool.wait_ge(r_stats, j + 1)
                    g.tensor_tensor(r_var[:, :], r_mv[:, :, 1:2].rearrange("p r o -> p (r o)"), r_eps[:, :], ALU.add
                                    ).then_inc(r_var_ready, 1)
                    pool.wait_ge(r_var_ready, j + 1)
                    pool.wait_ge(readout_scaled, j - 1 + TWO_FREE)
                    g.tensor_tensor(r_dev[:, 1 - e, :], r_var[:, :], minus_half[:, :].to_broadcast([P, 2]), ALU.pow
                                    ).then_inc(r_dev_ready, 1)


            pool.wait_ge(h_kept, NT + FREE)
            pool.wait_ge(k_cols_free, 1)
            for t in range(STEPS):
                body_readouts(readout, t, FIRST_READ)
            with pool.Fori(FIRST_READ + 1, BODIES) as i:
                for t in range(STEPS):
                    body_readouts(readout, t, i)
            rest_of_readouts(pool, readout)

        @block.scalar
        def _(act):
            a_ = nc.scalar
            for n, v in enumerate((norm_g, norm_b, w_delta, b_ro)):
                act.dma_start(cols[:, n:n + 1], v.rearrange("(p a) -> p a", a=1)).then_inc(rows_loaded, 16)
            for n, v in enumerate((b_delta, alpha, gamma)):
                act.dma_start(cols[:, 4 + n:5 + n], v.rearrange("(a n) -> a n", a=1).to_broadcast([P, 1])
                               ).then_inc(rows_loaded, 16)
            act.dma_start(mix[:, 0:1], alpha.rearrange("(a n) -> a n", a=1).to_broadcast([P, 1])).then_inc(rows_loaded, 16)
            act.dma_start(mix[:, 2:3], gamma.rearrange("(a n) -> a n", a=1).to_broadcast([P, 1])).then_inc(rows_loaded, 16)
            act.dma_start(ro_g_row[:, :], ro_g.rearrange("(a n) -> a n", a=1).to_broadcast([P, H])).then_inc(rows_loaded, 16)
            act.dma_start(ro_b_row[:, :], ro_b.rearrange("(a n) -> a n", a=1).to_broadcast([P, H])).then_inc(rows_loaded, 16)
            act.dma_start(b_gate_row[:, :], b_gate.rearrange("(a n) -> a n", a=1).to_broadcast([P, P])).then_inc(rows_loaded, 16)
            act.preload_act_table(ACT.Exp)
            with act.Fori(0, B // 2) as it:
                for i in range(2):
                    b = it * 2 + i
                    act.wait_ge(x_turned, b + 1)
                    a_.copy(x_t[:, i, :, :].rearrange("p k n -> p (k n)"), MISC).then_inc(x_t_ready, 1)
                    act.wait_ge(projected, b + 1)
                    act.wait_ge(const_ready, 3)
                    for k in range(NQ):
                        v1 = values[:, bass.ds(b * NQ + k, 1), :].rearrange("p o (a w) -> p (o a) w", w=VW)
                        last = a_.copy(v1[:, :, 0:C], PS[:, 2 + k, 64:64 + NA * C].rearrange("p (a c) -> p a c", c=C))
                    last.then_inc(v_first, 1)
                    act.wait_ge(k_rows_ready, b + FREE)
                    act.wait_ge(q_rows_ready, b + FREE)
                    a_.copy(part[:, 0, :, :, :].rearrange("p h k n -> p k h n"),
                            PS[:, 2:6, 0:64].rearrange("p k (h n) -> p k h n", h=2)).then_inc(qk_first, 1)
                    act.wait_ge(k_turned, b + 1 + FREE)
                    a_.copy(k_cols[:, bass.ds(b, 1), :, :].rearrange("p o a n -> p (o a n)"), OUT2[1].bitcast(BF16)
                            ).then_inc(k_cols_ready, 1)

            def work(p, j):
                if p in (4, 8, 12, 16):
                    a = (p - 4) // 4
                    act.wait_ge(q_turned, j * NA + (a + 1))
                    act.wait_ge(turned_ready, j * NA + (a - 3) + FOUR_FREE)
                    rows = slice(0, 64) if a % 2 == 0 else slice(64, P)
                    a_.copy(q_cols[rows, a, :], MISC16[rows, 0:P]).then_inc(q_ready, 1)
                if p in (9, 13, 17, 21):
                    a = (p - 9) // 4
                    at = (a % 2) * SLOT + SHIFT_AT
                    act.wait_ge(shift_turned, j * NA + (a + 1) + FREE)
                    a_.copy(q_cols[at:at + 2, a, :], SCORES16[a % 2][at:at + 2, 0:P]).then_inc(shift_placed, 1)
                if p in (13, 17, 21, 25):
                    a = (p - 13) // 4
                    act.wait_ge(turned_ready, j * NA + (a + 1) + FOUR_FREE)
                    act.wait_ge(prob_lo_ready, j * NA + (a - 1) + TWO_FREE)
                    a_.activation(prob[:, a % 2, :], TURNED, ACT.Exp, scale=float(D) ** -0.5)
                if p in (14, 18, 22, 26):
                    a = (p - 14) // 4
                    act.wait_ge(pv_done, j * NA + (a - 1) + TWO_FREE)
                    a_.activation(prob_hi[:, a % 2, :], TURNED, ACT.Exp, scale=float(D) ** -0.5).then_inc(prob_ready, 1)
                if p in (23, 31):
                    n = (p - 23) // 8
                    act.wait_ge(pv_done, j * NA + 2 * n + 2 + TWO_FREE)
                    if n == 0:
                        act.wait_ge(sum_b, j + FREE)
                        act.wait_ge(inv_ready, j + FREE)
                    a_.copy(o_sb[:, 2 * n:2 * n + 2, :], OUT2[n].rearrange("p (a w) -> p a w", a=2)[:, :, 0:VW]
                            ).then_inc(o_ready if n else o_half, 1)
                if p == 36:
                    act.wait_ge(h_ready, j + 1)
                    a_.copy(h_all[:, bass.ds(j, 1), :].rearrange("p o n -> p (o n)"), h_now[:, :]).then_inc(h_kept, 1)
                if p == 47:
                    act.wait_ge(gate_raw, j + 1 + FREE)
                    a_.activation(gate_all[:, bass.ds(j, 1), :].rearrange("p o n -> p (o n)"), gate_pre[:, :], ACT.Tanh,
                                  scale=0.5).then_inc(gate_ready, 1)

            def scan(t, i):
                act.wait_ge(pre_ready, i * STEPS + (t + 1))
                a_.activation(y[:, :].rearrange("p (m b) -> p m b", m=NH), PRE[t // 8][:, :, t % 8, :], ACT.Tanh,
                              scale=back).then_inc(acted, 1)

            def save(half, i):
                act.wait_ge(full_ready, i * STEPS + (half + 1) * HALF_STEPS)
                n = HALF_STEPS * NH * B
                a_.copy(states[:, bass.ds(i, 1), half * n:half * n + n].rearrange("p o n -> p (o n)"),
                        s_body[:, half * HALF_STEPS:(half + 1) * HALF_STEPS, :].rearrange("p t n -> p (t n)")
                        ).then_inc(saved, 1)

            act.wait_ge(wt_ready, 1)
            back = act.alloc_register("back")
            act.reg_load(back, setup[0:1, 7:8].bitcast(I32))

            for j in range(2):
                for p in range(STEPS):
                    tiles_at(work, p, j)
            with act.Fori(2, AHEAD) as j:
                for p in range(STEPS):
                    tiles_at(work, p, j)
            with act.Fori(0, NT - AHEAD) as i:
                for t in range(STEPS):
                    scan(t, i)
                    tiles_at(work, t, i + AHEAD)
                    if t % HALF_STEPS == 7:
                        save(t // HALF_STEPS, i)
            for i in range(NT - AHEAD, FIRST_DECAY):
                for t in range(STEPS):
                    scan(t, i)
                    tiles_at(work, t, i + AHEAD)
                    if t % HALF_STEPS == 7:
                        save(t // HALF_STEPS, i)

            def decay(n):
                c, m = n // 2, n % 2
                act.wait_ge(spread, 4 * c + 4)
                a_.activation(ssm[:, m, 1 + c // 2, (c % 2) * 4 * P:(c % 2) * 4 * P + 4 * P], PS[:, 4 + c % 2, :], ACT.Exp,
                              scale=a_cols[:, m:m + 1]).then_inc(decayed, 1)

            def readout(u, n, e, active, fed, kept_bodies):
                if 0 in active and u == 0:
                    act.wait_ge(read_piece, n * 4 - 4 + EIGHT_FREE)
                    act.wait_ge(saved, 2 * kept_bodies + TWO_FREE)
                    src = states[:, bass.ds(tile_q(n) * B, B), :].rearrange("p i (t m b) -> p m (i t) b", m=NH, b=B)
                    a_.copy(r_in[:, e, 0, :, :], src[:, :, :, bass.ds(n % B, 1)].rearrange("p m t o -> p m (t o)")
                            ).then_inc(states_in, 1)
                if 2 in active and u == 0:
                    j = n - 2
                    act.wait_ge(readout_scaled, j + 1 + TWO_FREE)
                    act.wait_ge(h2_ready, j - 1 + TWO_FREE)
                    a_.activation(r_act[:, e, :, :], r_pre[:, e, :, :], ACT.Gelu).then_inc(r_gelu, 1)
                if 0 in active and u == 1:
                    act.wait_ge(ssm_done, fed + EIGHT_FREE)
                    a_.copy(r_in[:, e, 1, :, :], ssm[:, :, bass.ds(tile_q(n) + 1, 1), bass.ds((n % B) * P, P)
                                                     ].rearrange("p m o n -> p m (o n)")).then_inc(ssm_in, 1)
                if 1 in active and u == 2:
                    gate = gate_all[:, bass.ds(n - 1, 1), :].rearrange("p o n -> p (o n)")
                    a_.activation(gate, gate, ACT.Identity, scale=0.5, bias=half_col[:, :]).then_inc(gate_scaled, 1)

            act.wait_ge(sp_step, 2)
            a_.activation(sp_tmp[:, 0, :], sp_tmp[:, 0, :], ACT.Exp, scale=-1.0).then_inc(sp_ready, 1)
            act.preload_act_table_set("natural_log_exp_and_others")
            act.wait_ge(sp_ready, 1)
            a_.activation(sp_tmp[:, 0, :], sp_tmp[:, 0, :], ACT.Ln, bias=1.0).then_inc(sp_ready, 1)
            act.preload_act_table(ACT.Exp)
            act.wait_ge(pv_done, NA * NT + TWO_FREE)
            for t in range(STEPS):
                scan(t, FIRST_DECAY)
                if t >= 6:
                    decay(t - 6)
                if t % HALF_STEPS == 7:
                    save(t // HALF_STEPS, FIRST_DECAY)
            for t in range(STEPS):
                scan(t, FIRST_DECAY + 1)
                if t < 6:
                    decay(t + 10)
                if t % HALF_STEPS == 7:
                    save(t // HALF_STEPS, FIRST_DECAY + 1)
            act.preload_act_table(ACT.Gelu)
            act.wait_ge(k_cols_free, 1)
            for t in range(STEPS):
                scan(t, FIRST_READ)
                body_readouts(readout, t, FIRST_READ)
                if t % HALF_STEPS == 7:
                    save(t // HALF_STEPS, FIRST_READ)
            with act.Fori(FIRST_READ + 1, BODIES) as i:
                for t in range(STEPS):
                    scan(t, i)
                    body_readouts(readout, t, i)
                    if t % HALF_STEPS == 7:
                        save(t // HALF_STEPS, i)
            rest_of_readouts(act, readout)

        @block.vector
        def _(dve):
            v = nc.vector
            dve.wait_ge(w_loaded, 16 * LOADS)
            dve.wait_ge(rows_loaded, 16 * ROW_LOADS)
            dve.wait_ge(const_ready, 1)
            n = [0]

            def seq(i):
                n[0] += 1
                i.then_inc(dve_seq, 1)
                dve.wait_ge(dve_seq, n[0])
            seq(v.tensor_scalar(res_abs, res_nat[:, :, :].rearrange("p m k -> p (m k)"), -1.0, None, ALU.mult))
            seq(v.tensor_tensor(res_abs, res_abs,
                                res_nat[:, :, :].rearrange("p m k -> p (m k)"), ALU.max))
            seq(v.reduce_max(setup[:, 2:3], res_abs, AX_X))
            dve.wait_ge(amax_ready, 1)
            seq(v.tensor_scalar(setup[:, 4:5], setup[:, 3:4], 2.0 ** -100, None, ALU.max))
            seq(v.tensor_scalar(setup[:, 4:5].bitcast(I32), setup[:, 4:5].bitcast(I32), 0x7F800000, None, ALU.bitwise_and))
            seq(v.reciprocal(setup[:, 5:6], setup[:, 4:5]))
            v.tensor_scalar(setup[:, 6:7], setup[:, 5:6], WEIGHT_UP, None, ALU.mult)
            v.tensor_scalar(setup[:, 7:8], setup[:, 4:5], 1.0 / (WEIGHT_UP * STATE_UP), None, ALU.mult)
            seq(v.tensor_scalar(setup[:, 8:9], setup[:, 5:6], WEIGHT_UP * STATE_UP, None, ALU.mult))
            seq(v.tensor_scalar(neg_inv_a[:, :], a_cols[:, :], 1e-8, None, ALU.add))
            seq(v.reciprocal(neg_inv_a[:, :], neg_inv_a[:, :]))
            seq(v.tensor_scalar(neg_inv_a[:, :], neg_inv_a[:, :], -1.0, None, ALU.mult))
            for m in range(NH):
                v.tensor_scalar(b_nat[:, m, :], b_nat[:, m, :], neg_inv_a[:, m:m + 1], None, ALU.mult)
            v.tensor_tensor(ro_tmp[:, :], ro_nat[:, :], ro_b_row[:, :], ALU.mult)
            seq(v.tensor_tensor(ro_nat[:, :], ro_nat[:, :], ro_g_row[:, :], ALU.mult))
            v.reduce_sum(setup[:, 9:10], ro_nat[:, :], AX_X)
            seq(v.reduce_sum(setup[:, 10:11], ro_tmp[:, :], AX_X))
            seq(v.tensor_scalar(setup[:, 9:10], setup[:, 9:10], 1.0 / H, None, ALU.mult))
            v.tensor_scalar(ro_nat[:, :], ro_nat[:, :], setup[:, 9:10], None, ALU.subtract)
            seq(v.tensor_tensor(setup[:, 10:11], setup[:, 10:11], cols[:, 3:4], ALU.add))
            v.tensor_scalar(ro_tmp[:, 0:P], ident[:, :], setup[:, 10:11], None, ALU.mult)
            v.tensor_tensor(setup[:, 11:12], cols[:, 1:2], cols[:, 2:3], ALU.mult)
            v.tensor_tensor(gate_t[:, P:P + 1], cols[:, 0:1], cols[:, 2:3], ALU.mult)
            q_stacks = q_rows[:, :, :, :].rearrange("p k b (a n) -> p (k b a) n", n=SLOT)
            v.memset(q_stacks[:, :, SHIFT_AT:SHIFT_AT + D], 0.0)
            v.memset(q_stacks[:, :, 7 * D:], 0.0)
            v.memset(mix[:, 1:2], 1.0)
            v.memset(mix[:, 3:4], 1.0)
            v.memset(kept[:, :], 0.0).then_inc(kept_ready, 1)
            v.memset(s_hi[:, :], 0.0).then_inc(hi_ready, 1)
            v.memset(s_lo[:, :], 0.0).then_inc(lo_ready, 1)
            v.memset(z_all[:, :], 0.0).then_inc(cvec_ready, 1)
            dve.wait_ge(wt_turned, 1)
            seq(v.tensor_scalar(res_hi[:, :, :].rearrange("p k m -> p (k m)"), PS[:, 2, :], setup[:, 6:7], None, ALU.mult))
            v.scalar_tensor_tensor(res_lo[:, :, :].rearrange("p k m -> p (k m)"), PS[:, 2, :], setup[:, 6:7],
                                   res_hi[:, :, :].rearrange("p k m -> p (k m)"), ALU.mult, ALU.subtract)
            v.tensor_scalar(in_t[:, :], PS[:, 3, 0:H], setup[:, 8:9], None, ALU.mult)
            v.tensor_copy(b_t[:, :], PS[:, 3, H:2 * H])
            v.tensor_copy(gate_t[:, 0:P], PS[:, 4, 0:P])
            for m in range(NH):
                v.tensor_copy(ro_pair[:, m, 0:P], ident[:, :])
                v.tensor_copy(ro_pair[:, m, P:2 * P], PS[:, 4, P + m * P:2 * P + m * P])
            v.tensor_copy(ro_row[:, :], PS[:, 5, 0:P])
            v.tensor_tensor(setup[:, 12:13], PS[:, 5, P:P + 1], cols[:, 4:5], ALU.add).then_inc(wt_ready, 1)

            with dve.Fori(0, B // 2) as it:
                for i in range(2):
                    b = it * 2 + i
                    vals = values[:, bass.ds(b * NQ, NQ), :].rearrange("p k (a w) -> p (k a) w", w=VW)
                    rest = rest_v[:, :, :].rearrange("p k (a c) -> p (k a) c", c=C)
                    dve.wait_ge(qk_first, b + 1)
                    dve.wait_ge(tiles_done, b + FREE)
                    for k in range(NQ):
                        one = values[:, bass.ds(b * NQ + k, 1), :].rearrange("p o (a w) -> p (o a) w", w=VW)
                        last = v.tensor_tensor(rest_v[:, k, :].rearrange("p (a c) -> p a c", c=C),
                                               PS[:, 2 + k, 64:64 + NA * C].rearrange("p (a c) -> p a c", c=C),
                                               one[:, :, 0:C], ALU.subtract)
                    last.then_inc(v_rest, 1)
                    v.tensor_tensor(rest_qk[:, :, :, :].rearrange("p h k n -> p k h n"),
                                    PS[:, 2:6, 0:64].rearrange("p k (h n) -> p k h n", h=2),
                                    part[:, 0, :, :, :].rearrange("p h k n -> p k h n"), ALU.subtract).then_inc(qk_rest, 1)
                    dve.wait_ge(v_rest, b + 1 + FREE)
                    v.tensor_copy(vals[:, :, C:2 * C], rest).then_inc(v_rest2, 1)
                    dve.wait_ge(qk_rest, b + 1 + FREE)
                    r = rest_qk[:, :, :, :].rearrange("p h k n -> p (h k n)")
                    p2 = part[:, 1, :, :, :].rearrange("p h k n -> p (h k n)")
                    v.tensor_copy(p2, r).then_inc(qk_step, 1)
                    dve.wait_ge(v_rest2, b + 1)
                    v.tensor_tensor(rest, rest, vals[:, :, C:2 * C], ALU.subtract).then_inc(v_parts, 1)
                    dve.wait_ge(qk_step, b * 2 + 1)
                    v.tensor_tensor(part[:, 2, :, :, :].rearrange("p h k n -> p (h k n)"), r, p2, ALU.subtract
                                    ).then_inc(qk_step, 1)
                    dve.wait_ge(qk_step, b * 2 + 2)
                    dve.wait_ge(k_turned, b + FREE)
                    kr = k_rows[:, :, :].rearrange("p k (a n) -> p (k a) n", n=SLOT)
                    qr = q_rows[:, :, bass.ds(b, 1), :].rearrange("p k o (a n) -> p k (o a) n", n=SLOT)
                    pk = part[:, :, 1, :, :].rearrange("p l k (a d) -> p l (k a) d", d=D)
                    pq = part[:, :, 0, :, :].rearrange("p l k (a d) -> p l k a d", d=D)
                    for l, slots in enumerate(((0, 1, 2), (3, 4), (5,))):
                        for z in slots:
                            last = v.tensor_copy(kr[:, :, place(z):place(z) + D], pk[:, l, :, :])
                    last.then_inc(k_rows_ready, 1)
                    for l, slots in enumerate(((0, 3, 5), (1, 4), (2,))):
                        for z in slots:
                            last = v.tensor_copy(qr[:, :, :, place(z):place(z) + D], pq[:, l, :, :, :])
                    last.then_inc(q_rows_ready, 1)

            def work(p, j):
                if p in (6, 10, 14, 18):
                    a = (p - 6) // 4
                    dve.wait_ge(scored, j * NA + (a + 1))
                    v.reduce_max(top[:, a % 2:a % 2 + 1], SCORES[a % 2], AX_X).then_inc(top_ready, 1)
                if p in (7, 11, 15, 19):
                    a = (p - 7) // 4
                    at = (a % 2) * SLOT + SHIFT_AT
                    dve.wait_ge(top_ready, j * NA + (a + 1))
                    dve.wait_ge(shift_turned, j * NA + a + FREE)
                    v.tensor_scalar(shift_rows[:, at:at + 1], top[:, a % 2:a % 2 + 1], SHIFT, None, ALU.subtract)
                    v.tensor_scalar(shift[:, :], top[:, a % 2:a % 2 + 1], SHIFT, None, ALU.subtract).then_inc(shift_raw, 1)
                    dve.wait_ge(shift_raw, j * NA + (a + 1))
                    v.tensor_tensor(shift_rows[:, at + 1:at + 2], shift[:, :], shift_rows[:, at:at + 1], ALU.subtract
                                    ).then_inc(shift_ready, 1)
                if p == 32:
                    dve.wait_ge(o_ready, j + 1 + FREE)
                    v.reciprocal(coef[:, :], o_sb[:, :, 2 * C:2 * C + 1].rearrange("p a o -> p (a o)")).then_inc(inv_ready, 1)
                    dve.wait_ge(inv_ready, j + 1 + FREE)
                    v.tensor_tensor(coef[:, :], coef[:, :], mix[:, :], ALU.mult).then_inc(coef_ready, 1)
                if p == 36:
                    dve.wait_ge(h_ready, j + 1)
                    v.bn_stats(stats[:, :], h_now[:, :]).then_inc(stat_a, 1)
                    dve.wait_ge(stat_a, j + 1)
                    dve.sem_inc(stats_waited, 1)
                    v.bn_aggr(mean_var[:, :], stats[:, :]).then_inc(stat_ready, 1)
                if p == 40:
                    dve.wait_ge(norm_ready, j + 1)
                    v.tensor_scalar(x_hat[:, :], h_now[:, :], mean_var[:, 0:1], small[:, 6:7], ALU.subtract, ALU.mult
                                    ).then_inc(hat_ready, 1)
                if p == 41:
                    dve.wait_ge(hat_turned, j + 1)
                    v.tensor_copy(x_hat_t[:, :], MISC[:, 0:P]).then_inc(hat_copied, 1)
                    dst = xn[:, 0:L * B].rearrange("p (q t b) -> p q t b", q=NQ, b=B)
                    v.tensor_scalar(dst[:, bass.ds(tile_q(j), 1), :, bass.ds(j % B, 1)].rearrange("p q t o -> p (q t o)"),
                                    MISC[:, 0:P], cols[:, 0:1], cols[:, 1:2], ALU.mult, ALU.add).then_inc(xn_ready, 1)
                if p == 45:
                    dve.wait_ge(gated, j + 1)
                    dve.wait_ge(gate_ready, j + FREE)
                    v.tensor_scalar(z_all[:, bass.ds(j, 1)], MISC[:, P:P + 1], setup[:, 12:13], None, ALU.add)
                    v.scalar_tensor_tensor(gate_pre[:, :], MISC[:, 0:P], small[:, 5:6], b_gate_row[:, :], ALU.mult, ALU.add
                                           ).then_inc(gate_raw, 1)

            def scan(t, i):
                n = i * STEPS + (t + 1)
                dve.wait_ge(acted, n)
                dve.wait_ge(kept_ready, n)
                v.scalar_tensor_tensor(s_hi[:, :], y[:, :], LEAK * STATE_UP, kept[:, :], ALU.mult, ALU.add).then_inc(hi_ready, 1)
                full = s_body[:, t, :]
                if t % HALF_STEPS == 0:
                    dve.wait_ge(saved, 2 * i - 1 + t // HALF_STEPS + TWO_FREE)
                v.scalar_tensor_tensor(full, y[:, :], LEAK * STATE_UP, kept[:, :], ALU.mult, ALU.add).then_inc(full_ready, 1)
                dve.wait_ge(full_ready, n)
                v.tensor_tensor(s_lo[:, :], full, s_hi[:, :], ALU.subtract).then_inc(lo_ready, 1)
                v.tensor_scalar(kept[:, :], full, KEEP, None, ALU.mult).then_inc(kept_ready, 1)

            for j in range(2):
                for p in range(STEPS):
                    tiles_at(work, p, j)
            with dve.Fori(2, AHEAD) as j:
                for p in range(STEPS):
                    tiles_at(work, p, j)
            with dve.Fori(0, NT - AHEAD) as i:
                for t in range(STEPS):
                    scan(t, i)
                    tiles_at(work, t, i + AHEAD)
            for i in range(NT - AHEAD, FIRST_DECAY):
                for t in range(STEPS):
                    scan(t, i)
                    tiles_at(work, t, i + AHEAD)

            def ssm_row(s, c):
                at = bass.ds((c % 2) * 4 * P + (s % 4) * P, P)
                return ssm[:, s // 4, bass.ds(half_q(c) + 1, 1), at].rearrange("p o n -> p (o n)")

            def feed(s, c):
                if s > 0:
                    recur(s - 1, c)
                elif not (isinstance(c, int) and c == 0):
                    recur(7, c - 1)
                dve.wait_ge(ssm_fed, c * 8 + s + 1)
                v.scalar_tensor_tensor(ssm_b_bar[:, s % 2, :], ssm_row(s, c), 1.0, PS[:, 6 + s % 2, 0:P],
                                       ALU.subtract, ALU.mult).then_inc(ssm_scaled, 1)

            def recur(s, c):
                m, k = s // 4, s % 4
                n = c * 8 + s
                row = ssm_row(s, c)
                dve.wait_ge(ssm_scaled, n + 1)
                dve.wait_ge(ssm_done, n - 7 + EIGHT_FREE)
                v.tensor_tensor_scan(row, row, ssm_b_bar[:, s % 2, :],
                                     ssm[:, m, bass.ds(half_q(c), 1), bass.ds((c % 2) * 4 * P + k * P + P - 1, 1)
                                         ].rearrange("p o n -> p (o n)"), ALU.mult, ALU.add).then_inc(ssm_done, 1)

            def readout(u, n, e, active, fed, kept_bodies):
                if 3 in active and u == 0:
                    dve.wait_ge(h2_ready, n - 3 + 1 + TWO_FREE)
                    v.bn_stats(ln_st[:, :], h_all[:, bass.ds(n - 3, 1), :].rearrange("p o n -> p (o n)")).then_inc(ln_stat_a, 1)
                if 3 in active and u == 1:
                    dve.wait_ge(ln_stat_a, n - 3 + 1)
                    dve.sem_inc(stats_waited, 1)
                    v.bn_aggr(ln_mv[:, 1 - e, :], ln_st[:, :]).then_inc(ln_stats, 1)
                if 1 in active and u == 1:
                    for r in range(2):
                        dve.wait_ge(read_piece, (n - 1) * 4 + (2 * r + 2) + EIGHT_FREE)
                        v.bn_stats(r_st[:, r, :], PS[:, 4 - 2 * e + r, 0:H]).then_inc(r_stat_a, 1)
                if 1 in active and u == 2:
                    j = n - 1
                    dve.wait_ge(r_stat_a, j * 2 + 2)
                    dve.wait_ge(r_dev_ready, j + FREE)
                    dve.sem_inc(stats_waited, 1)
                    for r in range(2):
                        last = v.bn_aggr(r_mv[:, r, :], r_st[:, r, :])
                    last.then_inc(r_stats, 1)
                if 1 in active and u == 3:
                    j = n - 1
                    dve.wait_ge(r_dev_ready, j + 1 + FREE)
                    dve.wait_ge(r_gelu, j - 1 + TWO_FREE)
                    for r in range(2):
                        last = v.scalar_tensor_tensor(r_pre[:, 1 - e, r, :], PS[:, 4 - 2 * e + r, H:H + P],
                                                      r_dev[:, 1 - e, r:r + 1], ro_row[:, :], ALU.mult, ALU.add)
                    last.then_inc(readout_scaled, 1)
                if 3 in active and u == 3:
                    j = n - 3
                    dve.wait_ge(ln_dev_ready, j + 1)
                    v.tensor_scalar(gate_all[:, bass.ds(j, 1), :].rearrange("p o n -> p (o n)"),
                                    h_all[:, bass.ds(j, 1), :].rearrange("p o n -> p (o n)"),
                                    ln_mv[:, 1 - e, 0:1], ln_small[:, 1 - e, 1:2], ALU.subtract, ALU.mult
                                    ).then_inc(readout_normed, 1)

            dve.wait_ge(gate_raw, NT + FREE)
            v.tensor_scalar(sp_tmp[:, 1, :], z_all[:, :], -1.0, None, ALU.mult).then_inc(sp_step, 1)
            dve.wait_ge(sp_step, 1)
            v.tensor_tensor(sp_tmp[:, 0, :], z_all[:, :], sp_tmp[:, 1, :], ALU.max).then_inc(sp_step, 1)
            v.tensor_scalar(delta[:, :], z_all[:, :], 0.0, None, ALU.max).then_inc(sp_step, 1)
            dve.wait_ge(sp_ready, 2)
            dve.wait_ge(sp_step, 3)
            v.tensor_tensor(delta[:, :], delta[:, :], sp_tmp[:, 0, :], ALU.add).then_inc(sp_step, 1)
            dve.wait_ge(pv_done, NA * NT + TWO_FREE)
            v.memset(ssm[:, :, 0, :].rearrange("p m (b n) -> p m b n", b=B)[:, :, :, P - 1:P], 0.0).then_inc(ssm_zeroed, 1)
            for t in range(STEPS):
                scan(t, FIRST_DECAY)
            dve.wait_ge(ssm_zeroed, 1)
            for t in range(STEPS):
                scan(t, FIRST_DECAY + 1)
                if t == 0:
                    dve.wait_ge(decayed, 4)
                if 7 <= t < 8:
                    feed(7, 0)
                elif t < 7:
                    feed(t, 0)
                if t >= 8:
                    feed(t - 8, 1)
            dve.wait_ge(decayed, 2 * 2 * NQ)
            for t in range(STEPS):
                scan(t, FIRST_READ)
                if t % 2 == 0:
                    feed(t // 2, FIRST_READ - FIRST_DECAY)
                body_readouts(readout, t, FIRST_READ)
            with dve.Fori(FIRST_READ + 1, BODIES) as i:
                for t in range(STEPS):
                    scan(t, i)
                    if t % 2 == 0:
                        feed(t // 2, i - FIRST_DECAY)
                    body_readouts(readout, t, i)
            recur(7, 2 * NQ - 1)
            rest_of_readouts(dve, readout)

        @block.tensor
        def _(pe):
            t_ = nc.tensor
            pe.wait_ge(cvec_ready, 1)
            pe.wait_ge(const_ready, 2)
            for m in range(NH):
                for k in range(NH):
                    t_.transpose(PS[:, 2, k * H + m * P:k * H + m * P + P], res_nat[:, m, k * P:k * P + P], ident[:, :])
                t_.transpose(PS[:, 3, m * P:m * P + P], in_nat[:, m, :], ident[:, :])
                t_.transpose(PS[:, 3, H + m * P:H + m * P + P], b_nat[:, m, :], ident[:, :])
                t_.transpose(PS[:, 4, P + m * P:2 * P + m * P], ro_nat[:, m * P:m * P + P], ident[:, :])
            t_.transpose(PS[:, 4, 0:P], gate_nat[:, :], ident[:, :])
            t_.matmul(PS[:, 5, 0:P], ones[:, :], ro_tmp[:, 0:P], start=True, stop=True)
            t_.matmul(PS[:, 5, P:P + 1], ones[:, :], setup[:, 11:12], start=True, stop=True).then_inc(wt_turned, 1)

            pe.wait_ge(wt_ready, 1)
            with pe.Fori(0, B // 2) as it:
                for i in range(2):
                    b = it * 2 + i
                    pe.wait_ge(x_loaded[i], it * 16 + 16)
                    pe.wait_ge(x_t_ready, b + FREE)
                    for k in range(NQ):
                        last = t_.transpose(MISC[:, k * P:k * P + P], x_in[:, i, k, :], ident[:, :])
                    last.then_inc(x_turned, 1)
                    pe.wait_ge(x_t_ready, b + 1 + FREE)
                    pe.wait_ge(v_rest, b + FREE)
                    pe.wait_ge(qk_rest, b + FREE)
                    for k in range(NQ):
                        last = t_.matmul(PS[:, 2 + k, 0:64 + NA * C], x_t[:, i, k, :], wall[:, :], start=True, stop=True)
                    last.then_inc(projected, 1)
                    pe.wait_ge(k_rows_ready, b + 1 + FREE)
                    pe.wait_ge(k_cols_ready, b + FREE)
                    turned = OUT2[1].bitcast(BF16).rearrange("p (a k n) -> p a k n", a=2, k=NQ)
                    for k in range(NQ):
                        for a in range(2):
                            last = t_.transpose(turned[:, a, k, :], k_rows[:, k, a * P:a * P + P], ident16[:, :])
                    last.then_inc(k_turned, 1)
            pe.wait_ge(k_cols_ready, B + FREE)
            pe.wait_ge(tiles_done, B + FREE)
            pe.wait_ge(q_rows_ready, B + FREE)

            def keep_clock(bank):
                t_.matmul(bank, ident16[:, :], ballast[:, :], start=True, stop=True, skip_group_check=True)

            def work(p, j):
                keys = k_cols[:, bass.ds(j % B, 1), :, :].rearrange("p o a n -> p (o a) n")
                peeled = isinstance(j, int)
                if p in (3, 7, 11, 15):
                    a = (p - 3) // 4
                    pe.wait_ge(q_ready, j * NA + a + FREE)
                    if a == 2 and not (peeled and j < 2):
                        pe.wait_ge(xn_ready, j - 1 + FREE)
                    if a == 3 and not (peeled and j < 2):
                        pe.wait_ge(gate_raw, j - 1 + FREE)
                    rows = q_rows[:, :, :, :].rearrange("p k b n -> p (k b) n")
                    at = (a // 2) * P
                    pe.sem_inc(queries_waited, 1)
                    t_.transpose(MISC16[:, 0:P], rows[:, bass.ds(j, 1), at:at + P].rearrange("p o n -> p (o n)"), ident16[:, :]
                                 ).then_inc(q_turned, 1)
                if p in (5, 9, 13, 17):
                    a = (p - 5) // 4
                    pe.wait_ge(q_ready, j * NA + (a + 1) + FREE)
                    pe.wait_ge(shift_placed, j * NA + (a - 1) + TWO_FREE)
                    if a in (0, 3):
                        keep_clock(SCORES[a % 2])
                    t_.matmul(SCORES[a % 2], q_cols[:, a, :], keys[:, a // 2, :], start=True, stop=True).then_inc(scored, 1)
                if p in (8, 12, 16, 20):
                    a = (p - 8) // 4
                    pe.wait_ge(shift_ready, j * NA + (a + 1))
                    t_.transpose(SCORES16[a % 2][:, 0:P], shift_rows[:, :], ident16[:, :]).then_inc(shift_turned, 1)
                if p in (12, 16, 20, 24):
                    a = (p - 12) // 4
                    pe.wait_ge(prob_ready, j * NA + a + FREE)
                    pe.wait_ge(shift_placed, j * NA + (a + 1) + TWO_FREE)
                    keep_clock(TURNED)
                    for k in range(NQ):
                        last = t_.matmul(TURNED[:, k * P:k * P + P], keys[:, a // 2, k * P:k * P + P], q_cols[:, a, :],
                                         start=k == 0, stop=k == NQ - 1, skip_group_check=True)
                    last.then_inc(turned_ready, 1)
                if p in (15, 19, 23, 27):
                    a = (p - 15) // 4
                    pe.wait_ge(prob_ready, j * NA + (a + 1) + FREE)
                    if a == 0:
                        pe.wait_ge(o_half, j + FREE)
                    if a == 2:
                        pe.wait_ge(o_ready, j + FREE)
                    weigh(a, j, prob_hi, VW)
                if p in (18, 22, 26, 30):
                    a = (p - 18) // 4
                    pe.wait_ge(prob_lo_ready, j * NA + (a + 1) + TWO_FREE)
                    weigh(a, j, prob_lo, 130).then_inc(pv_done, 1)
                if p == 41:
                    pe.wait_ge(hat_ready, j + 1)
                    pe.wait_ge(q_ready, min((j + 2) * NA + 2, NT * NA) + FREE if peeled else (j + 2) * NA + 2 + FREE)
                    t_.transpose(MISC[:, 0:P], x_hat[:, :], ident[:, :]).then_inc(hat_turned, 1)
                if p == 45:
                    pe.wait_ge(hat_copied, j + 1)
                    pe.wait_ge(xn_ready, j + 1 + FREE)
                    pe.wait_ge(q_ready, min((j + 2) * NA + 3, NT * NA) + FREE if peeled else (j + 2) * NA + 3 + FREE)
                    t_.matmul(MISC[:, 0:P + 1], x_hat_t[:, :], gate_t[:, :], start=True, stop=True).then_inc(gated, 1)

            def weigh(a, j, prob_part, width):
                dst = OUT2[a // 2][:, (a % 2) * 256:(a % 2) * 256 + width]
                for k in range(NQ):
                    vals = values[:, bass.ds((j % B) * NQ + k, 1), a * VW:a * VW + width].rearrange("p o w -> p (o w)")
                    last = t_.matmul(dst, prob_part[:, a % 2, k * P:k * P + P], vals, start=prob_part is prob_hi and k == 0,
                                     stop=prob_part is prob_lo and k == NQ - 1, skip_group_check=True)
                return last

            def scan(t, i):
                n = i * STEPS + (t + 1)
                pe.wait_ge(hi_ready, n)
                dst = PRE[t // 8][:, :, t % 8, :]
                for wts, st in ((res_hi, s_hi), (res_lo, s_hi), (res_hi, s_lo)):
                    if st is s_lo:
                        pe.wait_ge(lo_ready, n)
                    for k in range(NH):
                        for m in range(NH):
                            last = t_.matmul(dst[:, m, :], wts[:, k, m * P:m * P + P], st[:, k * B:k * B + B],
                                             start=False, stop=st is s_lo and k == NH - 1, skip_group_check=True)
                last.then_inc(pre_ready, 1)

            def fill(m, half, i):
                src = xn[:, bass.ds(i * SB + half * HALF, HALF)]
                t_.matmul(PS[:, half, m * HALF:m * HALF + HALF], in_t[:, m * P:m * P + P], src, start=m == 0, stop=True,
                          skip_group_check=True)

            def scan_body(t, i):
                scan(t, i)
                if t in (10, 11):
                    keep_clock(PS[:, 0, :])
                if t in (2, 6):
                    fill((t - 2) // 4, 1, i)
                if t in (14, 15):
                    fill(t - 14, 0, i + 1)

            for j in range(2):
                for p in range(STEPS):
                    tiles_at(work, p, j)
            with pe.Fori(2, AHEAD) as j:
                for p in range(STEPS):
                    tiles_at(work, p, j)
            pe.wait_ge(xn_ready, B + FREE)
            fill(0, 0, 0)
            fill(1, 0, 0)
            with pe.Fori(0, NT - AHEAD) as i:
                for t in range(STEPS):
                    if t == 14:
                        pe.wait_ge(xn_ready, i + (AHEAD - 2) + 1 + FREE)
                    scan_body(t, i)
                    tiles_at(work, t, i + AHEAD)
            for i in range(NT - AHEAD, FIRST_DECAY):
                for t in range(STEPS):
                    if t == 14:
                        pe.wait_ge(xn_ready, i + (AHEAD - 2) + 1 + FREE)
                    scan_body(t, i)
                    tiles_at(work, t, i + AHEAD)

            def feed(s, c):
                m, k = s // 4, s % 4
                pe.wait_ge(ssm_done, c * 8 + (s - 1) + EIGHT_FREE)
                xq = xn[:, 0:L * B].rearrange("p (q t b) -> p q b t", q=NQ, b=B)
                t_.matmul(PS[:, 6 + s % 2, 0:P], b_t[:, m * P:m * P + P],
                          xq[:, bass.ds(half_q(c), 1), bass.ds((c % 2) * 4 + k, 1), :].rearrange("p o b t -> p (o b t)"),
                          start=True, stop=True).then_inc(ssm_fed, 1)

            def spread_delta(n):
                c = n // 4
                if c >= 2:
                    pe.wait_ge(decayed, 2 * (c - 2) + 2)
                t_.matmul(PS[:, 4 + c % 2, (n % 4) * P:(n % 4) * P + P], delta[:, n:n + 1].to_broadcast([P, P]), ident[:, :],
                          start=True, stop=True).then_inc(spread, 1)

            def read_one(r, m, j, e):
                bank = PS[:, 2 + 2 * e + r, 0:4 * P].rearrange("p (g n) -> p g n", n=P)
                dst = bank[:, 0:3:2, :] if m == 0 else bank[:, 1:3, :]
                t_.matmul(dst, r_in[:, e, r, m, :], ro_pair[:, m, :].rearrange("p (g n) -> p g n", n=P),
                          start=m == 0, stop=m == NH - 1, skip_group_check=True).then_inc(read_piece, 1)

            def readout(u, n, e, active, fed, kept_bodies):
                if 1 in active and u == 0:
                    read_one(1, 1, n - 1, 1 - e)
                if 0 in active and u == 1:
                    pe.wait_ge(states_in, n + 1)
                    pe.wait_ge(readout_scaled, n - 1 + TWO_FREE)
                    keep_clock(PS[:, 2 + 2 * e, :])
                    read_one(0, 0, n, e)
                if 0 in active and u == 2:
                    read_one(0, 1, n, e)
                if 0 in active and u == 3:
                    pe.wait_ge(ssm_in, n + 1)
                    keep_clock(PS[:, 3 + 2 * e, :])
                    read_one(1, 0, n, e)

            pe.wait_ge(pv_done, NA * NT + TWO_FREE)
            pe.sem_inc(k_cols_free, 1)
            for t in range(STEPS):
                scan_body(t, FIRST_DECAY)
                if t == 4:
                    pe.wait_ge(sp_step, 4)
                if t >= 4:
                    spread_delta(2 * (t - 4))
                    spread_delta(2 * (t - 4) + 1)
            for t in range(STEPS):
                scan_body(t, FIRST_DECAY + 1)
                if t < 4:
                    spread_delta(24 + 2 * t)
                    spread_delta(24 + 2 * t + 1)
                if t < 8:
                    feed(t, 0)
                else:
                    feed(t - 8, 1)
                keep_clock(PS[:, 2, :])
            pe.wait_ge(decayed, 2 * 2 * NQ)
            for t in range(STEPS):
                scan_body(t, FIRST_READ)
                if t % 2 == 0:
                    feed(t // 2, FIRST_READ - FIRST_DECAY)
                body_readouts(readout, t, FIRST_READ)
            with pe.Fori(FIRST_READ + 1, BODIES) as i:
                for t in range(STEPS):
                    scan_body(t, i)
                    if t % 2 == 0:
                        feed(t // 2, i - FIRST_DECAY)
                    body_readouts(readout, t, i)
            rest_of_readouts(pe, readout)


_WEIGHTS = [f"L0_tok_w{n}" for n in range(1, 13)]
_OTHERS = ["L0_tok_alpha", "L0_tok_gamma", "L0_attn_norm_g", "L0_attn_norm_b", "L0_attn_W_in", "L0_attn_W_res",
           "L0_attn_A", "L0_attn_W_B", "L0_attn_w_delta", "L0_attn_b_delta", "L0_attn_ro_g", "L0_attn_ro_b",
           "L0_attn_W_ro", "L0_attn_b_ro", "L0_attn_W_gate", "L0_attn_b_gate"]


def kernel(**inputs):
    import concourse.bacc as bacc
    from concourse.bass_utils import run_bass_kernel_spmd

    nc = bacc.Bacc("TRN2", target_bir_lowering=False, num_devices=1)
    arrays, aps = {}, {}
    for name in ["x", *_WEIGHTS, *_OTHERS]:
        a = np.ascontiguousarray(inputs[name])
        if a.ndim == 0:
            a = a.reshape(1)
        arrays[f"in_{name}"] = a
        aps[name] = nc.dram_tensor(f"in_{name}", a.shape, mybir.dt.from_np(a.dtype), kind="ExternalInput").ap()
    out = nc.dram_tensor("out", (B, L, 2 * C), F32, kind="ExternalOutput").ap()
    build(nc, aps["x"], [aps[n] for n in _WEIGHTS], *[aps[n] for n in _OTHERS], out)
    r = run_bass_kernel_spmd(nc, [arrays], core_ids=[0])
    return r.results[0]["out"]
```

```python
from contextlib import ExitStack

import numpy as np
import concourse.bass as bass
from concourse import mybir

F32 = mybir.dt.float32
F16 = mybir.dt.float16
BF16 = mybir.dt.bfloat16
I32 = mybir.dt.int32
ALU = mybir.AluOpType
ACT = mybir.ActivationFunctionType
AX_X = mybir.AxisListType.X

B, L, C = 8, 512, 64
D = C // 8
P = 128
NA = 4
NQ = L // P
NT = NQ * B
H = 256
NH = H // P
STEPS = 16
BODIES = L // STEPS
SB = STEPS * B
HALF = SB // 2
HALF_STEPS = STEPS // 2
AHEAD = 10
SLOT = 64
SHIFT_AT = 32
VW = 194
LEAK, KEEP = 0.95, 1.0 - 0.95
EPS = 1e-5
MATS = NH * H + 2 * NH * P + H + P + NH + 4
ROWS = 2 * H + P + 3
STATE_UP = 4096.0
WEIGHT_UP = 128.0
SHIFT = 24.0


def build(nc, x, w_wall, w_mats, w_rows, out):
    ctx = ExitStack()
    with ctx:
        def sb(name, shape, dt=F32):
            return ctx.enter_context(nc.sbuf_tensor(name, shape, dt))

        def sem(name):
            return ctx.enter_context(nc.semaphore(name))

        ident = sb("ident", [P, P])
        ident16 = sb("ident16", [P, P], BF16)
        ballast = sb("ballast", [P, 512], BF16)
        ones = sb("ones", [P, P])
        wall = sb("wall", [P, 64 + NA * C])
        mats = sb("mats", [P, MATS])
        res_nat = mats[:, 0:NH * H].rearrange("p (m k) -> p m k", m=NH)
        in_nat = mats[:, 512:768].rearrange("p (m k) -> p m k", m=NH)
        b_nat = mats[:, 768:1024].rearrange("p (m k) -> p m k", m=NH)
        ro_nat = mats[:, 1024:1280]
        gate_nat = mats[:, 1280:1408]
        a_cols = mats[:, 1408:1410]
        cols = mats[:, 1410:1414]
        rows = sb("rows", [P, ROWS])
        ro_g_row, ro_b_row, b_gate_row = rows[:, 0:H], rows[:, H:2 * H], rows[:, 2 * H:2 * H + P]
        b_delta_col, alpha_col, gamma_col = (rows[:, 2 * H + P + n:2 * H + P + n + 1] for n in range(3))
        ro_tmp = sb("ro_tmp", [P, H])
        neg_inv_a = sb("neg_inv_a", [P, NH])
        mix = sb("mix", [P, NA])
        setup = sb("setup", [P, 16])
        res_hi = sb("res_hi", [P, NH, H], F16)
        res_lo = sb("res_lo", [P, NH, H], F16)
        in_t = sb("in_t", [P, H])
        b_t = sb("b_t", [P, H])
        gate_t = sb("gate_t", [P, P + 1])
        ro_pair = sb("ro_pair", [P, NH, 2 * P])
        ro_row = sb("ro_row", [P, P])

        states = sb("states", [P, BODIES, STEPS * NH * B])
        early = states[:, :, :].rearrange("p i n -> p (i n)")
        x_in = early[:, 0:1024].rearrange("p (i k n) -> p i k n", i=2, k=NQ)
        x_t = early[:, 1024:1280].rearrange("p (i n) -> p i n", i=2)
        rest_v = early[:, 2048:3072].rearrange("p (k n) -> p k n", k=NQ)
        rest_qk = early[:, 3072:3328].rearrange("p (h k n) -> p h k n", h=2, k=NQ)
        part = early[:, 3328:4096].bitcast(BF16).rearrange("p (i l h k n) -> p i l h k n", i=2, l=3, h=2, k=NQ)
        k_rows = early[:, 4096:4608].bitcast(BF16).rearrange("p (k n) -> p k n", k=NQ)
        res_abs = early[:, 4608:4608 + NH * H]
        q_rows = sb("q_rows", [P, NQ, B, NA * SLOT], BF16)
        k_cols = sb("k_cols", [P, B, 2, L], BF16)
        values = sb("values", [P, B * NQ, NA * VW], BF16)

        q_cols = sb("q_cols", [P, NA, P], BF16)
        top = sb("top", [P, 2])
        shift = sb("shift", [P, 1])
        shift_rows = sb("shift_rows", [P, P], BF16)
        prob = sb("prob", [P, 2, L])
        prob_hi = sb("prob_hi", [P, 2, L], F16)
        prob_lo = sb("prob_lo", [P, 2, L], F16)
        o_sb = sb("o_sb", [P, NA, VW])
        o_sum = sb("o_sum", [P, NA, C])
        coef = sb("coef", [P, NA])
        h_now = sb("h_now", [P, P])
        stats = sb("stats", [P, 6])
        mean_var = sb("mean_var", [P, 2])
        small = sb("small", [P, 8])
        minus_half = sb("minus_half", [P, 1])
        eps_col = sb("eps_col", [P, 1])
        half_col = sb("half_col", [P, 1])
        x_hat = sb("x_hat", [P, P])
        x_hat_t = sb("x_hat_t", [P, P])
        gate_pre = sb("gate_pre", [P, P])

        h_all = sb("h_all", [P, NT, P])
        gate_all = sb("gate_all", [P, NT, P])
        xn = sb("xn", [P, L * B + HALF])
        z_all = sb("z_all", [P, NT])

        y = sb("y", [P, NH * B])
        s_hi = sb("s_hi", [P, NH * B], F16)
        s_lo = sb("s_lo", [P, NH * B], F16)
        kept = sb("kept", [P, NH * B])
        s_body = sb("s_body", [P, STEPS, NH * B])


        delta = sb("delta", [P, NT])
        sp_tmp = sb("sp_tmp", [P, 2, NT])
        r_mv = sb("r_mv", [P, 2, 2])
        r_st = sb("r_st", [P, 2, 6])
        r_eps = sb("r_eps", [P, 2])
        r_var = sb("r_var", [P, 2])
        r_dev = sb("r_dev", [P, 2, 2])
        ln_st = sb("ln_st", [P, 6])
        ln_mv = sb("ln_mv", [P, 2, 2])
        ln_small = sb("ln_small", [P, 2, 2])
        v32 = values[:, :, :].rearrange("p k n -> p (k n)").bitcast(F32)
        SSM_LEN = NH * (NQ + 1) * B * P
        ssm = v32[:, 0:SSM_LEN].rearrange("p (m q n) -> p m q n", m=NH, q=NQ + 1)
        ssm_b_bar = v32[:, SSM_LEN:SSM_LEN + 2 * P].rearrange("p (s n) -> p s n", s=2)
        assert SSM_LEN + 2 * P <= B * NQ * NA * VW // 2
        k32 = k_cols[:, :, :, :].rearrange("p b a n -> p (b a n)").bitcast(F32)
        r_in = k32[:, 0:4 * NH * P].rearrange("p (e r m n) -> p e r m n", e=2, r=2, m=NH)
        r_pre = k32[:, 1024:1024 + 4 * P].rearrange("p (e r n) -> p e r n", e=2, r=2)
        r_act = k32[:, 1536:1536 + 4 * P].rearrange("p (e r n) -> p e r n", e=2, r=2)
        r_diff = k32[:, 2048:2048 + P]
        r_base = k32[:, 2176:2176 + P]

        PS = ctx.enter_context(nc.psum_tensor("PS", [P, 8, 512], F32))
        PRE = [PS[:, i, 0:SB].rearrange("p (m t b) -> p m t b", m=NH, b=B) for i in range(2)]
        SCORES = [PS[:, 2, :], PS[:, 3, :]]
        SCORES16 = [one.bitcast(BF16) for one in SCORES]
        TURNED = PS[:, 4, :]
        OUT2 = [PS[:, 5, :], PS[:, 6, :]]
        MISC = PS[:, 7, :]
        MISC16 = MISC.bitcast(BF16)

        wall_loaded = sem("wall_loaded")
        mats_loaded = sem("mats_loaded")
        rows_loaded = sem("rows_loaded")
        x_loaded_even = sem("x_loaded_even")
        x_loaded_odd = sem("x_loaded_odd")
        const_ready = sem("const_ready")
        dve_seq = sem("dve_seq")
        zeros_ready = sem("zeros_ready")
        amax_ready = sem("amax_ready")
        wt_turned = sem("wt_turned")
        hi_made = sem("hi_made")
        wt_ready = sem("wt_ready")
        cvec_ready = sem("cvec_ready")
        x_turned = sem("x_turned")
        x_t_ready = sem("x_t_ready")
        projected = sem("projected")
        first_ready = sem("first_ready")
        v_rest = sem("v_rest")
        qk_rest = sem("qk_rest")
        v_second = sem("v_second")
        qk_step = sem("qk_step")
        qk_parts = sem("qk_parts")
        v_done = sem("v_done")
        k_rows_ready = sem("k_rows_ready")
        q_rows_ready = sem("q_rows_ready")
        k_turned = sem("k_turned")
        k_cols_ready = sem("k_cols_ready")
        q_turned = sem("q_turned")
        q_ready = sem("q_ready")
        scored = sem("scored")
        top_ready = sem("top_ready")
        shift_raw = sem("shift_raw")
        shift_ready = sem("shift_ready")
        shift_turned = sem("shift_turned")
        shift_placed = sem("shift_placed")
        turned_ready = sem("turned_ready")
        prob_ready = sem("prob_ready")
        prob_lo_ready = sem("prob_lo_ready")
        pv_done = sem("pv_done")
        o_half = sem("o_half")
        o_ready = sem("o_ready")
        inv_ready = sem("inv_ready")
        coef_ready = sem("coef_ready")
        sum_a = sem("sum_a")
        sum_b = sem("sum_b")
        sum_c = sem("sum_c")
        h_ready = sem("h_ready")
        h_kept = sem("h_kept")
        stat_a = sem("stat_a")
        stat_ready = sem("stat_ready")
        norm_step = sem("norm_step")
        norm_ready = sem("norm_ready")
        hat_ready = sem("hat_ready")
        hat_turned = sem("hat_turned")
        hat_copied = sem("hat_copied")
        xn_ready = sem("xn_ready")
        gated = sem("gated")
        gate_raw = sem("gate_raw")
        gate_ready = sem("gate_ready")
        pre_ready = sem("pre_ready")
        acted = sem("acted")
        hi_ready = sem("hi_ready")
        full_ready = sem("full_ready")
        lo_ready = sem("lo_ready")
        kept_ready = sem("kept_ready")
        saved = sem("saved")
        sp_step = sem("sp_step")
        sp_ready = sem("sp_ready")
        k_cols_free = sem("k_cols_free")
        spread = sem("spread")
        decayed = sem("decayed")
        ssm_zeroed = sem("ssm_zeroed")
        ssm_fed = sem("ssm_fed")
        ssm_scaled = sem("ssm_scaled")
        ssm_done = sem("ssm_done")
        states_in = sem("states_in")
        ssm_in = sem("ssm_in")
        read_piece = sem("read_piece")
        r_stat_a = sem("r_stat_a")
        r_stats = sem("r_stats")
        r_var_ready = sem("r_var_ready")
        r_dev_ready = sem("r_dev_ready")
        readout_scaled = sem("readout_scaled")
        r_gelu = sem("r_gelu")
        gate_scaled = sem("gate_scaled")
        r_diff_ready = sem("r_diff_ready")
        r_blend = sem("r_blend")
        r_base_ready = sem("r_base_ready")
        h2_ready = sem("h2_ready")
        ln_stat_a = sem("ln_stat_a")
        ln_stats = sem("ln_stats")
        ln_var_ready = sem("ln_var_ready")
        ln_dev_ready = sem("ln_dev_ready")
        readout_normed = sem("readout_normed")
        stats_waited = sem("stats_waited")
        pool_waited = sem("pool_waited")
        queries_waited = sem("queries_waited")
        r_out = sem("r_out")
        out_done = sem("out_done")
        FREE, TWO_FREE, FOUR_FREE, EIGHT_FREE = 1, 2, 4, 8
        start_free = (gate_raw, gate_ready, h_kept, inv_ready, k_cols_ready, k_rows_ready, k_turned, q_rows_ready, sum_b, r_dev_ready, prob_ready, shift_turned, o_half, o_ready, q_ready, xn_ready)
        start_two_free = (saved, x_t_ready, projected, shift_placed, prob_lo_ready, pv_done, readout_scaled, r_gelu, h2_ready)


        x_loaded = [x_loaded_even, x_loaded_odd]

        def tile_q(j):
            if isinstance(j, int):
                return j // B
            return nc.s_assert_within(j >> 3, 0, NQ - 1, skip_runtime_bounds_check_because="j is below NT = 8 * NQ")

        def place(z):
            return z * D if z < SHIFT_AT // D else (z + 1) * D

        def tiles_at(work, p, newest, before_scan=False):
            for lag in (2, 1, 0):
                j = newest - lag
                if not isinstance(j, int) or 0 <= j < NT:
                    work(p + STEPS * lag, j, before_scan)

        def half_q(c):
            if isinstance(c, int):
                return c // 2
            return nc.s_assert_within(c >> 1, 0, NQ - 1, skip_runtime_bounds_check_because="c is below 2 * NQ")

        FIRST_DECAY = NT - AHEAD + 2
        FIRST_READ = FIRST_DECAY + 2
        LAGS = 5
        IN_SCAN = (BODIES - FIRST_READ) * 4
        assert IN_SCAN * P // B <= FIRST_DECAY * STEPS and BODIES - FIRST_READ + 2 == 2 * NQ

        def body_readouts(readout, t, i):
            n = (i - FIRST_READ) * 4 + t // 4
            active = range(LAGS) if not isinstance(i, int) else range(min(LAGS, n + 1))
            readout(t % 4, n, (t // 4) % 2, active, (i - FIRST_READ) * 4 * NH + 4 * NH, FIRST_DECAY)

        def rest_of_readouts(engine, readout):
            with engine.Fori(IN_SCAN // 2, NT // 2) as two:
                for e in range(2):
                    for u in range(4):
                        readout(u, two * 2 + e, e, range(LAGS), NT * NH, BODIES)
            for n in range(NT, NT + LAGS - 1):
                for u in range(4):
                    readout(u, n, n % 2, range(n - NT + 1, LAGS), NT * NH, BODIES)

        def tile_b(j):
            return j % B

        block = ctx.enter_context(nc.Block())

        x_v = x.rearrange("b (k p) c s -> p b k (c s)", p=P)

        @block.sync
        def _(sp):
            sp.dma_start(wall[:, :], w_wall).then_inc(wall_loaded, 16)
            for i in range(2):
                sp.dma_start(x_in[:, i, :, :], x_v[:, i, :, :]).then_inc(x_loaded[i], 16)
            with sp.Fori(1, B // 2) as it:
                for i in range(2):
                    sp.wait_ge(x_turned, (it * 2 + i - 1) * NQ)
                    sp.dma_start(x_in[:, i, :, :], x_v[:, bass.ds(it * 2 + i, 1), :, :]).then_inc(x_loaded[i], 16)
            out_v = out.rearrange("b (q p) c -> p q b c", p=P)
            with sp.Fori(0, NT) as j:
                sp.wait_ge(r_out, j + 1)
                sp.dma_start(out_v[:, bass.ds(tile_q(j), 1), bass.ds(j % B, 1), :], gate_all[:, bass.ds(j, 1), :]
                             ).then_inc(out_done, 16)
            sp.wait_ge(out_done, 16 * NT)

        @block.gpsimd
        def _(pool):
            g = nc.gpsimd
            for one in start_free:
                pool.sem_inc(one, FREE)
            for two in start_two_free:
                pool.sem_inc(two, TWO_FREE)
            for four in (turned_ready, qk_rest, v_done):
                pool.sem_inc(four, FOUR_FREE)
            for eight in (read_piece, ssm_done):
                pool.sem_inc(eight, EIGHT_FREE)
            g.memset(ident[:, :], 0.0).then_inc(zeros_ready, 1)
            pool.wait_ge(zeros_ready, 1)
            g.affine_select(out=ident[:, :], in_=ident[:, :], compare_op=ALU.not_equal, fill=1.0, base=0,
                            pattern=[[-1, P]], channel_multiplier=1).then_inc(const_ready, 1)
            stacks = k_rows[:, :, :].rearrange("p k (a n) -> p (k a) n", n=SLOT)
            g.memset(stacks[:, :, SHIFT_AT:SHIFT_AT + 2], -1.0)
            g.memset(stacks[:, :, SHIFT_AT + 2:SHIFT_AT + D], 0.0)
            g.memset(stacks[:, :, 7 * D:], 0.0)
            g.memset(shift_rows[:, :], 0.0)
            g.memset(q_cols[:, :, :], 0.0)
            g.memset(minus_half[:, :], -0.5)
            g.memset(eps_col[:, :], EPS)
            g.memset(half_col[:, :], 0.5)
            g.memset(ones[:, :], 1.0)
            g.memset(ballast[:, :], 0.0)
            pool.wait_ge(const_ready, 1)
            g.tensor_copy(ident16[:, :], ident[:, :]).then_inc(const_ready, 1)
            flat = values[:, :, :].rearrange("p k (a w) -> p (k a) w", w=VW)
            g.memset(flat[:, :, 2 * C:2 * C + 2], 1.0).then_inc(const_ready, 1)
            g.memset(xn[:, L * B:], 0.0)
            g.memset(r_eps[:, 0:1], EPS * STATE_UP ** 2)
            g.memset(r_eps[:, 1:2], EPS)
            pool.wait_ge(dve_seq, 3)
            g.partition_all_reduce(setup[:, 3:4], setup[:, 2:3], P, bass.bass_isa.ReduceOp.max).then_inc(amax_ready, 1)

            def split(b, i):
                for k in range(NQ):
                    n = b * NQ + k
                    pool.wait_ge(v_second, n + 1)
                    pool.sem_inc(pool_waited, 1)
                    vals = values[:, bass.ds(n, 1), :].rearrange("p k (a w) -> p (k a) w", w=VW)
                    g.tensor_tensor(vals[:, :, 130:130 + C], rest_v[:, k, :].rearrange("p (a c) -> p a c", c=C),
                                    vals[:, :, C:2 * C], ALU.subtract).then_inc(v_done, 1)

            with pool.Fori(0, B // 2) as it:
                for i in range(2):
                    split(it * 2 + i, i)

            def work(p, j, before_scan):
                if p in ((14, 22) if before_scan else (14, 18, 22, 26)):
                    a = (p - 14) // 4
                    if before_scan:
                        pool.wait_ge(prob_lo_ready, j * NA + a + TWO_FREE)
                    pool.wait_ge(prob_ready, j * NA + (a + 1) + FREE)
                    pool.wait_ge(pv_done, j * NA + (a - 1) + TWO_FREE)
                    g.tensor_tensor(prob_lo[:, a % 2, :], prob[:, a % 2, :], prob_hi[:, a % 2, :], ALU.subtract
                                    ).then_inc(prob_lo_ready, 1)
                if p == 32:
                    pool.wait_ge(o_ready, j + 1 + FREE)
                    g.tensor_tensor(o_sum[:, :, :], o_sb[:, :, C:2 * C], o_sb[:, :, 130:130 + C], ALU.add).then_inc(sum_a, 1)
                    pool.wait_ge(sum_a, j + 1)
                    g.tensor_tensor(o_sum[:, :, :], o_sum[:, :, :], o_sb[:, :, 0:C], ALU.add).then_inc(sum_b, 1)
                if p == 33:
                    pool.wait_ge(sum_b, j + 1 + FREE)
                    pool.wait_ge(coef_ready, j + 1)
                    g.tensor_tensor(o_sum[:, :, :], o_sum[:, :, :], coef[:, :].unsqueeze(2).to_broadcast([P, NA, C]), ALU.mult
                                    ).then_inc(sum_c, 1)
                    pool.wait_ge(sum_c, j + 1)
                    pool.wait_ge(h_kept, j + FREE)
                    o4 = o_sum[:, :, :].rearrange("p (g k) c -> p g k c", k=2)
                    g.tensor_tensor(h_now[:, :].rearrange("p (g c) -> p g c", c=C), o4[:, :, 0, :], o4[:, :, 1, :], ALU.add
                                    ).then_inc(h_ready, 1)
                if p == 37:
                    pool.wait_ge(stat_ready, j + 1)
                    n0 = j * 6

                    def step(i, n):
                        i.then_inc(norm_step, 1)
                        pool.wait_ge(norm_step, n0 + n)
                    step(g.tensor_tensor(small[:, 0:1], mean_var[:, 1:2], eps_col[:, :], ALU.add), 1)
                    step(g.tensor_tensor(small[:, 1:2], small[:, 0:1], minus_half[:, :], ALU.pow), 2)
                    step(g.tensor_tensor(small[:, 2:3], small[:, 1:2], small[:, 1:2], ALU.mult), 3)
                    step(g.tensor_tensor(small[:, 2:3], small[:, 2:3], mean_var[:, 1:2], ALU.mult), 4)
                    step(g.tensor_tensor(small[:, 3:4], small[:, 2:3], eps_col[:, :], ALU.add), 5)
                    step(g.tensor_tensor(small[:, 4:5], small[:, 3:4], minus_half[:, :], ALU.pow), 6)
                    pool.wait_ge(gate_raw, j + FREE)
                    g.tensor_tensor(small[:, 5:6], small[:, 3:4], small[:, 4:5], ALU.mult)
                    g.tensor_tensor(small[:, 6:7], small[:, 1:2], small[:, 4:5], ALU.mult).then_inc(norm_ready, 1)



            for j in range(2):
                for p in range(STEPS):
                    tiles_at(work, p, j, before_scan=True)
            with pool.Fori(2, AHEAD) as j:
                for p in range(STEPS):
                    tiles_at(work, p, j, before_scan=True)
            with pool.Fori(0, NT - AHEAD) as i:
                for p in range(STEPS):
                    tiles_at(work, p, i + AHEAD)
            for i in range(NT - AHEAD, FIRST_DECAY):
                for p in range(STEPS):
                    tiles_at(work, p, i + AHEAD)

            def readout(u, n, e, active, fed, kept_bodies):
                if 4 in active and u == 0:
                    j = n - 4
                    pool.wait_ge(readout_normed, j + 1)
                    pool.sem_inc(pool_waited, 1)
                    res = gate_all[:, bass.ds(j, 1), :].rearrange("p o n -> p (o n)")
                    g.tensor_tensor(res, res, h_all[:, bass.ds(j, 1), :].rearrange("p o n -> p (o n)"), ALU.add
                                    ).then_inc(r_out, 1)
                if 2 in active and u == 1:
                    j = n - 2
                    now = h_all[:, bass.ds(j, 1), :].rearrange("p o n -> p (o n)")
                    pool.wait_ge(r_gelu, j + 1 + TWO_FREE)
                    g.tensor_tensor(r_diff, r_act[:, e, 0, :], r_act[:, e, 1, :], ALU.subtract).then_inc(r_diff_ready, 1)
                    g.tensor_tensor(r_base, r_act[:, e, 1, :], now, ALU.add).then_inc(r_base_ready, 1)
                if 3 in active and u == 2:
                    j = n - 3
                    s = 1 - e
                    pool.wait_ge(ln_stats, j + 1)
                    g.tensor_tensor(ln_small[:, s, 0:1], ln_mv[:, s, 1:2], eps_col[:, :], ALU.add).then_inc(ln_var_ready, 1)
                    pool.wait_ge(ln_var_ready, j + 1)
                    g.tensor_tensor(ln_small[:, s, 1:2], ln_small[:, s, 0:1], minus_half[:, :], ALU.pow
                                    ).then_inc(ln_dev_ready, 1)
                if 2 in active and u == 2:
                    j = n - 2
                    pool.wait_ge(r_diff_ready, j + 1)
                    pool.wait_ge(gate_scaled, j + 1)
                    pool.sem_inc(pool_waited, 1)
                    g.tensor_tensor(r_diff, r_diff, gate_all[:, bass.ds(j, 1), :].rearrange("p o n -> p (o n)"), ALU.mult
                                    ).then_inc(r_blend, 1)
                    now = h_all[:, bass.ds(j, 1), :].rearrange("p o n -> p (o n)")
                    pool.wait_ge(r_blend, j + 1)
                    pool.wait_ge(r_base_ready, j + 1)
                    pool.sem_inc(pool_waited, 1)
                    g.tensor_tensor(now, r_base, r_diff, ALU.add).then_inc(h2_ready, 1)
                if 1 in active and u == 2:
                    j = n - 1
                    pool.wait_ge(r_stats, j + 1)
                    g.tensor_tensor(r_var[:, :], r_mv[:, :, 1:2].rearrange("p r o -> p (r o)"), r_eps[:, :], ALU.add
                                    ).then_inc(r_var_ready, 1)
                    pool.wait_ge(r_var_ready, j + 1)
                    pool.wait_ge(readout_scaled, j - 1 + TWO_FREE)
                    g.tensor_tensor(r_dev[:, 1 - e, :], r_var[:, :], minus_half[:, :].to_broadcast([P, 2]), ALU.pow
                                    ).then_inc(r_dev_ready, 1)


            pool.wait_ge(h_kept, NT + FREE)
            pool.wait_ge(k_cols_free, 1)
            for t in range(STEPS):
                body_readouts(readout, t, FIRST_READ)
            with pool.Fori(FIRST_READ + 1, BODIES) as i:
                for t in range(STEPS):
                    body_readouts(readout, t, i)
            rest_of_readouts(pool, readout)

        @block.scalar
        def _(act):
            a_ = nc.scalar
            act.dma_start(mats[:, :], w_mats).then_inc(mats_loaded, 16)
            act.dma_start(rows[:, :], w_rows.to_broadcast([P, ROWS])).then_inc(rows_loaded, 16)
            act.preload_act_table(ACT.Exp)

            def copy_x(b, k):
                n = b * NQ + k
                act.wait_ge(x_turned, n + 1)
                act.wait_ge(projected, n - 1 + TWO_FREE)
                a_.copy(x_t[:, k % 2, :], PS[:, k % 2, 0:P]).then_inc(x_t_ready, 1)

            def first_parts(b, i, k):
                n = b * NQ + k
                act.wait_ge(projected, n + 1 + TWO_FREE)
                if k == 0:
                    act.wait_ge(const_ready, 3)
                v1 = values[:, bass.ds(n, 1), :].rearrange("p o (a w) -> p (o a) w", w=VW)
                a_.copy(v1[:, :, 0:C], PS[:, 2 + k, 64:64 + NA * C].rearrange("p (a c) -> p a c", c=C))
                if k == 0 and not (isinstance(b, int) and b < 2):
                    act.wait_ge(k_rows_ready, b - 1 + FREE)
                    act.wait_ge(q_rows_ready, b - 1 + FREE)
                a_.copy(part[:, i, 0, :, k, :], PS[:, 2 + k, 0:64].rearrange("p (h n) -> p h n", h=2)).then_inc(first_ready, 1)

            def copy_keys(b):
                act.wait_ge(k_turned, b + 1 + FREE)
                a_.copy(k_cols[:, bass.ds(b, 1), :, :].rearrange("p o a n -> p (o a n)"), OUT2[1].bitcast(BF16)
                        ).then_inc(k_cols_ready, 1)

            def stack_queries(b, i):
                act.wait_ge(qk_parts, b * NQ + NQ)
                qr = q_rows[:, :, bass.ds(b, 1), :].rearrange("p k o (a n) -> p k (o a) n", n=SLOT)
                pq = part[:, i, :, 0, :, :].rearrange("p l k (a d) -> p l k a d", d=D)
                for l, slots in enumerate(((0, 3, 5), (1, 4), (2,))):
                    for z in slots:
                        last = a_.copy(qr[:, :, :, place(z):place(z) + D], pq[:, l, :, :, :])
                last.then_inc(q_rows_ready, 1)

            def project(b, i):
                for k in range(NQ):
                    if k + 1 < NQ:
                        copy_x(b, k + 1)
                    elif not (isinstance(b, int) and b == B - 1):
                        copy_x(b + 1, 0)
                    first_parts(b, i, k)
                    if k == 1 and not (isinstance(b, int) and b == 0):
                        stack_queries(b - 1, 1 - i)
                    if k == 2 and not (isinstance(b, int) and b == 0):
                        copy_keys(b - 1)

            copy_x(0, 0)
            for b in range(2):
                project(b, b % 2)
            with act.Fori(1, B // 2 - 1) as it:
                for i in range(2):
                    project(it * 2 + i, i)
            for b in range(B - 2, B):
                project(b, b % 2)
            stack_queries(B - 1, (B - 1) % 2)
            copy_keys(B - 1)

            def work(p, j, before_scan):
                if p in (4, 8, 12, 16):
                    a = (p - 4) // 4
                    act.wait_ge(q_turned, j * NA + (a + 1))
                    act.wait_ge(turned_ready, j * NA + (a - 3) + FOUR_FREE)
                    rows = slice(0, 64) if a % 2 == 0 else slice(64, P)
                    a_.copy(q_cols[rows, a, :], MISC16[rows, 0:P]).then_inc(q_ready, 1)
                if p - 2 * before_scan in (9, 13, 17, 21):
                    a = (p - 9) // 4
                    at = (a % 2) * SLOT + SHIFT_AT
                    act.wait_ge(shift_turned, j * NA + (a + 1) + FREE)
                    a_.copy(q_cols[at:at + 2, a, :], SCORES16[a % 2][at:at + 2, 0:P]).then_inc(shift_placed, 1)
                if p in (13, 17, 21, 25):
                    a = (p - 13) // 4
                    act.wait_ge(turned_ready, j * NA + (a + 1) + FOUR_FREE)
                    act.wait_ge(prob_lo_ready, j * NA + (a - 1) + TWO_FREE)
                    a_.activation(prob[:, a % 2, :], TURNED, ACT.Exp, scale=float(D) ** -0.5)
                if p in (14, 18, 22, 26):
                    a = (p - 14) // 4
                    act.wait_ge(pv_done, j * NA + (a - 1) + TWO_FREE)
                    a_.activation(prob_hi[:, a % 2, :], TURNED, ACT.Exp, scale=float(D) ** -0.5).then_inc(prob_ready, 1)
                if p in (23, 31):
                    n = (p - 23) // 8
                    act.wait_ge(pv_done, j * NA + 2 * n + 2 + TWO_FREE)
                    if n == 0:
                        act.wait_ge(sum_b, j + FREE)
                        act.wait_ge(inv_ready, j + FREE)
                    a_.copy(o_sb[:, 2 * n:2 * n + 2, :], OUT2[n].rearrange("p (a w) -> p a w", a=2)[:, :, 0:VW]
                            ).then_inc(o_ready if n else o_half, 1)
                if p == 36:
                    act.wait_ge(h_ready, j + 1)
                    a_.copy(h_all[:, bass.ds(j, 1), :].rearrange("p o n -> p (o n)"), h_now[:, :]).then_inc(h_kept, 1)
                if p == 47:
                    act.wait_ge(gate_raw, j + 1 + FREE)
                    a_.activation(gate_all[:, bass.ds(j, 1), :].rearrange("p o n -> p (o n)"), gate_pre[:, :], ACT.Tanh,
                                  scale=0.5).then_inc(gate_ready, 1)

            def scan(t, i):
                act.wait_ge(pre_ready, i * STEPS + (t + 1))
                a_.activation(y[:, :].rearrange("p (m b) -> p m b", m=NH), PRE[t // 8][:, :, t % 8, :], ACT.Tanh,
                              scale=back).then_inc(acted, 1)

            def save(half, i):
                act.wait_ge(full_ready, i * STEPS + (half + 1) * HALF_STEPS)
                n = HALF_STEPS * NH * B
                a_.copy(states[:, bass.ds(i, 1), half * n:half * n + n].rearrange("p o n -> p (o n)"),
                        s_body[:, half * HALF_STEPS:(half + 1) * HALF_STEPS, :].rearrange("p t n -> p (t n)")
                        ).then_inc(saved, 1)


            for j in range(2):
                for p in range(STEPS):
                    tiles_at(work, p, j, before_scan=True)
            with act.Fori(2, AHEAD) as j:
                for p in range(STEPS):
                    tiles_at(work, p, j, before_scan=True)
            act.wait_ge(wt_ready, 1)
            back = act.alloc_register("back")
            act.reg_load(back, setup[0:1, 7:8].bitcast(I32))
            with act.Fori(0, NT - AHEAD) as i:
                for t in range(STEPS):
                    scan(t, i)
                    tiles_at(work, t, i + AHEAD)
                    if t % HALF_STEPS == 7:
                        save(t // HALF_STEPS, i)
            for i in range(NT - AHEAD, FIRST_DECAY):
                for t in range(STEPS):
                    scan(t, i)
                    tiles_at(work, t, i + AHEAD)
                    if t % HALF_STEPS == 7:
                        save(t // HALF_STEPS, i)

            def decay(n):
                c, m = n // 2, n % 2
                act.wait_ge(spread, 4 * c + 4)
                a_.activation(ssm[:, m, 1 + c // 2, (c % 2) * 4 * P:(c % 2) * 4 * P + 4 * P], PS[:, 4 + c % 2, :], ACT.Exp,
                              scale=a_cols[:, m:m + 1]).then_inc(decayed, 1)

            def readout(u, n, e, active, fed, kept_bodies):
                if 0 in active and u == 0:
                    act.wait_ge(read_piece, n * 4 - 4 + EIGHT_FREE)
                    act.wait_ge(saved, 2 * kept_bodies + TWO_FREE)
                    src = states[:, bass.ds(tile_q(n) * B, B), :].rearrange("p i (t m b) -> p m (i t) b", m=NH, b=B)
                    a_.copy(r_in[:, e, 0, :, :], src[:, :, :, bass.ds(n % B, 1)].rearrange("p m t o -> p m (t o)")
                            ).then_inc(states_in, 1)
                if 2 in active and u == 0:
                    j = n - 2
                    act.wait_ge(readout_scaled, j + 1 + TWO_FREE)
                    act.wait_ge(h2_ready, j - 1 + TWO_FREE)
                    a_.activation(r_act[:, e, :, :], r_pre[:, e, :, :], ACT.Gelu).then_inc(r_gelu, 1)
                if 0 in active and u == 1:
                    act.wait_ge(ssm_done, fed + EIGHT_FREE)
                    a_.copy(r_in[:, e, 1, :, :], ssm[:, :, bass.ds(tile_q(n) + 1, 1), bass.ds((n % B) * P, P)
                                                     ].rearrange("p m o n -> p m (o n)")).then_inc(ssm_in, 1)
                if 1 in active and u == 2:
                    gate = gate_all[:, bass.ds(n - 1, 1), :].rearrange("p o n -> p (o n)")
                    a_.activation(gate, gate, ACT.Identity, scale=0.5, bias=half_col[:, :]).then_inc(gate_scaled, 1)

            act.wait_ge(sp_step, 2)
            a_.activation(sp_tmp[:, 0, :], sp_tmp[:, 0, :], ACT.Exp, scale=-1.0).then_inc(sp_ready, 1)
            act.preload_act_table_set("natural_log_exp_and_others")
            act.wait_ge(sp_ready, 1)
            a_.activation(sp_tmp[:, 0, :], sp_tmp[:, 0, :], ACT.Ln, bias=1.0).then_inc(sp_ready, 1)
            act.preload_act_table(ACT.Exp)
            act.wait_ge(pv_done, NA * NT + TWO_FREE)
            for t in range(STEPS):
                scan(t, FIRST_DECAY)
                if t >= 6:
                    decay(t - 6)
                if t % HALF_STEPS == 7:
                    save(t // HALF_STEPS, FIRST_DECAY)
            for t in range(STEPS):
                scan(t, FIRST_DECAY + 1)
                if t < 6:
                    decay(t + 10)
                if t % HALF_STEPS == 7:
                    save(t // HALF_STEPS, FIRST_DECAY + 1)
            act.preload_act_table(ACT.Gelu)
            act.wait_ge(k_cols_free, 1)
            for t in range(STEPS):
                scan(t, FIRST_READ)
                body_readouts(readout, t, FIRST_READ)
                if t % HALF_STEPS == 7:
                    save(t // HALF_STEPS, FIRST_READ)
            with act.Fori(FIRST_READ + 1, BODIES) as i:
                for t in range(STEPS):
                    scan(t, i)
                    body_readouts(readout, t, i)
                    if t % HALF_STEPS == 7:
                        save(t // HALF_STEPS, i)
            rest_of_readouts(act, readout)

        @block.vector
        def _(dve):
            v = nc.vector
            dve.wait_ge(mats_loaded, 16)
            dve.wait_ge(rows_loaded, 16)
            dve.wait_ge(const_ready, 1)
            n = [0]

            def seq(i):
                n[0] += 1
                i.then_inc(dve_seq, 1)
                dve.wait_ge(dve_seq, n[0])
            seq(v.tensor_scalar(res_abs, res_nat[:, :, :].rearrange("p m k -> p (m k)"), -1.0, None, ALU.mult))
            seq(v.tensor_tensor(res_abs, res_abs,
                                res_nat[:, :, :].rearrange("p m k -> p (m k)"), ALU.max))
            seq(v.reduce_max(setup[:, 2:3], res_abs, AX_X))
            dve.wait_ge(amax_ready, 1)
            seq(v.tensor_scalar(setup[:, 4:5], setup[:, 3:4], 2.0 ** -100, None, ALU.max))
            seq(v.tensor_scalar(setup[:, 4:5].bitcast(I32), setup[:, 4:5].bitcast(I32), 0x7F800000, None, ALU.bitwise_and))
            seq(v.reciprocal(setup[:, 5:6], setup[:, 4:5]))
            v.tensor_scalar(setup[:, 6:7], setup[:, 5:6], WEIGHT_UP, None, ALU.mult)
            v.tensor_scalar(setup[:, 7:8], setup[:, 4:5], 1.0 / (WEIGHT_UP * STATE_UP), None, ALU.mult)
            seq(v.tensor_scalar(setup[:, 8:9], setup[:, 5:6], WEIGHT_UP * STATE_UP, None, ALU.mult))
            seq(v.tensor_scalar(neg_inv_a[:, :], a_cols[:, :], 1e-8, None, ALU.add))
            seq(v.reciprocal(neg_inv_a[:, :], neg_inv_a[:, :]))
            seq(v.tensor_scalar(neg_inv_a[:, :], neg_inv_a[:, :], -1.0, None, ALU.mult))
            for m in range(NH):
                v.tensor_scalar(b_nat[:, m, :], b_nat[:, m, :], neg_inv_a[:, m:m + 1], None, ALU.mult)
            v.tensor_tensor(ro_tmp[:, :], ro_nat[:, :], ro_b_row[:, :], ALU.mult)
            seq(v.tensor_tensor(ro_nat[:, :], ro_nat[:, :], ro_g_row[:, :], ALU.mult))
            v.reduce_sum(setup[:, 9:10], ro_nat[:, :], AX_X)
            seq(v.reduce_sum(setup[:, 10:11], ro_tmp[:, :], AX_X))
            seq(v.tensor_scalar(setup[:, 9:10], setup[:, 9:10], 1.0 / H, None, ALU.mult))
            v.tensor_scalar(ro_nat[:, :], ro_nat[:, :], setup[:, 9:10], None, ALU.subtract)
            seq(v.tensor_tensor(setup[:, 10:11], setup[:, 10:11], cols[:, 3:4], ALU.add))
            v.tensor_scalar(ro_tmp[:, 0:P], ident[:, :], setup[:, 10:11], None, ALU.mult)
            v.tensor_tensor(setup[:, 11:12], cols[:, 1:2], cols[:, 2:3], ALU.mult)
            v.tensor_tensor(gate_t[:, P:P + 1], cols[:, 0:1], cols[:, 2:3], ALU.mult)
            q_stacks = q_rows[:, :, :, :].rearrange("p k b (a n) -> p (k b a) n", n=SLOT)
            v.memset(q_stacks[:, :, SHIFT_AT:SHIFT_AT + D], 0.0)
            v.memset(q_stacks[:, :, 7 * D:], 0.0)
            v.tensor_copy(mix[:, 0:1], alpha_col)
            v.tensor_copy(mix[:, 2:3], gamma_col)
            v.memset(mix[:, 1:2], 1.0)
            v.memset(mix[:, 3:4], 1.0)
            v.memset(kept[:, :], 0.0).then_inc(kept_ready, 1)
            v.memset(s_hi[:, :], 0.0).then_inc(hi_ready, 1)
            v.memset(s_lo[:, :], 0.0).then_inc(lo_ready, 1)
            v.memset(z_all[:, :], 0.0).then_inc(cvec_ready, 1)
            def split(b, i):
                for k in range(NQ):
                    n = b * NQ + k
                    vals = values[:, bass.ds(n, 1), :].rearrange("p o (a w) -> p (o a) w", w=VW)
                    rest = rest_v[:, k, :].rearrange("p (a c) -> p a c", c=C)
                    dve.wait_ge(first_ready, n + 1)
                    dve.wait_ge(v_done, n - 3 + FOUR_FREE)
                    v.tensor_tensor(rest, PS[:, 2 + k, 64:64 + NA * C].rearrange("p (a c) -> p a c", c=C),
                                    vals[:, :, 0:C], ALU.subtract).then_inc(v_rest, 1)
                    r, p2 = rest_qk[:, :, k, :], part[:, i, 1, :, k, :]
                    v.tensor_tensor(r, PS[:, 2 + k, 0:64].rearrange("p (h n) -> p h n", h=2), part[:, i, 0, :, k, :],
                                    ALU.subtract).then_inc(qk_rest, 1)
                    dve.wait_ge(v_rest, n + 1)
                    v.tensor_copy(vals[:, :, C:2 * C], rest).then_inc(v_second, 1)
                    dve.wait_ge(qk_rest, n + 1 + FOUR_FREE)
                    v.tensor_copy(p2, r).then_inc(qk_step, 1)
                    dve.wait_ge(qk_step, n + 1)
                    v.tensor_tensor(part[:, i, 2, :, k, :], r, p2, ALU.subtract).then_inc(qk_parts, 1)
                dve.wait_ge(qk_parts, b * NQ + NQ)
                dve.wait_ge(k_turned, b + FREE)
                kr = k_rows[:, :, :].rearrange("p k (a n) -> p (k a) n", n=SLOT)
                pk = part[:, i, :, 1, :, :].rearrange("p l k (a d) -> p l (k a) d", d=D)
                for l, slots in enumerate(((0, 1, 2), (3, 4), (5,))):
                    for z in slots:
                        last = v.tensor_copy(kr[:, :, place(z):place(z) + D], pk[:, l, :, :])
                last.then_inc(k_rows_ready, 1)

            with dve.Fori(0, B // 2) as it:
                for i in range(2):
                    split(it * 2 + i, i)

            def weights_out():
                dve.wait_ge(wt_turned, 1)
                hi, lo = (one[:, :, :].rearrange("p k m -> p (k m)") for one in (res_hi, res_lo))
                v.tensor_scalar(hi, PS[:, 0, :], setup[:, 6:7], None, ALU.mult).then_inc(hi_made, 1)
                v.tensor_scalar(in_t[:, :], PS[:, 1, 0:H], setup[:, 8:9], None, ALU.mult)
                v.tensor_copy(b_t[:, :], PS[:, 1, H:2 * H])
                v.tensor_copy(gate_t[:, 0:P], PS[:, 6, 0:P])
                for m in range(NH):
                    v.tensor_copy(ro_pair[:, m, 0:P], ident[:, :])
                    v.tensor_copy(ro_pair[:, m, P:2 * P], PS[:, 6, P + m * P:2 * P + m * P])
                v.tensor_copy(ro_row[:, :], PS[:, 6, 3 * P:4 * P])
                v.tensor_tensor(setup[:, 12:13], PS[:, 5, 0:1], b_delta_col, ALU.add)
                dve.wait_ge(hi_made, 1)
                v.scalar_tensor_tensor(lo, PS[:, 0, :], setup[:, 6:7], hi, ALU.mult, ALU.subtract).then_inc(wt_ready, 1)

            def work(p, j, before_scan):
                if p in (6, 10, 14, 18):
                    a = (p - 6) // 4
                    dve.wait_ge(scored, j * NA + (a + 1))
                    v.reduce_max(top[:, a % 2:a % 2 + 1], SCORES[a % 2], AX_X).then_inc(top_ready, 1)
                if p in (7, 11, 15, 19):
                    a = (p - 7) // 4
                    at = (a % 2) * SLOT + SHIFT_AT
                    dve.wait_ge(top_ready, j * NA + (a + 1))
                    dve.wait_ge(shift_turned, j * NA + a + FREE)
                    v.tensor_scalar(shift_rows[:, at:at + 1], top[:, a % 2:a % 2 + 1], SHIFT, None, ALU.subtract)
                    v.tensor_scalar(shift[:, :], top[:, a % 2:a % 2 + 1], SHIFT, None, ALU.subtract).then_inc(shift_raw, 1)
                    dve.wait_ge(shift_raw, j * NA + (a + 1))
                    v.tensor_tensor(shift_rows[:, at + 1:at + 2], shift[:, :], shift_rows[:, at:at + 1], ALU.subtract
                                    ).then_inc(shift_ready, 1)
                if before_scan and p in (20, 28):
                    a = (p - 16) // 4
                    dve.wait_ge(prob_ready, j * NA + (a + 1) + FREE)
                    dve.wait_ge(prob_lo_ready, j * NA + a + TWO_FREE)
                    dve.wait_ge(pv_done, j * NA + (a - 1) + TWO_FREE)
                    v.tensor_tensor(prob_lo[:, a % 2, :], prob[:, a % 2, :], prob_hi[:, a % 2, :], ALU.subtract
                                    ).then_inc(prob_lo_ready, 1)
                if p == 32:
                    dve.wait_ge(o_ready, j + 1 + FREE)
                    v.reciprocal(coef[:, :], o_sb[:, :, 2 * C:2 * C + 1].rearrange("p a o -> p (a o)")).then_inc(inv_ready, 1)
                    dve.wait_ge(inv_ready, j + 1 + FREE)
                    v.tensor_tensor(coef[:, :], coef[:, :], mix[:, :], ALU.mult).then_inc(coef_ready, 1)
                if p == 36:
                    dve.wait_ge(h_ready, j + 1)
                    v.bn_stats(stats[:, :], h_now[:, :]).then_inc(stat_a, 1)
                    dve.wait_ge(stat_a, j + 1)
                    dve.sem_inc(stats_waited, 1)
                    v.bn_aggr(mean_var[:, :], stats[:, :]).then_inc(stat_ready, 1)
                if p == 40:
                    dve.wait_ge(norm_ready, j + 1)
                    v.tensor_scalar(x_hat[:, :], h_now[:, :], mean_var[:, 0:1], small[:, 6:7], ALU.subtract, ALU.mult
                                    ).then_inc(hat_ready, 1)
                if p == 41:
                    dve.wait_ge(hat_turned, j + 1)
                    v.tensor_copy(x_hat_t[:, :], MISC[:, 0:P]).then_inc(hat_copied, 1)
                    dst = xn[:, 0:L * B].rearrange("p (q t b) -> p q t b", q=NQ, b=B)
                    v.tensor_scalar(dst[:, bass.ds(tile_q(j), 1), :, bass.ds(j % B, 1)].rearrange("p q t o -> p (q t o)"),
                                    MISC[:, 0:P], cols[:, 0:1], cols[:, 1:2], ALU.mult, ALU.add).then_inc(xn_ready, 1)
                if p == 45:
                    dve.wait_ge(gated, j + 1)
                    dve.wait_ge(gate_ready, j + FREE)
                    v.tensor_scalar(z_all[:, bass.ds(j, 1)], MISC[:, P:P + 1], setup[:, 12:13], None, ALU.add)
                    v.scalar_tensor_tensor(gate_pre[:, :], MISC[:, 0:P], small[:, 5:6], b_gate_row[:, :], ALU.mult, ALU.add
                                           ).then_inc(gate_raw, 1)

            def scan(t, i):
                n = i * STEPS + (t + 1)
                dve.wait_ge(acted, n)
                dve.wait_ge(kept_ready, n)
                v.scalar_tensor_tensor(s_hi[:, :], y[:, :], LEAK * STATE_UP, kept[:, :], ALU.mult, ALU.add).then_inc(hi_ready, 1)
                full = s_body[:, t, :]
                if t % HALF_STEPS == 0:
                    dve.wait_ge(saved, 2 * i - 1 + t // HALF_STEPS + TWO_FREE)
                v.scalar_tensor_tensor(full, y[:, :], LEAK * STATE_UP, kept[:, :], ALU.mult, ALU.add).then_inc(full_ready, 1)
                dve.wait_ge(full_ready, n)
                v.tensor_tensor(s_lo[:, :], full, s_hi[:, :], ALU.subtract).then_inc(lo_ready, 1)
                v.tensor_scalar(kept[:, :], full, KEEP, None, ALU.mult).then_inc(kept_ready, 1)

            for j in range(2):
                for p in range(STEPS):
                    tiles_at(work, p, j, before_scan=True)
                    if j == 0 and p == 14:
                        weights_out()
            with dve.Fori(2, AHEAD) as j:
                for p in range(STEPS):
                    tiles_at(work, p, j, before_scan=True)
            with dve.Fori(0, NT - AHEAD) as i:
                for t in range(STEPS):
                    scan(t, i)
                    tiles_at(work, t, i + AHEAD)
            for i in range(NT - AHEAD, FIRST_DECAY):
                for t in range(STEPS):
                    scan(t, i)
                    tiles_at(work, t, i + AHEAD)

            def ssm_row(s, c):
                at = bass.ds((c % 2) * 4 * P + (s % 4) * P, P)
                return ssm[:, s // 4, bass.ds(half_q(c) + 1, 1), at].rearrange("p o n -> p (o n)")

            def feed(s, c):
                if s > 0:
                    recur(s - 1, c)
                elif not (isinstance(c, int) and c == 0):
                    recur(7, c - 1)
                dve.wait_ge(ssm_fed, c * 8 + s + 1)
                v.scalar_tensor_tensor(ssm_b_bar[:, s % 2, :], ssm_row(s, c), 1.0, PS[:, 6 + s % 2, 0:P],
                                       ALU.subtract, ALU.mult).then_inc(ssm_scaled, 1)

            def recur(s, c):
                m, k = s // 4, s % 4
                n = c * 8 + s
                row = ssm_row(s, c)
                dve.wait_ge(ssm_scaled, n + 1)
                dve.wait_ge(ssm_done, n - 7 + EIGHT_FREE)
                v.tensor_tensor_scan(row, row, ssm_b_bar[:, s % 2, :],
                                     ssm[:, m, bass.ds(half_q(c), 1), bass.ds((c % 2) * 4 * P + k * P + P - 1, 1)
                                         ].rearrange("p o n -> p (o n)"), ALU.mult, ALU.add).then_inc(ssm_done, 1)

            def readout(u, n, e, active, fed, kept_bodies):
                if 3 in active and u == 0:
                    dve.wait_ge(h2_ready, n - 3 + 1 + TWO_FREE)
                    v.bn_stats(ln_st[:, :], h_all[:, bass.ds(n - 3, 1), :].rearrange("p o n -> p (o n)")).then_inc(ln_stat_a, 1)
                if 3 in active and u == 1:
                    dve.wait_ge(ln_stat_a, n - 3 + 1)
                    dve.sem_inc(stats_waited, 1)
                    v.bn_aggr(ln_mv[:, 1 - e, :], ln_st[:, :]).then_inc(ln_stats, 1)
                if 1 in active and u == 1:
                    for r in range(2):
                        dve.wait_ge(read_piece, (n - 1) * 4 + (2 * r + 2) + EIGHT_FREE)
                        v.bn_stats(r_st[:, r, :], PS[:, 4 - 2 * e + r, 0:H]).then_inc(r_stat_a, 1)
                if 1 in active and u == 2:
                    j = n - 1
                    dve.wait_ge(r_stat_a, j * 2 + 2)
                    dve.wait_ge(r_dev_ready, j + FREE)
                    dve.sem_inc(stats_waited, 1)
                    for r in range(2):
                        last = v.bn_aggr(r_mv[:, r, :], r_st[:, r, :])
                    last.then_inc(r_stats, 1)
                if 1 in active and u == 3:
                    j = n - 1
                    dve.wait_ge(r_dev_ready, j + 1 + FREE)
                    dve.wait_ge(r_gelu, j - 1 + TWO_FREE)
                    for r in range(2):
                        last = v.scalar_tensor_tensor(r_pre[:, 1 - e, r, :], PS[:, 4 - 2 * e + r, H:H + P],
                                                      r_dev[:, 1 - e, r:r + 1], ro_row[:, :], ALU.mult, ALU.add)
                    last.then_inc(readout_scaled, 1)
                if 3 in active and u == 3:
                    j = n - 3
                    dve.wait_ge(ln_dev_ready, j + 1)
                    v.tensor_scalar(gate_all[:, bass.ds(j, 1), :].rearrange("p o n -> p (o n)"),
                                    h_all[:, bass.ds(j, 1), :].rearrange("p o n -> p (o n)"),
                                    ln_mv[:, 1 - e, 0:1], ln_small[:, 1 - e, 1:2], ALU.subtract, ALU.mult
                                    ).then_inc(readout_normed, 1)

            dve.wait_ge(gate_raw, NT + FREE)
            v.tensor_scalar(sp_tmp[:, 1, :], z_all[:, :], -1.0, None, ALU.mult).then_inc(sp_step, 1)
            dve.wait_ge(sp_step, 1)
            v.tensor_tensor(sp_tmp[:, 0, :], z_all[:, :], sp_tmp[:, 1, :], ALU.max).then_inc(sp_step, 1)
            v.tensor_scalar(delta[:, :], z_all[:, :], 0.0, None, ALU.max).then_inc(sp_step, 1)
            dve.wait_ge(sp_ready, 2)
            dve.wait_ge(sp_step, 3)
            v.tensor_tensor(delta[:, :], delta[:, :], sp_tmp[:, 0, :], ALU.add).then_inc(sp_step, 1)
            dve.wait_ge(pv_done, NA * NT + TWO_FREE)
            v.memset(ssm[:, :, 0, :].rearrange("p m (b n) -> p m b n", b=B)[:, :, :, P - 1:P], 0.0).then_inc(ssm_zeroed, 1)
            for t in range(STEPS):
                scan(t, FIRST_DECAY)
            dve.wait_ge(ssm_zeroed, 1)
            for t in range(STEPS):
                scan(t, FIRST_DECAY + 1)
                if t == 0:
                    dve.wait_ge(decayed, 4)
                if 7 <= t < 8:
                    feed(7, 0)
                elif t < 7:
                    feed(t, 0)
                if t >= 8:
                    feed(t - 8, 1)
            dve.wait_ge(decayed, 2 * 2 * NQ)
            for t in range(STEPS):
                scan(t, FIRST_READ)
                if t % 2 == 0:
                    feed(t // 2, FIRST_READ - FIRST_DECAY)
                body_readouts(readout, t, FIRST_READ)
            with dve.Fori(FIRST_READ + 1, BODIES) as i:
                for t in range(STEPS):
                    scan(t, i)
                    if t % 2 == 0:
                        feed(t // 2, i - FIRST_DECAY)
                    body_readouts(readout, t, i)
            recur(7, 2 * NQ - 1)
            rest_of_readouts(dve, readout)

        @block.tensor
        def _(pe):
            t_ = nc.tensor
            def turn_x(b, i, k):
                n = b * NQ + k
                pe.wait_ge(x_t_ready, n - 1 + TWO_FREE)
                if k == 0:
                    pe.wait_ge(x_loaded[i], (b - i) * 8 + 16)
                t_.transpose(PS[:, k % 2, 0:P], x_in[:, i, k, :], ident[:, :]).then_inc(x_turned, 1)

            def turn_keys(b):
                pe.wait_ge(k_rows_ready, b + 1 + FREE)
                pe.wait_ge(k_cols_ready, b + FREE)
                turned = OUT2[1].bitcast(BF16).rearrange("p (a k n) -> p a k n", a=2, k=NQ)
                for k in range(NQ):
                    for a in range(2):
                        last = t_.transpose(turned[:, a, k, :], k_rows[:, k, a * P:a * P + P], ident16[:, :])
                last.then_inc(k_turned, 1)

            def project(b, i):
                for k in range(NQ):
                    n = b * NQ + k
                    if k + 1 < NQ:
                        turn_x(b, i, k + 1)
                    elif not (isinstance(b, int) and b == B - 1):
                        turn_x(b + 1, 1 - i, 0)
                    pe.wait_ge(x_t_ready, n + 1 + TWO_FREE)
                    pe.wait_ge(qk_rest, n - 3 + FOUR_FREE)
                    t_.matmul(PS[:, 2 + k, 0:64 + NA * C], x_t[:, k % 2, :], wall[:, :], start=True, stop=True
                              ).then_inc(projected, 1)
                    if k == 1 and not (isinstance(b, int) and b == 0):
                        turn_keys(b - 1)

            pe.wait_ge(const_ready, 2)
            pe.wait_ge(wall_loaded, 16)
            turn_x(0, 0, 0)
            for b in range(2):
                project(b, b % 2)
            with pe.Fori(1, B // 2 - 1) as it:
                for i in range(2):
                    project(it * 2 + i, i)
            for b in range(B - 2, B):
                project(b, b % 2)
            turn_keys(B - 1)
            pe.wait_ge(k_cols_ready, B + FREE)
            pe.wait_ge(v_done, NT + FOUR_FREE)
            pe.wait_ge(qk_rest, NT + FOUR_FREE)
            pe.wait_ge(q_rows_ready, B + FREE)

            def turn_weights():
                pe.wait_ge(cvec_ready, 1)
                for m in range(NH):
                    for k in range(NH):
                        t_.transpose(PS[:, 0, k * H + m * P:k * H + m * P + P], res_nat[:, m, k * P:k * P + P], ident[:, :])
                    t_.transpose(PS[:, 1, m * P:m * P + P], in_nat[:, m, :], ident[:, :])
                    t_.transpose(PS[:, 1, H + m * P:H + m * P + P], b_nat[:, m, :], ident[:, :])
                    t_.transpose(PS[:, 6, P + m * P:2 * P + m * P], ro_nat[:, m * P:m * P + P], ident[:, :])
                t_.transpose(PS[:, 6, 0:P], gate_nat[:, :], ident[:, :])
                t_.matmul(PS[:, 6, 3 * P:4 * P], ones[:, :], ro_tmp[:, 0:P], start=True, stop=True)
                t_.matmul(PS[:, 5, 0:1], ones[:, :], setup[:, 11:12], start=True, stop=True).then_inc(wt_turned, 1)

            def keep_clock(bank):
                t_.matmul(bank, ident16[:, :], ballast[:, :], start=True, stop=True, skip_group_check=True)

            def work(p, j, before_scan):
                keys = k_cols[:, bass.ds(j % B, 1), :, :].rearrange("p o a n -> p (o a) n")
                peeled = isinstance(j, int)
                if p in (3, 7, 11, 15):
                    a = (p - 3) // 4
                    pe.wait_ge(q_ready, j * NA + a + FREE)
                    if a == 2 and not (peeled and j < 2):
                        pe.wait_ge(xn_ready, j - 1 + FREE)
                    if a == 3 and not (peeled and j < 2):
                        pe.wait_ge(gate_raw, j - 1 + FREE)
                    rows = q_rows[:, :, :, :].rearrange("p k b n -> p (k b) n")
                    at = (a // 2) * P
                    pe.sem_inc(queries_waited, 1)
                    t_.transpose(MISC16[:, 0:P], rows[:, bass.ds(j, 1), at:at + P].rearrange("p o n -> p (o n)"), ident16[:, :]
                                 ).then_inc(q_turned, 1)
                if p in (5, 9, 13, 17):
                    a = (p - 5) // 4
                    pe.wait_ge(q_ready, j * NA + (a + 1) + FREE)
                    pe.wait_ge(shift_placed, j * NA + (a - 1) + TWO_FREE)
                    if a in (0, 3):
                        keep_clock(SCORES[a % 2])
                    t_.matmul(SCORES[a % 2], q_cols[:, a, :], keys[:, a // 2, :], start=True, stop=True).then_inc(scored, 1)
                if p - 2 * before_scan in (8, 12, 16, 20):
                    a = (p - 8) // 4
                    pe.wait_ge(shift_ready, j * NA + (a + 1))
                    t_.transpose(SCORES16[a % 2][:, 0:P], shift_rows[:, :], ident16[:, :]).then_inc(shift_turned, 1)
                if p in (12, 16, 20, 24):
                    a = (p - 12) // 4
                    pe.wait_ge(prob_ready, j * NA + a + FREE)
                    pe.wait_ge(shift_placed, j * NA + (a + 1) + TWO_FREE)
                    keep_clock(TURNED)
                    for k in range(NQ):
                        last = t_.matmul(TURNED[:, k * P:k * P + P], keys[:, a // 2, k * P:k * P + P], q_cols[:, a, :],
                                         start=k == 0, stop=k == NQ - 1, skip_group_check=True)
                    last.then_inc(turned_ready, 1)
                if p in (15, 19, 23, 27):
                    a = (p - 15) // 4
                    pe.wait_ge(prob_ready, j * NA + (a + 1) + FREE)
                    if a == 0:
                        pe.wait_ge(o_half, j + FREE)
                    if a == 2:
                        pe.wait_ge(o_ready, j + FREE)
                    weigh(a, j, prob_hi, VW)
                if p in (18, 22, 26, 30):
                    a = (p - 18) // 4
                    pe.wait_ge(prob_lo_ready, j * NA + (a + 1) + TWO_FREE)
                    weigh(a, j, prob_lo, 130).then_inc(pv_done, 1)
                if p == 41:
                    pe.wait_ge(hat_ready, j + 1)
                    pe.wait_ge(q_ready, min((j + 2) * NA + 2, NT * NA) + FREE if peeled else (j + 2) * NA + 2 + FREE)
                    t_.transpose(MISC[:, 0:P], x_hat[:, :], ident[:, :]).then_inc(hat_turned, 1)
                if p == 45:
                    pe.wait_ge(hat_copied, j + 1)
                    pe.wait_ge(xn_ready, j + 1 + FREE)
                    pe.wait_ge(q_ready, min((j + 2) * NA + 3, NT * NA) + FREE if peeled else (j + 2) * NA + 3 + FREE)
                    t_.matmul(MISC[:, 0:P + 1], x_hat_t[:, :], gate_t[:, :], start=True, stop=True).then_inc(gated, 1)

            def weigh(a, j, prob_part, width):
                dst = OUT2[a // 2][:, (a % 2) * 256:(a % 2) * 256 + width]
                for k in range(NQ):
                    vals = values[:, bass.ds((j % B) * NQ + k, 1), a * VW:a * VW + width].rearrange("p o w -> p (o w)")
                    last = t_.matmul(dst, prob_part[:, a % 2, k * P:k * P + P], vals, start=prob_part is prob_hi and k == 0,
                                     stop=prob_part is prob_lo and k == NQ - 1, skip_group_check=True)
                return last

            def scan(t, i):
                n = i * STEPS + (t + 1)
                pe.wait_ge(hi_ready, n)
                dst = PRE[t // 8][:, :, t % 8, :]
                for wts, st in ((res_hi, s_hi), (res_lo, s_hi), (res_hi, s_lo)):
                    if st is s_lo:
                        pe.wait_ge(lo_ready, n)
                    for k in range(NH):
                        for m in range(NH):
                            last = t_.matmul(dst[:, m, :], wts[:, k, m * P:m * P + P], st[:, k * B:k * B + B],
                                             start=False, stop=st is s_lo and k == NH - 1, skip_group_check=True)
                last.then_inc(pre_ready, 1)

            def fill(m, half, i):
                src = xn[:, bass.ds(i * SB + half * HALF, HALF)]
                t_.matmul(PS[:, half, m * HALF:m * HALF + HALF], in_t[:, m * P:m * P + P], src, start=m == 0, stop=True,
                          skip_group_check=True)

            def scan_body(t, i):
                scan(t, i)
                if t in (10, 11):
                    keep_clock(PS[:, 0, :])
                if t in (2, 6):
                    fill((t - 2) // 4, 1, i)
                if t in (14, 15):
                    fill(t - 14, 0, i + 1)

            for j in range(2):
                for p in range(STEPS):
                    if j == 0 and p == 15:
                        pe.wait_ge(wt_ready, 1)
                    tiles_at(work, p, j, before_scan=True)
                    if j == 0 and p == 5:
                        turn_weights()
            with pe.Fori(2, AHEAD) as j:
                for p in range(STEPS):
                    tiles_at(work, p, j, before_scan=True)
            pe.wait_ge(xn_ready, B + FREE)
            fill(0, 0, 0)
            fill(1, 0, 0)
            with pe.Fori(0, NT - AHEAD) as i:
                for t in range(STEPS):
                    if t == 14:
                        pe.wait_ge(xn_ready, i + (AHEAD - 2) + 1 + FREE)
                    scan_body(t, i)
                    tiles_at(work, t, i + AHEAD)
            for i in range(NT - AHEAD, FIRST_DECAY):
                for t in range(STEPS):
                    if t == 14:
                        pe.wait_ge(xn_ready, i + (AHEAD - 2) + 1 + FREE)
                    scan_body(t, i)
                    tiles_at(work, t, i + AHEAD)

            def feed(s, c):
                m, k = s // 4, s % 4
                pe.wait_ge(ssm_done, c * 8 + (s - 1) + EIGHT_FREE)
                xq = xn[:, 0:L * B].rearrange("p (q t b) -> p q b t", q=NQ, b=B)
                t_.matmul(PS[:, 6 + s % 2, 0:P], b_t[:, m * P:m * P + P],
                          xq[:, bass.ds(half_q(c), 1), bass.ds((c % 2) * 4 + k, 1), :].rearrange("p o b t -> p (o b t)"),
                          start=True, stop=True).then_inc(ssm_fed, 1)

            def spread_delta(n):
                c = n // 4
                if c >= 2:
                    pe.wait_ge(decayed, 2 * (c - 2) + 2)
                t_.matmul(PS[:, 4 + c % 2, (n % 4) * P:(n % 4) * P + P], delta[:, n:n + 1].to_broadcast([P, P]), ident[:, :],
                          start=True, stop=True).then_inc(spread, 1)

            def read_one(r, m, j, e):
                bank = PS[:, 2 + 2 * e + r, 0:4 * P].rearrange("p (g n) -> p g n", n=P)
                dst = bank[:, 0:3:2, :] if m == 0 else bank[:, 1:3, :]
                t_.matmul(dst, r_in[:, e, r, m, :], ro_pair[:, m, :].rearrange("p (g n) -> p g n", n=P),
                          start=m == 0, stop=m == NH - 1, skip_group_check=True).then_inc(read_piece, 1)

            def readout(u, n, e, active, fed, kept_bodies):
                if 1 in active and u == 0:
                    read_one(1, 1, n - 1, 1 - e)
                if 0 in active and u == 1:
                    pe.wait_ge(states_in, n + 1)
                    pe.wait_ge(readout_scaled, n - 1 + TWO_FREE)
                    keep_clock(PS[:, 2 + 2 * e, :])
                    read_one(0, 0, n, e)
                if 0 in active and u == 2:
                    read_one(0, 1, n, e)
                if 0 in active and u == 3:
                    pe.wait_ge(ssm_in, n + 1)
                    keep_clock(PS[:, 3 + 2 * e, :])
                    read_one(1, 0, n, e)

            pe.wait_ge(pv_done, NA * NT + TWO_FREE)
            pe.sem_inc(k_cols_free, 1)
            for t in range(STEPS):
                scan_body(t, FIRST_DECAY)
                if t == 4:
                    pe.wait_ge(sp_step, 4)
                if t >= 4:
                    spread_delta(2 * (t - 4))
                    spread_delta(2 * (t - 4) + 1)
            for t in range(STEPS):
                scan_body(t, FIRST_DECAY + 1)
                if t < 4:
                    spread_delta(24 + 2 * t)
                    spread_delta(24 + 2 * t + 1)
                if t < 8:
                    feed(t, 0)
                else:
                    feed(t - 8, 1)
                keep_clock(PS[:, 2, :])
            pe.wait_ge(decayed, 2 * 2 * NQ)
            for t in range(STEPS):
                scan_body(t, FIRST_READ)
                if t % 2 == 0:
                    feed(t // 2, FIRST_READ - FIRST_DECAY)
                body_readouts(readout, t, FIRST_READ)
            with pe.Fori(FIRST_READ + 1, BODIES) as i:
                for t in range(STEPS):
                    scan_body(t, i)
                    if t % 2 == 0:
                        feed(t // 2, i - FIRST_DECAY)
                    body_readouts(readout, t, i)
            rest_of_readouts(pe, readout)


def pack(inputs):
    get = lambda name: np.asarray(inputs[name])
    wall = np.zeros((P, 64 + NA * C), np.float32)
    for a, (q, k, v) in enumerate(((0, 0, 0), (0, 1, 1), (1, 1, 1), (1, 0, 0))):
        for n, (signal, at, width) in enumerate(((q, a * D, D), (k, 32 + a * D, D), (v, 64 + a * C, C))):
            wall[signal::2, at:at + width] = get(f"L0_tok_w{3 * a + n + 1}")

    def by_rows(m):
        return m.reshape(-1, P, m.shape[-1]).transpose(1, 0, 2).reshape(P, -1)

    attn = lambda name: get(f"L0_attn_{name}")
    mats = np.concatenate([by_rows(attn("W_res")), by_rows(attn("W_in")), by_rows(attn("W_B")), attn("W_ro"), attn("W_gate"),
                           attn("A").reshape(NH, P).T,
                           *(attn(n).reshape(P, 1) for n in ("norm_g", "norm_b", "w_delta", "b_ro"))], axis=1)
    rows = np.concatenate([attn("ro_g"), attn("ro_b"), attn("b_gate"), attn("b_delta").reshape(1),
                           get("L0_tok_alpha").reshape(1), get("L0_tok_gamma").reshape(1)]).reshape(1, ROWS)
    assert mats.shape == (P, MATS)
    return {"in_wall": wall, "in_mats": np.ascontiguousarray(mats), "in_rows": rows}


def kernel(**inputs):
    import concourse.bacc as bacc
    from concourse.bass_utils import run_bass_kernel_spmd

    nc = bacc.Bacc("TRN2", target_bir_lowering=False, num_devices=1)
    arrays = {"in_x": np.ascontiguousarray(inputs["x"]), **pack(inputs)}
    aps = [nc.dram_tensor(name, a.shape, mybir.dt.from_np(a.dtype), kind="ExternalInput").ap() for name, a in arrays.items()]
    out = nc.dram_tensor("out", (B, L, 2 * C), F32, kind="ExternalOutput").ap()
    build(nc, *aps, out)
    r = run_bass_kernel_spmd(nc, [arrays], core_ids=[0])
    return r.results[0]["out"]
```
